# Optimizing a Trainium2 kernel written in Bass

```python
import numpy as np
import jax
import jax.numpy as jnp

def _softmax(x, axis=-1):
    return jax.nn.softmax(x, axis=axis)

def _gelu(x):
    return jax.nn.gelu(x, approximate=True)

def _silu(x):
    return jax.nn.silu(x)

def _sigmoid(x):
    return jax.nn.sigmoid(x)

def _layernorm(x, axis=-1, eps=1e-05):
    m = jnp.mean(x, axis=axis, keepdims=True)
    v = jnp.var(x, axis=axis, keepdims=True)
    return (x - m) / jnp.sqrt(v + eps)

def _scatter_add(tgt, idx, src, axis=0):
    return tgt.at[idx].add(src)

def _segment_sum(src, seg, n):
    return jax.ops.segment_sum(src, seg, n)
kernel_name = 'mk_decoder_postln_d1_seqx_r4_aab375'

def setup_inputs(seed: int=0):
    np.random.seed(seed)
    _w = jnp.asarray

    def _rec_inputs():
        import jax
        import jax.numpy as jnp
        _rk = jax.random.key(seed)
        x = 7.22e-05 + 1 * jax.random.normal(jax.random.fold_in(_rk, 1), (4, 1024, 256), jnp.float32)
        _lenS = 1024 - jax.random.randint(jax.random.fold_in(_rk, 7), (4,), 0, max(1, 1024 // 4) + 1, jnp.int32)
        _lenS2 = 77 - jax.random.randint(jax.random.fold_in(_rk, 8), (4,), 0, max(1, 77 // 4) + 1, jnp.int32)
        _ctx_1024P = jax.random.normal(jax.random.fold_in(_rk, 11), (4, 16, 256), jnp.float32)
        _ctx_1024c = jax.random.dirichlet(jax.random.fold_in(_rk, 511), 0.3 * jnp.ones((16,), jnp.float32), (4, 77))
        _ctx_1024t = jnp.einsum('bsk,bkd->bsd', _ctx_1024c, _ctx_1024P)
        _ctx_1024t = _ctx_1024t * jax.lax.rsqrt(jnp.mean(jnp.square(_ctx_1024t)) + 1e-12) * 0.953939
        ctx_1024 = 4.13588e-05 + 0.999923 * (_ctx_1024t + 0.3 * jax.random.normal(jax.random.fold_in(_rk, 611), (4, 77, 256), jnp.float32))
        _validS = jnp.arange(1024)[None, :] < _lenS[:, None]
        _validS2 = jnp.arange(77)[None, :] < _lenS2[:, None]
        _causal = jnp.tril(jnp.ones((1024, 1024), dtype=bool))
        mask_BxSxS2_bk1 = jnp.broadcast_to(_validS2[:, None, :], (4, 1024, 77))
        return (x, ctx_1024, mask_BxSxS2_bk1)
    x, ctx_1024, mask_BxSxS2_bk1 = _rec_inputs()

    def _L0_attn_setup():
        import jax, jax.numpy as jnp
        import numpy as np
        import math
        D_MODEL, D_C, D_R, NH = (256, 128, 32, 16)
        HD = D_MODEL // NH
        B, T = (2, 512)

        def _rope_tables(T, d_R):
            inv_freq = 1.0 / 10000.0 ** (jnp.arange(0, d_R, 2, dtype=jnp.float32) / d_R)
            t = jnp.arange(T, dtype=jnp.float32)
            freqs = jnp.outer(t, inv_freq)
            return (jnp.cos(freqs), jnp.sin(freqs))

        def _rotary_apply(x, cos, sin):
            d = x.shape[-1]
            x1, x2 = (x[..., :d // 2], x[..., d // 2:])
            return jnp.concatenate([x1 * cos - x2 * sin, x2 * cos + x1 * sin], axis=-1)
        key = jax.random.key(seed)
        ks = jax.random.split(key, 8)
        s = lambda fan_in: 1.0 / math.sqrt(fan_in)
        return {'x': jax.random.normal(ks[0], (B, T, D_MODEL), jnp.float32), 'W_kv_down': jax.random.normal(ks[1], (D_MODEL, D_C), jnp.float32) * s(D_MODEL), 'W_k_up': jax.random.normal(ks[2], (D_C, D_MODEL), jnp.float32) * s(D_C), 'W_v_up': jax.random.normal(ks[3], (D_C, D_MODEL), jnp.float32) * s(D_C), 'W_q': jax.random.normal(ks[4], (D_MODEL, D_MODEL), jnp.float32) * s(D_MODEL), 'W_q_rope': jax.random.normal(ks[5], (D_MODEL, D_R), jnp.float32) * s(D_MODEL), 'W_k_rope': jax.random.normal(ks[6], (D_C, D_R), jnp.float32) * s(D_C), 'W_o': jax.random.normal(ks[7], (D_MODEL, D_MODEL), jnp.float32) * s(D_MODEL)}
    _L0_attn_all = _L0_attn_setup()
    _L0_attn_in = {k: v for k, v in _L0_attn_all.items() if k in ('W_kv_down', 'W_k_up', 'W_v_up', 'W_q', 'W_q_rope', 'W_k_rope', 'W_o')}
    del _L0_attn_all

    def _L0_xattn_setup():
        import jax, jax.numpy as jnp
        import numpy as np
        N, K, DIM_IN, DIM_Q, DIM_V = (4, 512, 256, 256, 256)
        key = jax.random.key(seed)
        ks = jax.random.split(key, 9)
        c_qk = np.sqrt(6.0 / (DIM_IN + DIM_Q))
        c_v = np.sqrt(6.0 / (DIM_IN + DIM_V))
        inp = {'query': jax.random.normal(ks[0], (N, K, DIM_IN), jnp.float32), 'key': jax.random.normal(ks[1], (N, K, DIM_IN), jnp.float32), 'value': jax.random.normal(ks[2], (N, K, DIM_IN), jnp.float32), 'mask': jnp.broadcast_to(jnp.triu(jnp.ones((K, K), bool), k=1), (N, K, K)), 'q_w': jax.random.uniform(ks[3], (DIM_Q, DIM_IN), jnp.float32, -c_qk, c_qk), 'q_b': jax.random.normal(ks[4], (DIM_Q,), jnp.float32) * 0.01, 'k_w': jax.random.uniform(ks[5], (DIM_Q, DIM_IN), jnp.float32, -c_qk, c_qk), 'k_b': jax.random.normal(ks[6], (DIM_Q,), jnp.float32) * 0.01, 'v_w': jax.random.uniform(ks[7], (DIM_V, DIM_IN), jnp.float32, -c_v, c_v), 'v_b': jax.random.normal(ks[8], (DIM_V,), jnp.float32) * 0.01}
        return inp
    _L0_xattn_all = _L0_xattn_setup()
    _L0_xattn_in = {k: v for k, v in _L0_xattn_all.items() if k in ('q_w', 'q_b', 'k_w', 'k_b', 'v_w', 'v_b')}
    del _L0_xattn_all

    def _L0_ffn_setup():
        import jax, jax.numpy as jnp
        import numpy as np
        B, T, C = (2, 256, 256)
        E, F, K = (8, 512, 2)
        key = jax.random.key(seed)
        ks = jax.random.split(key, 5)
        s = 1.0 / np.sqrt(C)
        return {'x': jax.random.normal(ks[0], (B, T, C), jnp.float32), 'Wr': jax.random.normal(ks[1], (E, C), jnp.float32) * s, 'w1': jax.random.normal(ks[2], (E, C, F), jnp.float32) * s, 'w3': jax.random.normal(ks[3], (E, C, F), jnp.float32) * s, 'w2': jax.random.normal(ks[4], (E, F, C), jnp.float32) * (1.0 / np.sqrt(F))}
    _L0_ffn_all = _L0_ffn_setup()
    _L0_ffn_in = {k: v for k, v in _L0_ffn_all.items() if k in ('Wr', 'w1', 'w3', 'w2')}
    del _L0_ffn_all
    return {'x': x, 'ctx_1024': ctx_1024, 'mask_BxSxS2_bk1': mask_BxSxS2_bk1, 'L0_attn_W_kv_down': _L0_attn_in['W_kv_down'], 'L0_attn_W_k_up': _L0_attn_in['W_k_up'], 'L0_attn_W_v_up': _L0_attn_in['W_v_up'], 'L0_attn_W_q': _L0_attn_in['W_q'], 'L0_attn_W_q_rope': _L0_attn_in['W_q_rope'], 'L0_attn_W_k_rope': _L0_attn_in['W_k_rope'], 'L0_attn_W_o': _L0_attn_in['W_o'], 'L0_xattn_q_w': _L0_xattn_in['q_w'], 'L0_xattn_q_b': _L0_xattn_in['q_b'], 'L0_xattn_k_w': _L0_xattn_in['k_w'], 'L0_xattn_k_b': _L0_xattn_in['k_b'], 'L0_xattn_v_w': _L0_xattn_in['v_w'], 'L0_xattn_v_b': _L0_xattn_in['v_b'], 'L0_ffn_Wr': _L0_ffn_in['Wr'], 'L0_ffn_w1': _L0_ffn_in['w1'], 'L0_ffn_w3': _L0_ffn_in['w3'], 'L0_ffn_w2': _L0_ffn_in['w2']}

def reference(x, ctx_1024, mask_BxSxS2_bk1, L0_attn_W_kv_down, L0_attn_W_k_up, L0_attn_W_v_up, L0_attn_W_q, L0_attn_W_q_rope, L0_attn_W_k_rope, L0_attn_W_o, L0_xattn_q_w, L0_xattn_q_b, L0_xattn_k_w, L0_xattn_k_b, L0_xattn_v_w, L0_xattn_v_b, L0_ffn_Wr, L0_ffn_w1, L0_ffn_w3, L0_ffn_w2):
    import jax
    import jax.numpy as jnp

    def _L0_attn_ref(x, W_kv_down, W_k_up, W_v_up, W_q, W_q_rope, W_k_rope, W_o):
        import jax, jax.numpy as jnp
        import numpy as np
        import math
        D_MODEL, D_C, D_R, NH = (256, 128, 32, 16)
        HD = D_MODEL // NH
        B, T = (2, 512)

        def _rope_tables(T, d_R):
            inv_freq = 1.0 / 10000.0 ** (jnp.arange(0, d_R, 2, dtype=jnp.float32) / d_R)
            t = jnp.arange(T, dtype=jnp.float32)
            freqs = jnp.outer(t, inv_freq)
            return (jnp.cos(freqs), jnp.sin(freqs))

        def _rotary_apply(x, cos, sin):
            d = x.shape[-1]
            x1, x2 = (x[..., :d // 2], x[..., d // 2:])
            return jnp.concatenate([x1 * cos - x2 * sin, x2 * cos + x1 * sin], axis=-1)
        Bb, Tt, _ = x.shape
        cos, sin = _rope_tables(Tt, D_R)
        cos = cos[None]
        sin = sin[None]
        c_kv = x @ W_kv_down
        k_rope = _rotary_apply(c_kv @ W_k_rope, cos, sin)
        k = (c_kv @ W_k_up).reshape(Bb, Tt, NH, HD)
        v = (c_kv @ W_v_up).reshape(Bb, Tt, NH, HD)
        q = (x @ W_q).reshape(Bb, Tt, NH, HD)
        q_rope = _rotary_apply(x @ W_q_rope, cos, sin)
        scale = math.sqrt(HD + D_R)
        scores = jnp.einsum('bqhd,bkhd->bhqk', q, k)
        scores = scores + jnp.einsum('bqr,bkr->bqk', q_rope, k_rope)[:, None]
        scores = scores / scale
        causal = jnp.triu(jnp.ones((Tt, Tt), dtype=bool), k=1)
        scores = jnp.where(causal[None, None], -jnp.inf, scores)
        w = jax.nn.softmax(scores, axis=-1)
        attn = jnp.einsum('bhqk,bkhd->bqhd', w, v).reshape(Bb, Tt, D_MODEL)
        return attn @ W_o

    def _L0_xattn_ref(query, key, value, mask, q_w, q_b, k_w, k_b, v_w, v_b):
        import jax, jax.numpy as jnp
        import numpy as np
        N, K, DIM_IN, DIM_Q, DIM_V = (4, 512, 256, 256, 256)
        q = jnp.einsum('nkm,qm->nkq', query, q_w) + q_b
        k = jnp.einsum('nkm,qm->nkq', key, k_w) + k_b
        v = jnp.einsum('nkm,vm->nkv', value, v_w) + v_b
        scores = jnp.einsum('nqd,nkd->nqk', q, k) / jnp.sqrt(jnp.float32(DIM_Q))
        scores = jnp.where(mask, jnp.float32(-1000000000.0), scores)
        weights = jax.nn.softmax(scores, axis=2)
        y = jnp.einsum('nqk,nkv->nqv', weights, v)
        return y

    def _L0_ffn_ref(x, Wr, w1, w3, w2):
        import jax, jax.numpy as jnp
        import numpy as np
        B, T, C = (2, 256, 256)
        E, F, K = (8, 512, 2)
        Bq, Tq, Cq = x.shape
        flat = x.reshape(-1, Cq)
        N = flat.shape[0]
        probs = jax.nn.softmax(flat @ Wr.T, axis=-1)
        topw, topi = jax.lax.top_k(probs, K)
        topw = topw / jnp.sum(topw, axis=-1, keepdims=True)
        gates = jnp.zeros((N, E), flat.dtype).at[jnp.arange(N)[:, None], topi].set(topw)
        h1 = jnp.einsum('nd,edf->nef', flat, w1)
        h3 = jnp.einsum('nd,edf->nef', flat, w3)
        h = jax.nn.silu(h1) * h3
        y = jnp.einsum('nef,efd->ned', h, w2)
        out = jnp.einsum('ned,ne->nd', y, gates)
        return out.reshape(Bq, Tq, Cq)
    x = _layernorm(x + _L0_attn_ref(x, L0_attn_W_kv_down, L0_attn_W_k_up, L0_attn_W_v_up, L0_attn_W_q, L0_attn_W_q_rope, L0_attn_W_k_rope, L0_attn_W_o), axis=-1)
    x = _layernorm(x + _L0_xattn_ref(x, ctx_1024, ctx_1024, mask_BxSxS2_bk1, L0_xattn_q_w, L0_xattn_q_b, L0_xattn_k_w, L0_xattn_k_b, L0_xattn_v_w, L0_xattn_v_b), axis=-1)
    x = _layernorm(x + _L0_ffn_ref(x, L0_ffn_Wr, L0_ffn_w1, L0_ffn_w3, L0_ffn_w2), axis=-1)
    return x

_drawn_inputs = setup_inputs


def setup_inputs(seed=0):
    import zlib

    import numpy as np

    out = dict(_drawn_inputs(seed))
    spreads = {}
    factors = {'L0_xattn_q_b': 4.126, 'L0_xattn_k_b': 8.0}
    for name, (base, spread) in spreads.items():
        noise = np.random.default_rng([zlib.crc32(name.encode()), seed]).standard_normal(out[name].shape)
        drawn = base * np.exp(spread * noise) if base else spread * noise
        out[name] = jnp.asarray(drawn.astype(out[name].dtype))
    for name, factor in factors.items():
        out[name] = (out[name] * factor).astype(out[name].dtype)
    return out
```

```python
from contextlib import ExitStack

import numpy as np

import concourse.bass as bass
from concourse import mybir

F32 = mybir.dt.float32
F32R = mybir.dt.float32r
BF16 = mybir.dt.bfloat16
U32 = mybir.dt.uint32
U8 = mybir.dt.uint8
ALU = mybir.AluOpType
ACT = mybir.ActivationFunctionType
AX = mybir.AxisListType

P = 128
B, T, D = 4, 1024, 256
NT = T // P
NH, HD, DR, DC = 16, 16, 32, 128
NS, NSP = 77, 96
E = 8
HG = 4
NG = NH // HG
F = 512
NB = 2 * B * T // P + E
NB_B = NB // B
KROWS = 2 * (HD + DR)
ATT_SCALE = 1.0 / float(np.sqrt(HD + DR))
X_SCALE = 1.0 / 16.0
EPS = 1e-5
MASKED = -1e9 / X_SCALE
CAUSAL = -1e30
HALF = T // 2

W_KV, W_Q, W_QR, W_KU, W_VU, W_KR, W_O = 0, 256, 768, 896, 1152, 1408, 1472
W_COLS = 1984

PROJ = ([("x", c, h) for h in range(2) for c in range(2)] + [("ckv", 0, h) for h in range(2)]
        + [("q", c, h) for c in range(2) for h in range(2)] + [("k", c, h) for c in range(2) for h in range(2)]
        + [("qr", 0, h) for h in range(2)] + [("kr", 0, h) for h in range(2)] + [("v", 0, j) for j in range(4)])
N_PROJ = len(PROJ)
N_SPLIT = 14
RING = 6

S1_UNITS = [(i, h) for i in range(NT) for h in range(HG)]
N_S1 = len(S1_UNITS) + 1
S2_STEPS = [(j, c) for j in range(NT) for c in range(2) if c == 1 or j < NT // 2]
N_S2 = len(S2_STEPS) * HG
N_PV = len(S2_STEPS)


class Steps:

    def __init__(self, eng, sem, base, per):
        self.eng, self.sem, self.base, self.per, self.n = eng, sem, base, per, 0

    def __call__(self, ins):
        ins.then_inc(self.sem, 1)
        self.n += 1
        self.eng.wait_ge(self.sem, self.base * self.per + self.n)


def layer(nc, x, ctxT, mask, w_all, kwT, qw, vwT, qb, kb, vb, wrT, w1, w3, w2, ident, causal_q, causal_k, before,
          numbers, rope, out):
    ctx = ExitStack()
    with ctx:
        top = [16512]

        def at(name, shape, dt, offset=None):
            size = int(np.prod(shape[1:])) * mybir.dt.size(dt)
            if offset is None:
                offset = top[0]
                top[0] += (size + 63) // 64 * 64
            return nc.alloc_sbuf_tensor_at(name, shape, dt, offset=offset)

        def region(size):
            top[0] += size
            return top[0] - size

        def sem(name):
            return ctx.enter_context(nc.semaphore(name))

        idf = at("idf", [P, P], F32)
        cst_b = at("cst_b", [P, 3, P], BF16)

        idb, mask_q, mask_k = cst_b[:, 0, :], cst_b[:, 1, :], cst_b[:, 2, :]
        nhalf = at("nhalf", [P, NT], F32)
        gates = at("gates", [P, B * NT, 2], F32)
        picks = at("picks", [P, B * NT, 2], F32)
        kept = top[0]
        cs = at("cs", [2 * DR, T], F32)
        wh = at("wh", [P, W_COLS], F32R)
        wl = at("wl", [P, W_COLS], F32R)
        m_all = at("m_all", [P, 2, B, NSP], F32)
        brow = at("brow", [P, B, NSP], F32)
        vall = at("vall", [NSP, B, D], F32)
        wr = at("wr", [P, 2, NSP], F32)
        vaug = at("vaug", [P, NT, NH, HD + 1], F32)
        nmax = at("nmax", [P, HG * NT], F32)
        nmaxT = at("nmaxT", [HG * NT, P], F32R)
        xa = at("xa", [P, NT, D], F32)
        ckh = at("ckh", [P, T], F32R)
        ckl = at("ckl", [P, T], F32R)
        r2 = region(16384)
        xTh = at("xTh", [P, 2, T], F32R, r2)
        xTl = at("xTl", [P, 2, T], F32R, r2 + 8192)
        oT = at("oT", [P, NG, T], F32, r2)
        r1 = region(32768)
        stg = at("stg", [P, 4, 2, HALF], F32R, r1)
        rs = at("rs", [DR, 4, T], F32R, r1 + 16384)
        pT = at("pT", [P, 3, HG, HALF], F32, r1)
        kas = at("kas", [KROWS + 1, 2, HG, T], F32R)
        qs_at = region(32768)
        qs = at("qs", [KROWS + 1, 2, HG, T], F32R, qs_at)
        kbs_at = region(16384)
        kbs = at("kbs", [KROWS, HG, T], F32R, kbs_at)
        rt = at("rt", [DR, 3, HALF], F32, kbs_at)
        att = at("att", [P, NT, D], F32, qs_at)
        x1 = at("x1", [P, NT, D], F32, qs_at + 8192)
        x1T = at("x1T", [P, 2, NT, P], F32, qs_at + 16384)
        xr = at("xr", [P, NT, D], F32, qs_at + 24576)
        x2T = at("x2T", [P, 2, NT, P], F32, qs_at)
        sc = at("sc", [P, NT, NS], F32, kbs_at)
        keep = at("keep", [P, NT, NS], F32, kbs_at + 2496)
        neg = at("neg", [P, NT, NS], F32, kbs_at + 2 * 2496)
        mk = at("mk", [P, NT, NS], U8, kbs_at + 3 * 2496)
        pxT = at("pxT", [NSP, NT, P], F32, kbs_at + 3 * 2496 + 640)
        zero = at("zero", [P, D], F32)
        px = at("px", [P, NT, NSP], F32)
        x2 = at("x2", [P, NT, D], F32)
        atth = at("atth", [P, 2, 2, P], F32R)
        attl = at("attl", [P, 2, 2, P], F32R)
        rden = at("rden", [P, 2, NH], F32)
        st = at("st", [P, 2, NT, 6], F32)
        mv = at("mv", [P, 2, NT, 2], F32)
        ve = at("ve", [P, 2, NT], F32)
        rstd = at("rstd", [P, 2, NT], F32)
        sx = at("sx", [P, 3, NT], F32)
        lg = at("lg", [P, 3, NT, E], F32)
        top8 = at("top8", [P, NT, E], F32)
        idx8 = at("idx8", [P, NT, E], U32)
        sl = at("sl", [P, 4, NT], F32)
        w_in = at("w_in", [P, W_COLS], F32, r1)
        cst_f = at("cst_f", [P, 2, P], F32, qs_at + 13376)
        cxT = at("cxT", [P, 2, B * NS], F32, qs_at)
        kw_s = at("kw_s", [P, 2, D], F32, qs_at + 2560)
        qw_s = at("qw_s", [P, 2, D], F32, qs_at + 4608)
        vw_s = at("vw_s", [P, 2, D], F32, qs_at + 6656)
        kxT = at("kxT", [P, 2, B * NS], F32, qs_at + 8704)
        bias_s = at("bias_s", [P, 4], F32, qs_at + 11264)
        qb_b = at("qb_b", [P, 2, P], F32, qs_at + 11328)
        vb_b = at("vb_b", [P, D], F32, qs_at + 12352)

        ps = ctx.enter_context(nc.psum_tensor("ps", [P, 8, 512], F32))

        scr_q = nc.dram_tensor("scr_q", [B, 2, D, T], F32)
        scr_k = nc.dram_tensor("scr_k", [B, 2, D, T], F32)
        scr_x2 = nc.dram_tensor("scr_x2", [B, T, D], F32)
        xs = nc.dram_tensor("xs", [NB * P, D], F32)
        ys = nc.dram_tensor("ys", [NB * P, D], F32)

        s_w, s_cx, s_c = sem("w_loaded"), sem("ctx_loaded"), sem("consts_loaded")
        s_wh, s_wl, s_init = sem("w_high_done"), sem("w_low_done"), sem("init_done")
        s_qbb, s_xk, s_xk_read = sem("qb_spread"), sem("xk_ready"), sem("xk_read")
        s_xm, s_xm_read = sem("xm_ready"), sem("xm_read")
        with nc.Block() as block:
            @block.sync
            def _(sp):
                sp.dma_start(w_in[:, :], w_all).then_inc(s_w, 16)
                sp.dma_start(idf[:, :], ident).then_inc(s_c, 16)
                sp.dma_start(cst_f[:, 0, :], causal_q).then_inc(s_c, 16)
                sp.dma_start(cst_f[:, 1, :], causal_k).then_inc(s_c, 16)
                sp.dma_start(cs[:, :], rope).then_inc(s_c, 16)
                sp.wait_ge(s_init, 1)
                sp.dma_start(wr[:, :, 0:E], wrT.rearrange("(c p) e -> p c e", p=P)).then_inc(s_c, 16)

            @block.scalar
            def _(act):
                act.dma_start(cxT[:, :, :], ctxT.rearrange("(c p) n -> p c n", p=P)).then_inc(s_cx, 16)
                act.dma_start(kw_s[:, :, :], kwT.rearrange("(c p) n -> p c n", p=P)).then_inc(s_cx, 16)
                act.dma_start(qw_s[:, :, :], qw.rearrange("(c p) n -> p c n", p=P)).then_inc(s_cx, 16)
                act.dma_start(vw_s[:, :, :], vwT.rearrange("(c p) n -> p c n", p=P)).then_inc(s_cx, 16)
                act.dma_start(bias_s[:, 0:2], qb).then_inc(s_cx, 16)
                act.dma_start(bias_s[:, 2:4], kb).then_inc(s_cx, 16)
                act.dma_start(vb_b[:, :], vb.rearrange("(o n) -> o n", o=1).to_broadcast([P, D])).then_inc(s_cx, 16)
                act.wait_ge(s_w, 16)
                act.activation(wh[:, :], w_in[:, :], ACT.Copy).then_inc(s_wh, 1)

            @block.gpsimd
            def _(pool):
                pool.memset(wr[:, :, :], 0.0).then_inc(s_init, 1)
                pool.memset(m_all[:, :, :, :], 0.0).then_inc(s_init, 1)
                pool.memset(vall[:, :, :], 0.0).then_inc(s_init, 1)
                pool.memset(vaug[:, :, :, HD:HD + 1], 1.0).then_inc(s_init, 1)
                pool.memset(px[:, :, :], 0.0).then_inc(s_init, 1)
                pool.memset(zero[:, :], 0.0).then_inc(s_init, 1)
                pool.memset(nhalf[:, :], -0.5).then_inc(s_init, 1)
                pool.wait_ge(s_init, 7)
                pool.memset(kas[KROWS:KROWS + 1, :, :, :].bitcast(F32), 1.0).then_inc(s_init, 1)

            @block.vector
            def _(dve):
                dve.memset(ps[:, 6:8, :], 0.0).then_inc(s_wl, 1)
                dve.wait_ge(s_c, 80)
                dve.tensor_copy(cst_b[:, 0, :], idf[:, :]).then_inc(s_wl, 1)
                dve.tensor_copy(cst_b[:, 1:3, :], cst_f[:, :, :]).then_inc(s_wl, 1)
                dve.wait_ge(s_cx, 112)
                for c in range(2):
                    dve.tensor_copy(qb_b[:, c, :], bias_s[:, c:c + 1].to_broadcast([P, P])).then_inc(s_qbb, 1)
                dve.wait_ge(s_wh, 1)
                dve.tensor_tensor(wl[:, :], w_in[:, :], wh[:, :].bitcast(F32), ALU.subtract).then_inc(s_wl, 1)
                dve.wait_ge(s_init, 8)
                for c in range(2):
                    dve.wait_ge(s_xk, c + 1)
                    dve.tensor_scalar(kxT[:, c, :], ps[:, c, 0:B * NS], bias_s[:, 2 + c:3 + c], None,
                                      ALU.add).then_inc(s_xk_read, 1)
                for b in range(B):
                    dve.wait_ge(s_xk, 3 + b)
                    dve.tensor_tensor(vall[0:NS, b, :], ps[0:NS, 2 + b, 0:D], vb_b[0:NS, :],
                                      ALU.add).then_inc(s_xm_read, 1)
                for c in range(2):
                    dve.wait_ge(s_xm, c + 1)
                    dve.tensor_copy(m_all[:, c, :, 0:NS],
                                    ps[:, c, 0:B * NS].rearrange("p (b n) -> p b n", b=B)).then_inc(s_xm_read, 1)
                dve.wait_ge(s_xm, 3)
                dve.tensor_copy(brow[:, :, 0:NS],
                                ps[:, 2, 0:B * NS].rearrange("p (b n) -> p b n", b=B)).then_inc(s_xm_read, 1)

            @block.tensor
            def _(pe):
                pe.wait_ge(s_cx, 112)
                for c in range(2):
                    for m in range(2):
                        ins = pe.matmul(ps[:, c, 0:B * NS], kw_s[:, m, c * P:(c + 1) * P], cxT[:, m, :],
                                        start=m == 0, stop=m == 1)
                    ins.then_inc(s_xk, 1)
                for b in range(B):
                    for m in range(2):
                        ins = pe.matmul(ps[0:NS, 2 + b, 0:D], cxT[:, m, b * NS:(b + 1) * NS], vw_s[:, m, :],
                                        start=m == 0, stop=m == 1)
                    ins.then_inc(s_xk, 1)
                pe.wait_ge(s_xk_read, 2)
                for c in range(2):
                    for q in range(2):
                        ins = pe.matmul(ps[:, c, 0:B * NS], qw_s[:, q, c * P:(c + 1) * P], kxT[:, q, :],
                                        start=q == 0, stop=q == 1)
                    ins.then_inc(s_xm, 1)
                pe.wait_ge(s_qbb, 2)
                pe.wait_ge(s_xm_read, 1)
                for q in range(2):
                    ins = pe.matmul(ps[:, 2, 0:B * NS], qb_b[:, q, :], kxT[:, q, :], start=q == 0, stop=q == 1)
                ins.then_inc(s_xm, 1)

        s_x = sem("x_loaded")
        s_pr, s_ph, s_pl = sem("proj_ready"), sem("proj_high"), sem("proj_low")
        s_rr, s_rs, s_vc = sem("rope_psum_read"), sem("rope_done"), sem("v_copied")
        s_stg = [sem(f"stage{i}_saved") for i in range(4)]
        s_qk = [[sem(f"heads_set{p}_half{h}") for h in range(2)] for p in range(2)]
        s_kb = [sem(f"klow_half{h}") for h in range(2)]
        s_s1, s_s1r = sem("scores_for_max"), sem("max_taken")
        s_mx = sem("max_rows_placed")
        s_s2, s_exp, s_pv = sem("scores_ready"), sem("probs_ready"), sem("probs_used")
        s_oT = sem("heads_out_copied")
        s_xr, s_mk = sem("residual_loaded"), sem("mask_loaded")
        s_t1, s_t1r = sem("attn_turned"), sem("attn_normed")
        s_t2, s_t2h, s_t2l = sem("attnT_ready"), sem("attnT_high"), sem("attnT_low")
        s_t3, s_t3r = sem("y_ready"), sem("y_added")
        s_ve1, s_pow1, s_ln1 = sem("var1_ready"), sem("rstd1_ready"), sem("x1_ready")
        s_t4, s_t4r = sem("x1T_ready"), sem("x1T_copied")
        s_t5, s_t5r, s_sh = sem("xscores_ready"), sem("xscores_read"), sem("xscores_shifted")
        s_xe = sem("xprobs_ready")
        s_t6, s_t6r = sem("xprobsT_ready"), sem("xprobsT_copied")
        s_t7, s_t7r = sem("xy_ready"), sem("xy_added")
        s_ve2, s_pow2, s_ln2 = sem("var2_ready"), sem("rstd2_ready"), sem("x2_ready")
        s_x2s = sem("x2_saved")
        s_t8, s_t8r = sem("x2T_ready"), sem("x2T_copied")
        s_t9, s_t9r, s_le, s_lex = sem("logits_ready"), sem("logits_read"), sem("logits_shifted"), sem("logits_exp")
        s_zero = sem("sorted_rows_zeroed")
        s_stat, s_agg = sem("stats_ready"), sem("mean_var_ready")
        s_dve = sem("dve_step")

        DVE_STEPS = 4 * 2 + 1 + NT + 5 + 9

        def s1_at(g, n):
            return g * N_S1 + n

        def ring(i):
            return ps[:, i % RING, :]

        with nc.Block() as block:
            @block.gpsimd
            def _(pool):
                with pool.Fori(0, B) as b:
                    pool.dma_start(xa[:, :, :], x[bass.ds(b, 1)].rearrange("o (t p) d -> p (o t) d", p=P)).then_inc(s_x, 16)
                    pool.dma_start(xs[bass.ds(b * NB_B * P, NB_B * P)].rearrange("(n p) d -> p n d", p=P),
                                   zero[:, :].rearrange("p (o d) -> p o d", o=1).to_broadcast([P, NB_B, D])
                                   ).then_inc(s_zero, 16)
                    pool.wait_ge(s_ve1, b + 1)
                    pool.tensor_tensor(rstd[:, 0, :], ve[:, 0, :], nhalf[:, :], ALU.pow).then_inc(s_pow1, 1)
                    pool.wait_ge(s_ve2, b + 1)
                    pool.tensor_tensor(rstd[:, 1, :], ve[:, 1, :], nhalf[:, :], ALU.pow).then_inc(s_pow2, 1)

            @block.sync
            def _(sp):
                def load_heads(b, g, h):
                    p, cols = g % 2, slice(h * HALF, (h + 1) * HALF)
                    for scr, dst, parts in ((scr_q, qs, (0, 1)), (scr_k, kas, (0, 0))):
                        for r, part in enumerate(parts):
                            src = scr[bass.ds(b, 1), part, g * HG * HD:(g + 1) * HG * HD, cols]
                            sp.dma_start(dst[r * HD:(r + 1) * HD, p, :, cols].bitcast(F32),
                                         src.rearrange("o (h r) n -> r (o h) n", r=HD)).then_inc(s_qk[p][h], 16)

                def load_klow(b, g, h):
                    cols = slice(h * HALF, (h + 1) * HALF)
                    for r in range(2):
                        src = scr_k[bass.ds(b, 1), 1, g * HG * HD:(g + 1) * HG * HD, cols]
                        sp.dma_start(kbs[r * HD:(r + 1) * HD, :, cols].bitcast(F32),
                                     src.rearrange("o (h r) n -> r (o h) n", r=HD)).then_inc(s_kb[h], 16)

                def place_rope(dst, part, sem_):
                    for h in range(2):
                        cols = slice(h * HALF, (h + 1) * HALF)
                        for k in range(2):
                            src = rs[:, part + (k if part == 0 else 0), cols].bitcast(F32)
                            sp.dma_start(dst[DR + k * DR:2 * DR + k * DR, :, cols].bitcast(F32),
                                         src.rearrange("p (o n) -> p o n", o=1).to_broadcast([DR, HG, HALF])
                                         ).then_inc(sem_[h], 16)

                with sp.Fori(0, B) as b:
                    for m in range(8):
                        name, c, h = PROJ[6 + m]
                        sp.wait_ge(s_pl, b * N_SPLIT + 7 + m)
                        dst = (scr_q if name == "q" else scr_k)[bass.ds(b, 1), :, c * P:(c + 1) * P, h * HALF:(h + 1) * HALF]
                        sp.dma_start(dst.rearrange("o s p n -> p (o s) n"), stg[:, m % 4, :, :].bitcast(F32)
                                     ).then_inc(s_stg[m % 4], 16)
                    for s in s_stg:
                        sp.wait_ge(s, b * 32 + 32)
                    for h in range(2):
                        load_heads(b, 0, h)
                    sp.wait_ge(s_rs, b * 4 + 4)
                    place_rope(qs[:, 0], 0, s_qk[0])
                    place_rope(kas[:, 0], 2, s_qk[0])
                    for h in range(2):
                        load_klow(b, 0, h)
                    place_rope(kbs, 3, s_kb)
                    for h in range(2):
                        load_heads(b, 1, h)
                    place_rope(qs[:, 1], 0, s_qk[1])
                    place_rope(kas[:, 1], 2, s_qk[1])
                    for g in range(NG):
                        sp.wait_ge(s_s1r, b * NG * N_S1 + s1_at(g + 1, 0))
                        sp.dma_start(qs[KROWS:KROWS + 1, g % 2, :, :].bitcast(F32),
                                     nmaxT[:, :].bitcast(F32)).then_inc(s_mx, 16)
                        if g >= 1:
                            for h in range(2):
                                sp.wait_ge(s_s2, (b * NG + g - 1) * N_S2 + (8 * HG if h == 0 else N_S2))
                                load_klow(b, g, h)
                                if g + 1 < NG:
                                    load_heads(b, g + 1, h)
                    sp.wait_ge(s_s2, (b + 1) * NG * N_S2)
                    sp.dma_start(xr[:, :, :], x[bass.ds(b, 1)].rearrange("o (t p) d -> p (o t) d", p=P)).then_inc(s_xr, 16)
                    sp.dma_start(mk[:, :, :], mask[bass.ds(b, 1)].rearrange("o (t p) n -> p (o t) n", p=P)).then_inc(s_mk, 16)
                    sp.wait_ge(s_ln2, (b + 1) * NT)
                    sp.dma_start(scr_x2[bass.ds(b, 1)].rearrange("o (t p) d -> p (o t) d", p=P), x2[:, :, :]).then_inc(s_x2s, 16)

            @block.tensor
            def _(pe):
                def products(outp, terms, last=True, first=True):
                    for n, (a, w) in enumerate(terms):
                        ins = pe.matmul(outp, a, w, start=first and n == 0, stop=last and n == len(terms) - 1)
                    return ins

                def parts(ah, al, bh, bl):
                    return [(ah, bh), (al, bh), (ah, bl)]

                def wsl(o, n):
                    return wh[:, o:o + n], wl[:, o:o + n]

                def s1_unit(b, g, n):
                    slot = (s1_at(g, n) % 2) * 2
                    if s1_at(g, n) >= 2:
                        pe.wait_ge(s_s1r, b * NG * N_S1 + s1_at(g, n) - 1)
                    if n < N_S1 - 1:
                        i, h = S1_UNITS[n]
                        for bank in range((i * P) // HALF + 1):
                            k0, k1 = bank * HALF, min((bank + 1) * HALF, (i + 1) * P)
                            diag = k1 == (i + 1) * P
                            ins = pe.matmul(ps[:, slot + bank, 0:k1 - k0], qs[0:KROWS, g % 2, h, i * P:(i + 1) * P],
                                            kas[0:KROWS, g % 2, h, k0:k1], start=True, stop=not diag)
                            if diag:
                                ins = pe.matmul(ps[:, slot + bank, i * P - k0:k1 - k0], idb, mask_q,
                                                start=False, stop=True)
                        ins.then_inc(s_s1, 1)
                    else:
                        pe.wait_ge(s_s1r, b * NG * N_S1 + s1_at(g, n))
                        pe.transpose(ps[0:HG * NT, slot, 0:P], nmax[:, :], idf[:, :]).then_inc(s_s1, 1)

                def s2_unit(b, g, u, h):
                    n = g * N_S2 + u * HG + h
                    j, c = S2_STEPS[u]
                    q0, q1 = max(j * P, c * HALF), (c + 1) * HALF
                    o = ps[:, 4 + n % 2, 0:q1 - q0]
                    if n >= 2:
                        pe.wait_ge(s_exp, b * NG * N_S2 + n - 1)
                    diag = q0 == j * P
                    pe.matmul(o, kas[:, g % 2, h, j * P:(j + 1) * P], qs[:, g % 2, h, q0:q1], start=True, stop=False)
                    ins = pe.matmul(o, kbs[:, h, j * P:(j + 1) * P], qs[0:KROWS, g % 2, h, q0:q1],
                                    start=False, stop=not diag)
                    if diag:
                        ins = pe.matmul(o[:, 0:P], idb, mask_k, start=False, stop=True)
                    ins.then_inc(s_s2, 1)

                def pv_step(b, g, u):
                    j, c = S2_STEPS[u]
                    q0, q1 = max(j * P, c * HALF), (c + 1) * HALF
                    if u == 0 and g > 0:
                        pe.wait_ge(s_oT, b * NG + g)
                    pe.wait_ge(s_exp, (b * NG + g) * N_S2 + (u + 1) * HG)
                    last = S2_STEPS.index((3, 0)) if c == 0 else N_PV - 1
                    for h in range(HG):
                        ins = pe.matmul(ps[h * 32:h * 32 + HD + 1, 6 + c, q0 - c * HALF:HALF],
                                        vaug[:, j, g * HG + h, :], pT[:, u % 3, h, 0:q1 - q0],
                                        start=j == 0, stop=u == last, tile_position=(0, h * 32))
                    ins.then_inc(s_pv, 1)

                with pe.Fori(0, B) as b:
                    freed = {"v": (s_vc, 4), "qr": (s_rr, 4), "kr": (s_rr, 4)}
                    pe.wait_ge(s_x, b * 16 + 16)
                    for u, (name, c, h) in enumerate(PROJ):
                        cols = slice(h * HALF, (h + 1) * HALF)
                        if u >= RING:
                            prev = PROJ[u - RING][0]
                            s, per = freed.get(prev, (s_pl, N_SPLIT))
                            k = sum(freed.get(p[0], (s_pl, 0))[0] is s for p in PROJ[:u - RING + 1])
                            pe.wait_ge(s, b * per + k)
                        o = ring(u)
                        if name == "x":
                            for t in range(4):
                                ins = pe.transpose(o[:, t * P:(t + 1) * P], xa[:, h * 4 + t, c * P:(c + 1) * P], idf[:, :])
                        elif name == "ckv":
                            pe.wait_ge(s_pl, b * N_SPLIT + 2 * (h + 1))
                            terms = []
                            for m in range(2):
                                terms += parts(*wsl(W_KV + m * DC, DC), xTh[:, m, cols], xTl[:, m, cols])
                            ins = products(o, terms)
                        elif name == "q":
                            terms = []
                            for m in range(2):
                                terms += parts(*wsl(W_Q + m * D + c * P, P), xTh[:, m, cols], xTl[:, m, cols])
                            ins = products(o, terms)
                        elif name == "k":
                            pe.wait_ge(s_pl, b * N_SPLIT + 6)
                            ins = products(o, parts(*wsl(W_KU + c * P, P), ckh[:, cols], ckl[:, cols]))
                        elif name == "qr":
                            terms = []
                            for m in range(2):
                                terms += parts(*wsl(W_QR + m * 2 * DR, 2 * DR), xTh[:, m, cols], xTl[:, m, cols])
                            ins = products(o[0:2 * DR, :], terms)
                        elif name == "kr":
                            ins = products(o[0:2 * DR, :], parts(*wsl(W_KR, 2 * DR), ckh[:, cols], ckl[:, cols]))
                        else:
                            for t in range(2):
                                tok = slice((2 * h + t) * P, (2 * h + t + 1) * P)
                                vh, vl = wsl(W_VU, D)
                                ins = products(o[:, t * D:(t + 1) * D], [(ckh[:, tok], vh), (ckl[:, tok], vh), (ckh[:, tok], vl)])
                        ins.then_inc(s_pr, 1)
                    pe.wait_ge(s_vc, b * 4 + 4)
                    pe.wait_ge(s_rr, b * 4 + 4)

                    def heads_here(g, h):
                        p, k = g % 2, g // 2
                        pe.wait_ge(s_qk[p][h], b * 192 + (128 if k == 0 else 192))

                    def klow_here(g, h):
                        pe.wait_ge(s_kb[h], b * 160 + 64 + 32 * g)

                    heads_here(0, 0)
                    for n in range(N_S1):
                        if n == 16:
                            heads_here(0, 1)
                        s1_unit(b, 0, n)
                    for g in range(NG):
                        pe.wait_ge(s_mx, (b * NG + g + 1) * 16)
                        klow_here(g, 0)
                        done = 0
                        for u in range(N_PV):
                            if u == 8:
                                klow_here(g, 1)
                            for h in range(HG):
                                s2_unit(b, g, u, h)
                                k = u * HG + h
                                while g + 1 < NG and done < N_S1 and done * 38 < (k - 4) * N_S1:
                                    if done == 0:
                                        heads_here(g + 1, 0)
                                    if done == 16:
                                        heads_here(g + 1, 1)
                                    s1_unit(b, g + 1, done)
                                    done += 1
                            if u >= 1:
                                pv_step(b, g, u - 1)
                        pv_step(b, g, N_PV - 1)
                        assert g + 1 == NG or done == N_S1

                    pe.wait_ge(s_oT, b * NG + NG)
                    for t in range(NT + 1):
                        if t < NT:
                            if t >= 2:
                                pe.wait_ge(s_t1r, b * NT + t - 1)
                            for g in range(NG):
                                ins = pe.transpose(ps[:, t % 2, g * P:(g + 1) * P], oT[:, g, t * P:(t + 1) * P], idf[:, :])
                            ins.then_inc(s_t1, 1)
                        if t >= 1:
                            u = t - 1
                            pe.wait_ge(s_t1r, b * NT + u + 1)
                            if u >= 2:
                                pe.wait_ge(s_t2l, b * NT + u - 1)
                            for c in range(2):
                                ins = pe.transpose(ps[:, 2 + u % 2, c * P:(c + 1) * P], att[:, u, c * P:(c + 1) * P], idf[:, :])
                            ins.then_inc(s_t2, 1)
                            pe.wait_ge(s_t2l, b * NT + u + 1)
                            if u >= 2:
                                pe.wait_ge(s_t3r, b * NT + u - 1)
                            terms = []
                            for c in range(2):
                                vh, vl = wsl(W_O + c * D, D)
                                terms += [(atth[:, u % 2, c, :], vh), (attl[:, u % 2, c, :], vh), (atth[:, u % 2, c, :], vl)]
                            products(ps[:, 4 + u % 2, 0:D], terms).then_inc(s_t3, 1)

                    def turn(src, ready, done_sem, copied):
                        for t in range(NT):
                            pe.wait_ge(ready, b * NT + t + 1)
                            if t >= 2:
                                pe.wait_ge(copied, b * NT + t - 1)
                            for c in range(2):
                                ins = pe.transpose(ps[:, t % 2, c * P:(c + 1) * P], src[:, t, c * P:(c + 1) * P], idf[:, :])
                            ins.then_inc(done_sem, 1)

                    turn(x1, s_ln1, s_t4, s_t4r)
                    for hf in range(2):
                        pe.wait_ge(s_t4r, b * NT + 4 * hf + 4)
                        for t in range(4 * hf, 4 * hf + 4):
                            for c in range(2):
                                ins = pe.matmul(ps[:, 2 + hf, (t % 4) * NSP:(t % 4 + 1) * NSP], x1T[:, c, t, :],
                                                m_all[:, c, bass.ds(b, 1), :].rearrange("p o n -> p (o n)"),
                                                start=c == 0, stop=c == 1)
                        ins.then_inc(s_t5, 1)
                    pe.wait_ge(s_xe, b + 1)
                    for hf in range(2):
                        for t in range(4 * hf, 4 * hf + 4):
                            ins = pe.transpose(ps[0:NSP, 4 + hf, (t % 4) * P:(t % 4 + 1) * P], px[:, t, :], idf[:, :])
                        ins.then_inc(s_t6, 1)
                    for t in range(NT):
                        pe.wait_ge(s_t6r, b * 2 + t // 4 + 1)
                        if t >= 2:
                            pe.wait_ge(s_t7r, b * NT + t - 1)
                        pe.matmul(ps[:, 6 + t % 2, 0:D], pxT[:, t, :],
                                  vall[:, bass.ds(b, 1), :].rearrange("p o n -> p (o n)"),
                                  start=True, stop=True).then_inc(s_t7, 1)
                    turn(x2, s_ln2, s_t8, s_t8r)
                    for hf in range(2):
                        pe.wait_ge(s_t8r, b * NT + 4 * hf + 4)
                        for t in range(4 * hf, 4 * hf + 4):
                            for c in range(2):
                                ins = pe.matmul(ps[:, 2 + hf, (t % 4) * NSP:(t % 4 + 1) * NSP], x2T[:, c, t, :], wr[:, c, :],
                                                start=c == 0, stop=c == 1)
                        ins.then_inc(s_t9, 1)
                    pe.wait_ge(s_t9r, b * 2 + 2)

            @block.scalar
            def _(act):
                with act.Fori(0, B) as b:
                    def high(unit, dst):
                        act.wait_ge(s_pr, b * N_PROJ + unit + 1)
                        act.activation(dst, ring(unit), ACT.Copy).then_inc(s_ph, 1)

                    for u, (name, c, h) in enumerate(PROJ):
                        cols = slice(h * HALF, (h + 1) * HALF)
                        if name == "x":
                            high(u, xTh[:, c, cols])
                        elif name == "ckv":
                            high(u, ckh[:, cols])
                        elif name in "qk":
                            m = u - 6
                            if m >= 4:
                                act.wait_ge(s_stg[m % 4], b * 32 + 16)
                            high(u, stg[:, m % 4, 0, :])
                        elif name == "v":
                            act.wait_ge(s_pr, b * N_PROJ + u + 1)
                            act.activation(vaug[:, 2 * h:2 * h + 2, :, 0:HD],
                                           ring(u).rearrange("p (t h d) -> p t h d", t=2, h=NH), ACT.Copy).then_inc(s_vc, 1)
                    for g in range(NG):
                        for u, (j, c) in enumerate(S2_STEPS):
                            n_q = (c + 1) * HALF - max(j * P, c * HALF)
                            if g * N_PV + u >= 3:
                                act.wait_ge(s_pv, b * NG * N_PV + g * N_PV + u - 2)
                            for h in range(HG):
                                n = g * N_S2 + u * HG + h
                                act.wait_ge(s_s2, b * NG * N_S2 + n + 1)
                                act.activation(pT[:, u % 3, h, 0:n_q], ps[:, 4 + n % 2, 0:n_q], ACT.Exp,
                                               scale=ATT_SCALE).then_inc(s_exp, 1)
                        act.wait_ge(s_pv, (b * NG + g + 1) * N_PV)
                        act.activation(oT[:, g, :], ps[:, 6:8, :].rearrange("p c n -> p (c n)"), ACT.Copy).then_inc(s_oT, 1)
                    for t in range(NT):
                        act.wait_ge(s_t2, b * NT + t + 1)
                        if t >= 2:
                            act.wait_ge(s_t3, b * NT + t - 1)
                        act.activation(atth[:, t % 2, :, :], ps[:, 2 + t % 2, 0:D].rearrange("p (c n) -> p c n", c=2),
                                       ACT.Copy).then_inc(s_t2h, 1)

                    def copies(ready, dst, done_sem):
                        for t in range(NT):
                            act.wait_ge(ready, b * NT + t + 1)
                            act.activation(dst[:, :, t, :], ps[:, t % 2, 0:D].rearrange("p (c n) -> p c n", c=2),
                                           ACT.Copy).then_inc(done_sem, 1)

                    copies(s_t4, x1T, s_t4r)
                    act.wait_ge(s_sh, b + 1)
                    act.activation(px[:, :, 0:NS], sc[:, :, :], ACT.Exp, scale=X_SCALE).then_inc(s_xe, 1)
                    for hf in range(2):
                        act.wait_ge(s_t6, b * 2 + hf + 1)
                        act.activation(pxT[:, 4 * hf:4 * hf + 4, :],
                                       ps[0:NSP, 4 + hf, :].rearrange("p (t n) -> p t n", t=4), ACT.Copy).then_inc(s_t6r, 1)
                    copies(s_t8, x2T, s_t8r)
                    act.wait_ge(s_le, b + 1)
                    act.activation(lg[:, 1, :, :], lg[:, 0, :, :], ACT.Exp).then_inc(s_lex, 1)
                    act.wait_ge(s_x2s, b * 16 + 16)

            @block.vector
            def _(dve):
                with dve.Fori(0, B) as b:
                    step = Steps(dve, s_dve, b, DVE_STEPS)

                    def low(s, unit, dst, high_):
                        dve.wait_ge(s_ph, b * N_SPLIT + s + 1)
                        dve.tensor_tensor(dst, ring(unit), high_.bitcast(F32), ALU.subtract).then_inc(s_pl, 1)

                    for u, (name, c, h) in enumerate(PROJ):
                        cols = slice(h * HALF, (h + 1) * HALF)
                        if name == "x":
                            low(u, u, xTl[:, c, cols], xTh[:, c, cols])
                        elif name == "ckv":
                            low(u, u, ckl[:, cols], ckh[:, cols])
                        elif name in "qk":
                            m = u - 6
                            low(u, u, stg[:, m % 4, 1, :], stg[:, m % 4, 0, :])
                        elif name in ("qr", "kr"):
                            o, part = ring(u), 0 if name == "qr" else 2
                            dve.wait_ge(s_pr, b * N_PROJ + u + 1)
                            dve.tensor_tensor(rt[:, 0, :], o[0:DR, :], cs[0:DR, cols], ALU.mult)
                            ins = dve.tensor_tensor(rt[:, 1, :], o[DR:2 * DR, :], cs[DR:2 * DR, cols], ALU.mult)
                            ins.then_inc(s_rr, 1)
                            dve.wait_ge(s_rr, b * 4 + (part + h + 1))
                            step(dve.tensor_tensor(rt[:, 2, :], rt[:, 0, :], rt[:, 1, :], ALU.add))
                            step(dve.tensor_copy(rs[:, part, cols], rt[:, 2, :]))
                            dve.tensor_tensor(rs[:, part + 1, cols], rt[:, 2, :], rs[:, part, cols].bitcast(F32),
                                              ALU.subtract).then_inc(s_rs, 1)
                            dve.wait_ge(s_rs, b * 4 + (part + h + 1))
                    for g in range(NG):
                        for n in range(N_S1):
                            slot = (s1_at(g, n) % 2) * 2
                            dve.wait_ge(s_s1, b * NG * N_S1 + s1_at(g, n) + 1)
                            if n < N_S1 - 1:
                                i, h = S1_UNITS[n]
                                k = h * NT + i
                                dve.tensor_reduce(nmax[:, k:k + 1],
                                                  ps[:, slot:slot + 2, :].rearrange("p s n -> p (s n)")[:, 0:(i + 1) * P],
                                                  AX.X, ALU.max, negate=True).then_inc(s_s1r, 1)
                            else:
                                if g > 0:
                                    dve.wait_ge(s_mx, (b * NG + g) * 16)
                                dve.tensor_copy(nmaxT[:, :], ps[0:HG * NT, slot, 0:P]).then_inc(s_s1r, 1)
                    dve.wait_ge(s_xr, b * 16 + 16)
                    dve.wait_ge(s_mk, b * 16 + 16)
                    dve.tensor_scalar(keep[:, :, :], mk[:, :, :], -1.0, 1.0, ALU.mult, ALU.add)
                    step(dve.tensor_scalar(neg[:, :, :], mk[:, :, :], MASKED, None, ALU.mult))

                    def stats(k, t, src):
                        if t > 0:
                            dve.wait_ge(s_stat, b * 2 * NT + k * NT + t)
                        dve.bn_stats(st[:, k, t, :], src).then_inc(s_stat, 1)
                        if t > 0:
                            dve.bn_aggr(mv[:, k, t - 1, :], st[:, k, t - 1, :]).then_inc(s_agg, 1)

                    for t in range(NT + 1):
                        if t < NT:
                            dve.wait_ge(s_t1, b * NT + t + 1)
                            po = ps[:, t % 2, :].rearrange("p (h d) -> p h d", h=NH)
                            step(dve.reciprocal(rden[:, t % 2, :], po[:, :, HD]))
                            dve.tensor_tensor(att[:, t, :].rearrange("p (h d) -> p h d", h=NH), po[:, :, 0:HD],
                                              rden[:, t % 2, :].rearrange("p (h o) -> p h o", o=1).to_broadcast([P, NH, HD]),
                                              ALU.mult).then_inc(s_t1r, 1)
                        if t >= 1:
                            u = t - 1
                            dve.wait_ge(s_t2h, b * NT + u + 1)
                            dve.tensor_tensor(attl[:, u % 2, :, :], ps[:, 2 + u % 2, 0:D].rearrange("p (c n) -> p c n", c=2),
                                              atth[:, u % 2, :, :].bitcast(F32), ALU.subtract).then_inc(s_t2l, 1)
                            dve.wait_ge(s_t3, b * NT + u + 1)
                            dve.tensor_tensor(x1[:, u, :], ps[:, 4 + u % 2, 0:D], xr[:, u, :], ALU.add).then_inc(s_t3r, 1)
                            dve.wait_ge(s_t3r, b * NT + u + 1)
                            stats(0, u, x1[:, u, :])

                    def norm(k, buf, s_ve, s_pow, s_ln):
                        def add_eps(t0, t1, n):
                            dve.wait_ge(s_agg, b * 2 * NT + k * NT + n)
                            return dve.tensor_scalar(ve[:, k, t0:t1], mv[:, k, t0:t1, 1], EPS, None, ALU.add)

                        dve.wait_ge(s_stat, b * 2 * NT + (k + 1) * NT)
                        add_eps(0, NT - 1, NT - 1)
                        dve.bn_aggr(mv[:, k, NT - 1, :], st[:, k, NT - 1, :]).then_inc(s_agg, 1)
                        add_eps(NT - 1, NT, NT).then_inc(s_ve, 1)
                        dve.wait_ge(s_pow, b + 1)
                        for t in range(NT):
                            dve.tensor_scalar(buf[:, t, :], buf[:, t, :], mv[:, k, t, 0:1], rstd[:, k, t:t + 1],
                                              ALU.subtract, ALU.mult).then_inc(s_ln, 1)

                    norm(0, x1, s_ve1, s_pow1, s_ln1)
                    for hf in range(2):
                        dve.wait_ge(s_t5, b * 2 + hf + 1)
                        ins = dve.tensor_tensor(
                            sc[:, 4 * hf:4 * hf + 4, :],
                            ps[:, 2 + hf, 0:4 * NSP].rearrange("p (t n) -> p t n", t=4)[:, :, 0:NS],
                            brow[:, bass.ds(b, 1), 0:NS].to_broadcast([P, 4, NS]), ALU.add)
                    ins.then_inc(s_t5r, 1)
                    dve.wait_ge(s_t5r, b + 1)
                    step(dve.tensor_tensor(sc[:, :, :], sc[:, :, :], keep[:, :, :], ALU.mult))
                    step(dve.tensor_tensor(sc[:, :, :], sc[:, :, :], neg[:, :, :], ALU.add))
                    step(dve.tensor_reduce(sx[:, 0, :], sc[:, :, :], AX.X, ALU.max))
                    dve.tensor_tensor(sc[:, :, :], sc[:, :, :],
                                      sx[:, 0, :].rearrange("p (t o) -> p t o", o=1).to_broadcast([P, NT, NS]),
                                      ALU.subtract).then_inc(s_sh, 1)
                    dve.wait_ge(s_xe, b + 1)
                    step(dve.tensor_reduce(sx[:, 1, :], px[:, :, 0:NS], AX.X, ALU.add))
                    step(dve.reciprocal(sx[:, 2, :], sx[:, 1, :]))
                    for t in range(NT):
                        dve.wait_ge(s_t7, b * NT + t + 1)
                        dve.scalar_tensor_tensor(x2[:, t, :], ps[:, 6 + t % 2, 0:D], sx[:, 2, t:t + 1], x1[:, t, :],
                                                 ALU.mult, ALU.add).then_inc(s_t7r, 1)
                        dve.wait_ge(s_t7r, b * NT + t + 1)
                        stats(1, t, x2[:, t, :])
                    norm(1, x2, s_ve2, s_pow2, s_ln2)
                    for hf in range(2):
                        dve.wait_ge(s_t9, b * 2 + hf + 1)
                        ins = dve.tensor_copy(lg[:, 0, 4 * hf:4 * hf + 4, :],
                                              ps[:, 2 + hf, 0:4 * NSP].rearrange("p (t n) -> p t n", t=4)[:, :, 0:E])
                        ins.then_inc(s_t9r, 1)
                    dve.wait_ge(s_t9r, b * 2 + 2)
                    step(dve.tensor_reduce(sl[:, 0, :], lg[:, 0, :, :], AX.X, ALU.max))
                    dve.tensor_tensor(lg[:, 0, :, :], lg[:, 0, :, :],
                                      sl[:, 0, :].rearrange("p (t o) -> p t o", o=1).to_broadcast([P, NT, E]),
                                      ALU.subtract).then_inc(s_le, 1)
                    dve.wait_ge(s_lex, b + 1)
                    step(dve.tensor_reduce(sl[:, 1, :], lg[:, 1, :, :], AX.X, ALU.add))
                    step(dve.reciprocal(sl[:, 2, :], sl[:, 1, :]))
                    halves = [slice(0, NT // 2), slice(NT // 2, NT)]

                    def over(buf, j):
                        return sl[:, j, :].rearrange("p (t o) -> p t o", o=1)[:, buf, :]

                    def probs(hf):
                        return dve.tensor_tensor(lg[:, 2, hf, :], lg[:, 1, hf, :], over(hf, 2).to_broadcast([P, NT // 2, E]), ALU.mult)

                    def find(call, hf):
                        for t in range(hf.start, hf.stop):
                            ins = call(t)
                        return ins

                    def best(t):
                        return dve.max(top8[:, t, :], lg[:, 2, t, :])

                    def where(t):
                        return dve.max_index(idx8[:, t, :], top8[:, t, :], lg[:, 2, t, :])

                    def both(hf):
                        return dve.tensor_tensor(sl[:, 3, hf], top8[:, hf, 0], top8[:, hf, 1], ALU.add)

                    step(probs(halves[0]))
                    probs(halves[1]).then_inc(s_dve, 1)
                    find(best, halves[0]).then_inc(s_dve, 1)
                    step.n += 2
                    dve.wait_ge(s_dve, b * DVE_STEPS + step.n)
                    both(halves[0])
                    step(find(best, halves[1]))
                    both(halves[1])
                    find(where, halves[0])
                    step(find(where, halves[1]))
                    step(dve.reciprocal(sl[:, 0, :], sl[:, 3, :]))
                    dve.tensor_tensor(gates[:, bass.ds(b * NT, NT), :], top8[:, :, 0:2],
                                      sl[:, 0, :].rearrange("p (t o) -> p t o", o=1).to_broadcast([P, NT, 2]), ALU.mult)
                    dve.tensor_copy(picks[:, bass.ds(b * NT, NT), :], idx8[:, :, 0:2])
                    assert step.n == DVE_STEPS, (step.n, DVE_STEPS)

        NTT = B * NT
        top[0] = kept
        w1h = at("w1h", [P, E, 2, F], F32R)
        w1l = at("w1l", [P, E, 2, F], F32R)
        w3h = at("w3h", [P, E, 2, F], F32R)
        w3l = at("w3l", [P, E, 2, F], F32R)
        w2s = at("w2s", [P, E, F // P, D], F32)
        x2r = at("x2r", [P, 2, NT, D], F32)
        xb = at("xb", [P, 2, D], F32)
        work = top[0]
        xbh = at("xbh", [P, 2, 2, P], F32R)
        xbl = at("xbl", [P, 2, 2, P], F32R)
        sil = at("sil", [P, 2, F], F32)
        hid = at("hid", [P, 2, F], F32)
        hidT = at("hidT", [P, 2, F // P, P], F32)
        yb = at("yb", [P, 2, D], F32)
        w_stage = at("w_stage", [P, 4, 2, F], F32, work)
        slots = at("slots", [P, 2, NTT], U32)
        owner = at("owner", [P, NB], U32)
        got = at("got", [P, 8, 2, D], F32, kept)
        z = at("z", [P, 2, NT, D], F32, kept + 16384)
        zst = at("zst", [P, 2, NT, 6], F32, kept + 32768)
        zmv = at("zmv", [P, 2, NT, 2], F32, kept + 33280)
        zve = at("zve", [P, 2, NT], F32, kept + 33536)
        zrs = at("zrs", [P, 2, NT], F32, kept + 33664)
        rout = kept + 131072
        one = at("one", [P, P], F32, rout)
        bef = at("bef", [P, P], F32, rout + 512)
        num = at("num", [P, NB], F32, rout + 1024)
        oh = at("oh", [P, 3, NTT, E], F32, rout + 1536)
        run_ = at("run_", [P, NTT, E], F32, rout + 4608)
        tot = at("tot", [P, NTT, E], F32, rout + 5632)
        pos = at("pos", [P, NTT, E], F32, rout + 6656)
        sel = at("sel", [P, 2, NTT, E], F32, rout + 7680)
        slf = at("slf", [P, 2, NTT], F32, rout + 9728)
        cnt = at("cnt", [P, 6, E], F32, rout + 9984)
        cnti = at("cnti", [P, 2, E], mybir.dt.int32, rout + 10240)
        ownf = at("ownf", [P, 2, NB], F32, rout + 10368)
        cmp_ = at("cmp_", [P, NB, E], F32, rout + 11264)

        s_rc, s_one = sem("routing_consts"), sem("ones_set")
        s_oh, s_cnt = sem("onehots_ready"), sem("counts_ready")
        s_slot, s_own = sem("slots_ready"), sem("owners_ready")
        s_rstep = sem("routing_step")
        s_wst, s_wsh, s_wsl = [sem(f"w_stage{i}_loaded") for i in range(4)], sem("w13_high"), sem("w13_low")
        s_w2 = sem("w2_loaded")
        s_x2r = [sem(f"x2_tiles{b}") for b in range(B)]
        s_sc = [sem(f"rows_sorted{b}") for b in range(B)]
        s_xb = [sem(f"block_rows{p}") for p in range(2)]
        s_xt, s_xh, s_xl = sem("blockT_ready"), sem("blockT_high"), sem("blockT_low")
        s_h1, s_h3, s_si, s_hd = sem("h1_ready"), sem("h3_ready"), sem("silu_ready"), sem("hidden_ready")
        s_ht, s_hc = sem("hiddenT_ready"), sem("hiddenT_copied")
        s_y, s_yc = sem("block_y_ready"), sem("block_y_copied")
        s_ys = [sem(f"block_y_saved{p}") for p in range(2)]
        s_got = [sem(f"outputs_gathered{i}") for i in range(8)]
        s_z0, s_z1, s_zv, s_zp, s_zn = sem("z_first"), sem("z_both"), sem("var3_ready"), sem("rstd3_ready"), sem("z_normed")
        s_out = [sem(f"out_saved{i}") for i in range(2)]
        ORDER = (2, 3, 0, 1)

        def over(n, k):
            return n > k if isinstance(n, int) else True

        def last(n):
            return isinstance(n, int) and n == NB - 1

        def over_blocks(eng, steps):
            for n in range(3):
                steps(n, n % 2, n // 2)
            with eng.Fori(0, (NB - 4) // 2) as m:
                steps(2 * m + 3, 1, m + 1)
                steps(2 * m + 4, 0, m + 2)
            steps(NB - 1, 1, NB // 2 - 1)

        with nc.Block() as block:
            @block.sync
            def _(sp):
                sp.dma_start(bef[:, :], before).then_inc(s_rc, 16)
                sp.dma_start(num[:, :], numbers).then_inc(s_rc, 16)
                for b in range(2):
                    sp.dma_start(x2r[:, b, :, :], scr_x2[b].rearrange("(t p) d -> p t d", p=P)).then_inc(s_x2r[b], 16)
                for n in range(2 * E):
                    e, src = n // 2, (w1, w3)[n % 2]
                    if n >= 4:
                        sp.wait_ge(s_wsl, n - 3)
                    sp.dma_start(w_stage[:, n % 4, :, :], src[e].rearrange("(c p) f -> p c f", p=P)).then_inc(s_wst[n % 4], 16)
                    if n in (7, 11):
                        b = 2 if n == 7 else 3
                        sp.wait_ge(s_sc[b - 2], NT * 32)
                        sp.dma_start(x2r[:, b % 2, :, :], scr_x2[b].rearrange("(t p) d -> p t d", p=P)).then_inc(s_x2r[b], 16)
                sp.wait_ge(s_own, 1)
                sp.dma_start(w2s[:, :, :, :], w2.rearrange("e (c p) d -> p e c d", p=P)).then_inc(s_w2, 16)
                for b in range(B):
                    sp.wait_ge(s_sc[b], NT * 32)

                def fetch(n, p):
                    if over(n, 1):
                        sp.wait_ge(s_xt, n - 1)
                    sp.dma_start(xb[:, p, :], xs[bass.ds(n * P, P)]).then_inc(s_xb[p], 16)

                def save(n, p):
                    sp.wait_ge(s_yc, n + 1)
                    sp.dma_start(ys[bass.ds(n * P, P)], yb[:, p, :]).then_inc(s_ys[p], 16)

                def block_steps(n, p, uses):
                    if not isinstance(n, int) or n + 2 < NB:
                        fetch(n + 2, p)
                    if over(n, 0):
                        save(n - 1, 1 - p)

                fetch(0, 0)
                fetch(1, 1)
                for n in range(3):
                    block_steps(n, n % 2, n // 2)
                with sp.Fori(0, (NB - 6) // 2) as m:
                    block_steps(2 * m + 3, 1, m + 1)
                    block_steps(2 * m + 4, 0, m + 2)
                for n in range(NB - 3, NB):
                    block_steps(n, n % 2, n // 2)
                save(NB - 1, 1)
                for q, b in enumerate(ORDER):
                    if b < 2:
                        sp.wait_ge(s_z0, (q - 1) * NT)
                        sp.dma_start(x2r[:, b % 2, :, :], scr_x2[b].rearrange("(t p) d -> p t d", p=P)).then_inc(s_x2r[b], 16)
                    if q >= 1:
                        sp.wait_ge(s_zn, q * NT)
                        sp.dma_start(out[ORDER[q - 1]].rearrange("(t p) d -> p t d", p=P), z[:, (q - 1) % 2, :, :]).then_inc(s_out[(q - 1) % 2], 16)
                sp.wait_ge(s_zn, B * NT)
                sp.dma_start(out[ORDER[3]].rearrange("(t p) d -> p t d", p=P), z[:, 1, :, :]).then_inc(s_out[1], 16)
                for s_ in s_out:
                    sp.wait_ge(s_, 32)

            @block.gpsimd
            def _(pool):
                for b in range(B):
                    pool.wait_ge(s_x2r[b], 16)
                    if b == 0:
                        pool.wait_ge(s_zero, B * 16)
                        pool.wait_ge(s_slot, 2)
                    for t in range(NT):
                        for k in range(2):
                            pool.indirect_dma_start(
                                out=xs[:, :], out_offset=bass.IndirectOffsetOnAxis(slots[:, k, b * NT + t:b * NT + t + 1], 0),
                                in_=x2r[:, b % 2, t, :], in_offset=None).then_inc(s_sc[b], 16)
                for p in range(2):
                    pool.wait_ge(s_ys[p], NB // 2 * 16)
                for q in range(B + 1):
                    if q < B:
                        for t in range(NT):
                            k, i = ORDER[q] * NT + t, q * NT + t
                            if i >= 8:
                                pool.wait_ge(s_z1, i - 7)
                            for j in range(2):
                                pool.indirect_dma_start(
                                    out=got[:, i % 8, j, :], out_offset=None, in_=ys[:, :],
                                    in_offset=bass.IndirectOffsetOnAxis(slots[:, j, k:k + 1], 0)).then_inc(s_got[i % 8], 16)
                    if q > 0:
                        pool.wait_ge(s_zv, q)
                        pool.tensor_tensor(zrs[:, (q - 1) % 2, :], zve[:, (q - 1) % 2, :], nhalf[:, :], ALU.pow).then_inc(s_zp, 1)

            @block.vector
            def _(dve):
                n_step = [0]

                def step(ins):
                    n_step[0] += 1
                    ins.then_inc(s_rstep, 1)
                    dve.wait_ge(s_rstep, n_step[0])

                dve.memset(one[:, :], 1.0).then_inc(s_one, 1)
                dve.wait_ge(s_rc, 32)
                dve.wait_ge(s_one, 1)
                for k in range(2):
                    step(dve.tensor_tensor(oh[:, k, :, :], picks[:, :, k:k + 1].to_broadcast([P, NTT, E]),
                                           num[:, 0:E].rearrange("p (o e) -> p o e", o=1).to_broadcast([P, NTT, E]), ALU.is_equal))
                dve.tensor_tensor(oh[:, 2, :, :], oh[:, 0, :, :], oh[:, 1, :, :], ALU.add).then_inc(s_oh, 1)
                dve.wait_ge(s_cnt, 1)
                step(dve.tensor_copy(tot[:, :, :], ps[:, 1, 0:NTT * E].rearrange("p (t e) -> p t e", e=E)))
                for e in range(E):
                    ins = dve.tensor_tensor_scan(run_[:, :, e], one[:, 0:NTT], tot[:, :, e], 0.0, ALU.mult, ALU.add)
                step(ins)
                step(dve.tensor_scalar(cnti[:, 0, :], run_[:, NTT - 1, :], float(P - 1), None, ALU.add))
                step(dve.tensor_scalar(cnti[:, 1, :], cnti[:, 0, :], 7, None, ALU.logical_shift_right))
                step(dve.tensor_copy(cnt[:, 0, :], cnti[:, 1, :]))
                step(dve.tensor_tensor_scan(cnt[:, 1, :], one[:, 0:E], cnt[:, 0, :], 0.0, ALU.mult, ALU.add))
                step(dve.tensor_tensor(cnt[:, 2, :], cnt[:, 1, :], cnt[:, 0, :], ALU.subtract))
                step(dve.tensor_scalar(cnt[:, 3, :], cnt[:, 2, :], float(P), None, ALU.mult))
                step(dve.tensor_tensor(pos[:, :, :], run_[:, :, :], tot[:, :, :], ALU.subtract))
                step(dve.tensor_tensor(pos[:, :, :], pos[:, :, :], ps[:, 0, 0:NTT * E].rearrange("p (t e) -> p t e", e=E), ALU.add))
                step(dve.tensor_tensor(pos[:, :, :], pos[:, :, :],
                                       cnt[:, 3, :].rearrange("p (o e) -> p o e", o=1).to_broadcast([P, NTT, E]), ALU.add))
                for k in range(2):
                    step(dve.tensor_tensor(sel[:, k, :, :], pos[:, :, :], oh[:, k, :, :], ALU.mult))
                    step(dve.tensor_reduce(slf[:, k, :], sel[:, k, :, :], AX.X, ALU.add))
                    dve.tensor_copy(slots[:, k, :], slf[:, k, :]).then_inc(s_slot, 1)
                step(dve.tensor_tensor(cmp_[:, :, :], num[:, :].rearrange("p (n o) -> p n o", o=1).to_broadcast([P, NB, E]),
                                       cnt[:, 1, :].rearrange("p (o e) -> p o e", o=1).to_broadcast([P, NB, E]), ALU.is_ge))
                step(dve.tensor_reduce(ownf[:, 0, :], cmp_[:, :, :], AX.X, ALU.add))
                dve.tensor_scalar(owner[:, :], ownf[:, 0, :], float(E - 1), None, ALU.min).then_inc(s_own, 1)
                for n in range(2 * E):
                    hi, lo = ((w1h, w1l), (w3h, w3l))[n % 2]
                    dve.wait_ge(s_wsh, n + 1)
                    dve.tensor_tensor(lo[:, n // 2, :, :], w_stage[:, n % 4, :, :], hi[:, n // 2, :, :].bitcast(F32),
                                      ALU.subtract).then_inc(s_wsl, 1)

                def low(n, p):
                    dve.wait_ge(s_xh, n + 1)
                    dve.tensor_tensor(xbl[:, p, :, :], ps[:, p, 0:D].rearrange("p (c n) -> p c n", c=2),
                                      xbh[:, p, :, :].bitcast(F32), ALU.subtract).then_inc(s_xl, 1)

                def gate(n, p):
                    dve.wait_ge(s_si, n + 1)
                    dve.wait_ge(s_h3, n + 1)
                    if over(n, 1):
                        dve.wait_ge(s_ht, n - 1)
                    dve.tensor_tensor(hid[:, p, :], ps[:, 4 + p, :], sil[:, p, :], ALU.mult).then_inc(s_hd, 1)

                def y_out(n, p, uses):
                    dve.wait_ge(s_y, n + 1)
                    if over(n, 1):
                        dve.wait_ge(s_ys[p], uses * 16)
                    dve.tensor_copy(yb[:, p, :], ps[:, 7, 0:D]).then_inc(s_yc, 1)

                def block_steps(n, p, uses):
                    if not last(n):
                        low(n + 1, 1 - p)
                    gate(n, p)
                    if over(n, 0):
                        y_out(n - 1, 1 - p, uses if p == 1 else uses - 1)

                low(0, 0)
                over_blocks(dve, block_steps)
                y_out(NB - 1, 1, NB // 2 - 1)
                for i in range(NTT):
                    b, t = ORDER[i // NT], i % NT
                    k = b * NT + t
                    dve.wait_ge(s_got[i % 8], 32 * (i // 8 + 1))
                    dve.wait_ge(s_x2r[b], 32 if b < 2 else 16)
                    if t == 0 and i >= 2 * NT:
                        dve.wait_ge(s_out[i // NT % 2], 16)
                    zt = z[:, i // NT % 2, t, :]
                    dve.scalar_tensor_tensor(zt, got[:, i % 8, 0, :], gates[:, k, 0:1], x2r[:, b % 2, t, :],
                                             ALU.mult, ALU.add).then_inc(s_z0, 1)
                    dve.wait_ge(s_z0, i + 1)
                    dve.scalar_tensor_tensor(zt, got[:, i % 8, 1, :], gates[:, k, 1:2], zt,
                                             ALU.mult, ALU.add).then_inc(s_z1, 1)
                    dve.wait_ge(s_z1, i + 1)
                    step(dve.bn_stats(zst[:, i // NT % 2, t, :], zt))
                    step(dve.bn_aggr(zmv[:, i // NT % 2, t, :], zst[:, i // NT % 2, t, :]))
                    if t == NT - 1:
                        q = i // NT
                        dve.tensor_scalar(zve[:, q % 2, :], zmv[:, q % 2, :, 1], EPS, None, ALU.add).then_inc(s_zv, 1)
                        dve.wait_ge(s_zp, q + 1)
                        for t in range(NT):
                            zt = z[:, q % 2, t, :]
                            dve.tensor_scalar(zt, zt, zmv[:, q % 2, t, 0:1], zrs[:, q % 2, t:t + 1],
                                              ALU.subtract, ALU.mult).then_inc(s_zn, 1)

            @block.scalar
            def _(act):
                for n in range(2 * E):
                    hi = (w1h, w3h)[n % 2]
                    act.wait_ge(s_wst[n % 4], (n // 4 + 1) * 16)
                    act.activation(hi[:, n // 2, :, :], w_stage[:, n % 4, :, :], ACT.Copy).then_inc(s_wsh, 1)
                act.wait_ge(s_wsl, 2 * E)

                def high(n, p):
                    act.wait_ge(s_xt, n + 1)
                    if over(n, 1):
                        act.wait_ge(s_h3, n - 1)
                    act.activation(xbh[:, p, :, :], ps[:, p, 0:D].rearrange("p (c n) -> p c n", c=2), ACT.Copy).then_inc(s_xh, 1)

                def block_steps(n, p, uses):
                    if not last(n):
                        high(n + 1, 1 - p)
                    act.wait_ge(s_h1, n + 1)
                    if over(n, 1):
                        act.wait_ge(s_hd, n - 1)
                    act.activation(sil[:, p, :], ps[:, 2 + p, :], ACT.Silu).then_inc(s_si, 1)
                    act.wait_ge(s_ht, n + 1)
                    if over(n, 1):
                        act.wait_ge(s_y, n - 1)
                    act.activation(hidT[:, p, :, :], ps[:, 6, :].rearrange("p (c n) -> p c n", c=F // P), ACT.Copy).then_inc(s_hc, 1)

                high(0, 0)
                over_blocks(act, block_steps)

            @block.tensor
            def _(pe):
                pe.wait_ge(s_oh, 1)
                pe.matmul(ps[:, 0, 0:NTT * E], bef[:, :], oh[:, 2, :, :].rearrange("p t e -> p (t e)"), start=True, stop=True)
                pe.matmul(ps[:, 1, 0:NTT * E], one[:, :], oh[:, 2, :, :].rearrange("p t e -> p (t e)"),
                          start=True, stop=True).then_inc(s_cnt, 1)
                pe.wait_ge(s_own, 1)
                pe.wait_ge(s_wsl, 2 * E)
                pe.wait_ge(s_w2, 16)

                def turn_rows(n, p, uses):
                    pe.wait_ge(s_xb[p], uses * 16)
                    for c in range(2):
                        ins = pe.transpose(ps[:, p, c * P:(c + 1) * P], xb[:, p, c * P:(c + 1) * P], idf[:, :])
                    ins.then_inc(s_xt, 1)

                def expert(n):
                    return pe.value_load(owner[0:1, n:n + 1] if isinstance(n, int) else owner[0:1, bass.ds(n, 1)],
                                         min_val=0, max_val=E - 1)

                def wide(w, e, c):
                    return w[:, bass.ds(e, 1), c, :].rearrange("p o f -> p (o f)")

                def y_block(n, p, e):
                    pe.wait_ge(s_hc, n + 1)
                    if over(n, 0):
                        pe.wait_ge(s_yc, n)
                    for c in range(F // P):
                        ins = pe.matmul(ps[:, 7, 0:D], hidT[:, p, c, :], wide(w2s, e, c), start=c == 0, stop=c == F // P - 1)
                    ins.then_inc(s_y, 1)

                def block_steps(n, p, uses):
                    e = expert(n)
                    if not last(n):
                        turn_rows(n + 1, 1 - p, uses + (1 if p == 1 else 0) + 1)
                    pe.wait_ge(s_xl, n + 1)
                    for bank, wh_, wl_, done in ((2, w1h, w1l, s_h1), (4, w3h, w3l, s_h3)):
                        terms = [(a, w, c) for c in range(2) for a, w in ((xbh, wh_), (xbl, wh_), (xbh, wl_))]
                        for k, (a, w, c) in enumerate(terms):
                            ins = pe.matmul(ps[:, bank + p, :], a[:, p, c, :], wide(w, e, c), start=k == 0, stop=k == len(terms) - 1)
                        ins.then_inc(done, 1)
                    if over(n, 0):
                        y_block(n - 1, 1 - p, expert(n - 1))
                    pe.wait_ge(s_hd, n + 1)
                    if over(n, 0):
                        pe.wait_ge(s_hc, n)
                    for c in range(F // P):
                        ins = pe.transpose(ps[:, 6, c * P:(c + 1) * P], hid[:, p, c * P:(c + 1) * P], idf[:, :])
                    ins.then_inc(s_ht, 1)

                turn_rows(0, 0, 1)
                over_blocks(pe, block_steps)
                y_block(NB - 1, 1, expert(NB - 1))


def rope_tables():
    inv = (np.float32(1.0) / np.power(np.float32(10000.0), np.arange(0, DR, 2, dtype=np.float32) / np.float32(DR))).astype(np.float32)
    ang = np.outer(np.arange(T, dtype=np.float32), inv).astype(np.float32)
    c, s = np.cos(ang).astype(np.float32).T, np.sin(ang).astype(np.float32).T
    return np.ascontiguousarray(np.concatenate([c, c, -s, s], 0))


def chunks(w):
    return np.concatenate([w[i:i + P] for i in range(0, w.shape[0], P)], 1)


def kernel(**inputs):
    import concourse.bacc as bacc
    from concourse.bass_utils import run_bass_kernel_spmd

    a = {k: np.asarray(v) for k, v in inputs.items()}
    pre = "L0_attn_W_"
    swap = np.r_[DR // 2:DR, 0:DR // 2]
    numbers = np.tile(np.arange(NB, dtype=np.float32), (P, 1))
    wq_r, wk_r = a[pre + "q_rope"], a[pre + "k_rope"]
    w_all = np.concatenate([
        chunks(a[pre + "kv_down"]), chunks(a[pre + "q"]), chunks(np.concatenate([wq_r, wq_r[:, swap]], 1)),
        a[pre + "k_up"], a[pre + "v_up"], wk_r, wk_r[:, swap], chunks(a[pre + "o"])], 1)
    tri = np.triu(np.ones((P, P), np.float32), 1) * np.float32(CAUSAL)
    arrays = {
        "x": a["x"], "ctxT": a["ctx_1024"].transpose(2, 0, 1).reshape(D, B * NS), "mask": a["mask_BxSxS2_bk1"],
        "w_all": w_all, "kwT": a["L0_xattn_k_w"].T, "qw": a["L0_xattn_q_w"], "vwT": a["L0_xattn_v_w"].T,
        "qb": a["L0_xattn_q_b"].reshape(2, P).T, "kb": a["L0_xattn_k_b"].reshape(2, P).T, "vb": a["L0_xattn_v_b"], "wrT": a["L0_ffn_Wr"].T,
        "ident": np.eye(P, dtype=np.float32), "causal_q": tri, "causal_k": tri.T,
        "before": np.triu(np.ones((P, P), np.float32), 1), "numbers": numbers,
        "w1": a["L0_ffn_w1"], "w3": a["L0_ffn_w3"], "w2": a["L0_ffn_w2"], "rope": rope_tables(),
    }
    arrays = {k: np.ascontiguousarray(v) for k, v in arrays.items()}
    nc = bacc.Bacc("TRN2", target_bir_lowering=False, num_devices=1)
    args = {k: nc.dram_tensor(k, v.shape, mybir.dt.from_np(v.dtype), kind="ExternalInput").ap() for k, v in arrays.items()}
    args["out"] = nc.dram_tensor("out", (B, T, D), F32, kind="ExternalOutput").ap()
    layer(nc, **args)
    r = run_bass_kernel_spmd(nc, [arrays], core_ids=[0])
    return r.results[0]["out"]
```

```python
from contextlib import ExitStack

import numpy as np

import concourse.bass as bass
from concourse import mybir

F32 = mybir.dt.float32
F32R = mybir.dt.float32r
BF16 = mybir.dt.bfloat16
U32 = mybir.dt.uint32
U8 = mybir.dt.uint8
ALU = mybir.AluOpType
ACT = mybir.ActivationFunctionType
AX = mybir.AxisListType

P = 128
B, T, D = 4, 1024, 256
NT = T // P
NH, HD, DR, DC = 16, 16, 32, 128
NS, NSP = 77, 96
E = 8
HG = 4
NG = NH // HG
F = 512
NB = 2 * B * T // P + E
CAP = B * T + P
ROWS = E * CAP + E * P
W_ROW = D + 2
KROWS = 2 * (HD + DR)
ATT_SCALE = 1.0 / float(np.sqrt(HD + DR))
X_SCALE = 1.0 / 16.0
EPS = 1e-5
MASKED = -1e9 / X_SCALE
CAUSAL = -1e30
WIDE = 256
HALF = T // 2

W_KV, W_Q, W_QR, W_KU, W_VU, W_KR, W_O = 0, 256, 768, 896, 1152, 1408, 1472
W_COLS = 1984

PROJ = ([("x", c, h) for h in range(2) for c in range(2)] + [("ckv", 0, h) for h in range(2)]
        + [("q", c, h) for c in range(2) for h in range(2)] + [("k", c, h) for c in range(2) for h in range(2)]
        + [("qr", 0, h) for h in range(2)] + [("kr", 0, h) for h in range(2)] + [("v", 0, j) for j in range(4)])
N_PROJ = len(PROJ)
N_SPLIT = 14
N_ROPE = 4 * 2

S1_UNITS = [(i, h) for i in range(NT) for h in range(HG)]
N_S1 = len(S1_UNITS) + 1
S2_STEPS = [(j, c) for j in range(NT) for c in range(2) if c == 1 or j < NT // 2]
N_S2 = len(S2_STEPS) * HG
N_PV = len(S2_STEPS)
S1_TIME = [int(t) for t in np.cumsum([0] + [(i + 1) * P + 64 for i, _ in S1_UNITS] + [P])]
S2_TIME = [int(t) for t in np.cumsum([0] + [(c + 1) * HALF - max(j * P, c * HALF) + 64 for j, c in S2_STEPS for _ in range(HG)])]
AHEAD = 4
FIRST, SPARE = 1, 12


class Steps:

    def __init__(self, eng, sem, base, per):
        self.eng, self.sem, self.base, self.per, self.n = eng, sem, base, per, 0

    def __call__(self, ins):
        ins.then_inc(self.sem, 1)
        self.n += 1
        self.eng.wait_ge(self.sem, self.base * self.per + self.n)


def layer(nc, x, ctxT, mask, w_all, kwT, qw, vwT, qb, kb, vb, wrT, w1, w3, w2, ident, causal_q, causal_k, before,
          numbers, filling, rope, out):
    ctx = ExitStack()
    with ctx:
        top = [16512]

        def at(name, shape, dt, offset=None):
            size = int(np.prod(shape[1:])) * mybir.dt.size(dt)
            if offset is None:
                offset = top[0]
                top[0] += (size + 63) // 64 * 64
            return nc.alloc_sbuf_tensor_at(name, shape, dt, offset=offset)

        def region(size):
            top[0] += size
            return top[0] - size

        def sem(name):
            return ctx.enter_context(nc.semaphore(name))

        idf = at("idf", [P, P], F32)
        cst_b = at("cst_b", [P, 3, P], BF16)

        idb, mask_q, mask_k = cst_b[:, 0, :], cst_b[:, 1, :], cst_b[:, 2, :]
        mark = at("mark", [P, 2], F32)
        nhalf = at("nhalf", [P, NT], F32)
        taken = at("taken", [P, E], F32)
        one = at("one", [P, P], F32)
        num = at("num", [P, NB], F32)
        kept = top[0]
        cs = at("cs", [2 * DR, T], F32)
        wh = at("wh", [P, W_COLS], F32R)
        wl = at("wl", [P, W_COLS], F32R)
        m_all = at("m_all", [P, 2, B, NSP], F32)
        brow = at("brow", [P, B, NSP], F32)
        vall = at("vall", [NSP, B, D], F32)
        wr = at("wr", [P, 2, NSP], F32)
        vaug = at("vaug", [P, NT, NH, HD + 1], F32)
        nmax = at("nmax", [P, HG * NT], F32)
        nmaxT = at("nmaxT", [HG * NT, P], F32R)
        xa = at("xa", [P, NT, D], F32)
        ckh = at("ckh", [P, T], F32R)
        ckl = at("ckl", [P, T], F32R)
        r2 = region(16384)
        oT = at("oT", [P, NG, T], F32, r2)
        r1 = region(32768)
        stg = at("stg", [P, 4, 2, HALF], F32R, r1)
        rs = at("rs", [DR, 4, T], F32R, r1 + 16384)
        pT = at("pT", [P, 3, HG, HALF], F32, r1)
        kas_at = region(32768)
        kas = at("kas", [KROWS + 1, 2, HG, T], F32R, kas_at)
        xTh = at("xTh", [P, 2, T], F32R, kas_at + 16384)
        xTl = at("xTl", [P, 2, T], F32R, kas_at + 24576)
        rt = at("rt", [DR, 3, HALF], F32, kas_at)
        qs_at = region(32768)
        qs = at("qs", [KROWS + 1, 2, HG, T], F32R, qs_at)
        kbs_at = region(16384)
        kbs = at("kbs", [KROWS, HG, T], F32R, kbs_at)
        att = at("att", [P, NT, D], F32, qs_at)
        xr = at("xr", [P, NT, D], F32, qs_at + 8192)
        x1T = at("x1T", [P, 2, NT, P], F32, qs_at + 16384)
        x1 = at("x1", [P, NT, D], F32, qs_at + 24576)
        x2T = at("x2T", [P, 2, NT, P], F32, qs_at)
        sc = at("sc", [P, NT, NS], F32, kbs_at)
        keep = at("keep", [P, NT, NS], F32, kbs_at + 2496)
        neg = at("neg", [P, NT, NS], F32, kbs_at + 2 * 2496)
        pxT = at("pxT", [NSP, NT, P], F32, kbs_at + 3 * 2496 + 640)
        after_kbs = top[0]
        px = at("px", [P, NT, NSP], F32)
        x2 = at("x2", [P, NT, W_ROW], F32)
        x2b = at("x2b", [P, NT, W_ROW], F32, qs_at + 16384)
        ids = at("ids", [P, NT], F32)
        mk = at("mk", [P, NT, NS], U8)
        picks = at("picks", [P, NT, 2], F32)
        bef = at("bef", [P, P], F32)
        oh = at("oh", [P, 3, NT, E], F32)
        run_ = at("run_", [P, NT, E], F32)
        pos = at("pos", [P, NT, E], F32)
        sel = at("sel", [P, 2, NT, E], F32)
        slf = at("slf", [P, 2, NT], F32)
        slots = at("slots", [P, 2, NT], U32)
        exp_at = at("exp_at", [P, E], F32)
        atth = at("atth", [P, 2, 2, P], F32R)
        attl = at("attl", [P, 2, 2, P], F32R)
        rden = at("rden", [P, 2, NH], F32)
        st = at("st", [P, 2, NT, 6], F32)
        mv = at("mv", [P, 2, NT, 2], F32)
        ve = at("ve", [P, 2, NT], F32)
        rstd = at("rstd", [P, 2, NT], F32)
        sx = at("sx", [P, 3, NT], F32)
        lg = at("lg", [P, 3, NT, E], F32)
        top8 = at("top8", [P, NT, E], F32)
        idx8 = at("idx8", [P, NT, E], U32)
        sl = at("sl", [P, 4, NT], F32)
        w_in = at("w_in", [P, W_COLS], F32, r1)
        cst_f = at("cst_f", [P, 2, P], F32, qs_at + 13376)
        cxT = at("cxT", [P, 2, B * NS], F32, qs_at)
        kw_s = at("kw_s", [P, 2, D], F32, qs_at + 2560)
        qw_s = at("qw_s", [P, 2, D], F32, qs_at + 4608)
        vw_s = at("vw_s", [P, 2, D], F32, qs_at + 6656)
        kxT = at("kxT", [P, 2, B * NS], F32, qs_at + 8704)
        bias_s = at("bias_s", [P, 4], F32, qs_at + 11264)
        qb_b = at("qb_b", [P, 2, P], F32, qs_at + 11328)
        vb_b = at("vb_b", [P, D], F32, qs_at + 12352)

        ps = ctx.enter_context(nc.psum_tensor("ps", [P, 8, 512], F32))

        scr_q = nc.dram_tensor("scr_q", [B, 2, D, T], F32)
        scr_k = nc.dram_tensor("scr_k", [B, 2, D, T], F32)
        sums = nc.dram_tensor("sums", [2 * B * T + 2 * E * P, D], F32)
        xs = nc.dram_tensor("xs", [ROWS, W_ROW], F32)

        s_sc = sem("rows_sorted")
        s_w, s_cx, s_c = sem("w_loaded"), sem("ctx_loaded"), sem("consts_loaded")
        s_wh, s_wl, s_init = sem("w_high_done"), sem("w_low_done"), sem("init_done")
        s_qbb, s_xk, s_xk_read = sem("qb_spread"), sem("xk_ready"), sem("xk_read")
        s_xm, s_xm_read = sem("xm_ready"), sem("xm_read")
        with nc.Block() as block:
            @block.sync
            def _(sp):
                sp.dma_start(w_in[:, :], w_all).then_inc(s_w, 16)
                sp.dma_start(idf[:, :], ident).then_inc(s_c, 16)
                sp.dma_start(cst_f[:, 0, :], causal_q).then_inc(s_c, 16)
                sp.dma_start(cst_f[:, 1, :], causal_k).then_inc(s_c, 16)
                sp.dma_start(cs[:, :], rope).then_inc(s_c, 16)
                sp.dma_start(bef[:, :], before).then_inc(s_c, 16)
                sp.dma_start(num[:, :], numbers[:, 0:NB]).then_inc(s_c, 16)
                sp.dma_start(exp_at[:, :], numbers[:, NB:NB + E]).then_inc(s_c, 16)
                sp.dma_start(ids[:, :], numbers[:, NB + E:]).then_inc(s_c, 16)
                sp.wait_ge(s_init, 1)
                sp.dma_start(wr[:, :, 0:E], wrT.rearrange("(c p) e -> p c e", p=P)).then_inc(s_c, 16)

            @block.scalar
            def _(act):
                act.dma_start(cxT[:, :, :], ctxT.rearrange("(c p) n -> p c n", p=P)).then_inc(s_cx, 16)
                act.dma_start(kw_s[:, :, :], kwT.rearrange("(c p) n -> p c n", p=P)).then_inc(s_cx, 16)
                act.dma_start(qw_s[:, :, :], qw.rearrange("(c p) n -> p c n", p=P)).then_inc(s_cx, 16)
                act.dma_start(vw_s[:, :, :], vwT.rearrange("(c p) n -> p c n", p=P)).then_inc(s_cx, 16)
                act.dma_start(bias_s[:, 0:2], qb).then_inc(s_cx, 16)
                act.dma_start(bias_s[:, 2:4], kb).then_inc(s_cx, 16)
                act.dma_start(vb_b[:, :], vb.rearrange("(o n) -> o n", o=1).to_broadcast([P, D])).then_inc(s_cx, 16)
                act.wait_ge(s_w, 16)
                act.activation(wh[:, :], w_in[:, :], ACT.Copy).then_inc(s_wh, 1)

            @block.gpsimd
            def _(pool):
                pool.dma_start(xs[E * CAP:ROWS], filling[E * P:]).then_inc(s_sc, 16)
                pool.memset(wr[:, :, :], 0.0).then_inc(s_init, 1)
                pool.memset(m_all[:, :, :, :], 0.0).then_inc(s_init, 1)
                pool.memset(vall[:, :, :], 0.0).then_inc(s_init, 1)
                pool.memset(vaug[:, :, :, HD:HD + 1], 1.0).then_inc(s_init, 1)
                pool.memset(px[:, :, :], 0.0).then_inc(s_init, 1)
                pool.memset(one[:, :], 1.0).then_inc(s_init, 1)
                pool.memset(taken[:, :], 0.0).then_inc(s_init, 1)
                pool.memset(nhalf[:, :], -0.5).then_inc(s_init, 1)
                pool.wait_ge(s_init, 8)
                pool.memset(kas[KROWS:KROWS + 1, :, :, :].bitcast(F32), 1.0).then_inc(s_init, 1)

            @block.vector
            def _(dve):
                dve.memset(ps[:, 6:8, :], 0.0).then_inc(s_wl, 1)
                dve.wait_ge(s_c, 144)
                dve.tensor_copy(cst_b[:, 0, :], idf[:, :]).then_inc(s_wl, 1)
                dve.tensor_copy(cst_b[:, 1:3, :], cst_f[:, :, :]).then_inc(s_wl, 1)
                dve.wait_ge(s_cx, 112)
                for c in range(2):
                    dve.tensor_copy(qb_b[:, c, :], bias_s[:, c:c + 1].to_broadcast([P, P])).then_inc(s_qbb, 1)
                dve.wait_ge(s_wh, 1)
                dve.tensor_tensor(wl[:, :], w_in[:, :], wh[:, :].bitcast(F32), ALU.subtract).then_inc(s_wl, 1)
                dve.wait_ge(s_init, 9)
                for c in range(2):
                    dve.wait_ge(s_xk, c + 1)
                    dve.tensor_scalar(kxT[:, c, :], ps[:, c, 0:B * NS], bias_s[:, 2 + c:3 + c], None,
                                      ALU.add).then_inc(s_xk_read, 1)
                for b in range(B):
                    dve.wait_ge(s_xk, 3 + b)
                    dve.tensor_tensor(vall[0:NS, b, :], ps[0:NS, 2 + b, 0:D], vb_b[0:NS, :],
                                      ALU.add).then_inc(s_xm_read, 1)
                for c in range(2):
                    dve.wait_ge(s_xm, c + 1)
                    dve.tensor_copy(m_all[:, c, :, 0:NS],
                                    ps[:, c, 0:B * NS].rearrange("p (b n) -> p b n", b=B)).then_inc(s_xm_read, 1)
                dve.wait_ge(s_xm, 3)
                dve.tensor_copy(brow[:, :, 0:NS],
                                ps[:, 2, 0:B * NS].rearrange("p (b n) -> p b n", b=B)).then_inc(s_xm_read, 1)

            @block.tensor
            def _(pe):
                pe.wait_ge(s_cx, 112)
                for c in range(2):
                    for m in range(2):
                        ins = pe.matmul(ps[:, c, 0:B * NS], kw_s[:, m, c * P:(c + 1) * P], cxT[:, m, :],
                                        start=m == 0, stop=m == 1)
                    ins.then_inc(s_xk, 1)
                for b in range(B):
                    for m in range(2):
                        ins = pe.matmul(ps[0:NS, 2 + b, 0:D], cxT[:, m, b * NS:(b + 1) * NS], vw_s[:, m, :],
                                        start=m == 0, stop=m == 1)
                    ins.then_inc(s_xk, 1)
                pe.wait_ge(s_xk_read, 2)
                for c in range(2):
                    for q in range(2):
                        ins = pe.matmul(ps[:, c, 0:B * NS], qw_s[:, q, c * P:(c + 1) * P], kxT[:, q, :],
                                        start=q == 0, stop=q == 1)
                    ins.then_inc(s_xm, 1)
                pe.wait_ge(s_qbb, 2)
                pe.wait_ge(s_xm_read, 1)
                for q in range(2):
                    ins = pe.matmul(ps[:, 2, 0:B * NS], qb_b[:, q, :], kxT[:, q, :], start=q == 0, stop=q == 1)
                ins.then_inc(s_xm, 1)

        s_x = sem("x_loaded")
        s_pr, s_ph, s_pl = sem("proj_ready"), sem("proj_high"), sem("proj_low")
        s_rr, s_rs, s_vc = sem("rope_psum_read"), sem("rope_done"), sem("v_copied")
        s_stg = [sem(f"stage{i}_saved") for i in range(4)]
        s_qk = [[sem(f"heads_set{p}_half{h}") for h in range(2)] for p in range(2)]
        s_kb = [sem(f"klow_half{h}") for h in range(2)]
        s_s1, s_s1r = sem("scores_for_max"), sem("max_taken")
        s_mx = sem("max_rows_placed")
        s_s2, s_exp, s_pv = sem("scores_ready"), sem("probs_ready"), sem("probs_used")
        s_oT = sem("heads_out_copied")
        s_xr, s_mk = sem("residual_loaded"), sem("mask_loaded")
        s_t1, s_t1r = sem("attn_turned"), sem("attn_normed")
        s_t2, s_t2h, s_t2l = sem("attnT_ready"), sem("attnT_high"), sem("attnT_low")
        s_t3, s_t3r = sem("y_ready"), sem("y_added")
        s_ve1, s_pow1, s_ln1 = sem("var1_ready"), sem("rstd1_ready"), sem("x1_ready")
        s_t4, s_t4r = sem("x1T_ready"), sem("x1T_copied")
        s_t5, s_t5r, s_sh = sem("xscores_ready"), sem("xscores_read"), sem("xscores_shifted")
        s_xe = sem("xprobs_ready")
        s_t6, s_t6r = sem("xprobsT_ready"), sem("xprobsT_copied")
        s_t7, s_t7r = sem("xy_ready"), sem("xy_added")
        s_ve2, s_pow2, s_ln2 = sem("var2_ready"), sem("rstd2_ready"), sem("x2_ready")
        s_t8, s_t8r = sem("x2T_ready"), sem("x2T_copied")
        s_t9, s_t9r, s_le, s_lex = sem("logits_ready"), sem("logits_read"), sem("logits_shifted"), sem("logits_exp")
        s_stat, s_agg = sem("stats_ready"), sem("mean_var_ready")
        s_x2b, s_meta, s_oh, s_cnt = sem("second_rows_copied"), sem("gates_placed"), sem("onehots_ready"), sem("counts_ready")
        s_left, s_held = sem("rows_left"), sem("wait_before_scatter_met")
        s_cr, s_slot = sem("counts_read"), sem("slots_ready")
        s_dve, s_rope, s_ones = sem("dve_step"), sem("rope_step"), sem("ones_row_placed")

        DVE_STEPS = 1 + NT + 5 + 9 + 4 + 1 + 1 + 4 + 1

        def s1_at(g, n):
            return g * N_S1 + n

        def s1_slot(g, n):
            pairs = [((k % 3 if k < N_S1 else k % 2) * 2) for k in range(s1_at(g, n) + 1)]
            used = [k for k, p in enumerate(pairs[:-1]) if p == pairs[-1]]
            return pairs[-1], used[-1] if used else None

        def s2_bank(g, n):
            return (4, 5, 2, 3)[n % 4] if g == NG - 1 else 4 + n % 2

        def proj_bank(u, first):
            return ps[:, u % 6 if first else 6 + u % 2, :]

        DEEP = 4
        assert r1 - kept >= 4 * 2 * E * 2 * F and kas_at == r1 + 32768 and qs_at == r1 + 65536
        w13h = at("w13h", [P, E, 2, 2, F], F32R, kept)
        w13l = at("w13l", [P, E, 2, 2, F], F32R, r1)
        w2s = at("w2s", [P, E, F // P, D], F32, qs_at)
        top[0] = kbs_at
        xb = at("xb", [P, DEEP, W_ROW], F32)
        cmp_ = at("cmp_", [P, 2, NB, E], F32, top[0])
        own = at("own", [P, 5, NB], F32, top[0] + 2 * NB * E * 4)
        sil = at("sil", [P, 2, F], F32)
        hid = at("hid", [P, 2, F], F32)
        cnt = at("cnt", [P, 3, E], F32)
        cnti = at("cnti", [P, 3, E], mybir.dt.int32)
        owner = at("owner", [P, NB], U32)
        first = at("first", [P, NB], U32)
        xbh = at("xbh", [P, 2, 2, P], F32R)
        assert top[0] <= after_kbs
        top[0] = after_kbs
        xbl = at("xbl", [P, 2, 2, P], F32R)
        hidT = at("hidT", [P, 2, F // P, P], F32)
        yb = at("yb", [P, DEEP, D], F32)
        xhf = at("xhf", [P, 2, D], F32)
        gb = at("gb", [P, DEEP, 1], F32)
        ib = at("ib", [P, DEEP, 1], U32)
        NQ, QT = 8, B * NT // 8
        z = at("z", [P, NQ, QT, D], F32, kept)
        z2 = at("z2", [P, NQ, QT, D], F32, kept + 35840)
        zbi = at("zbi", [P, NQ, QT], F32, kept + 34816)
        zst = at("zst", [P, NQ, QT, 6], F32, kept + 32768)
        zmv = at("zmv", [P, NQ, QT, 2], F32, kept + 33792)
        zve = at("zve", [P, NQ, QT], F32, kept + 34304)
        zrs = at("zrs", [P, NQ, QT], F32, kept + 34560)

        s_rstep = sem("block_list_step")
        s_took, s_own = sem("counts_whole"), sem("owners_ready")
        s_pad = sem("fillings_placed")
        s_wst, s_wsh, s_wsl = [sem(f"w13_loaded{n}") for n in range(2 * E)], sem("w13_high"), sem("w_expert_low")
        s_w2 = sem("w2_loaded")
        s_xb = [sem(f"block_rows{d}") for d in range(DEEP)]
        s_xt, s_xh, s_xl = sem("blockT_ready"), sem("blockT_high"), sem("blockT_low")
        s_h1, s_h3, s_si, s_hd = sem("h1_ready"), sem("h3_ready"), sem("silu_ready"), sem("hidden_ready")
        s_ht, s_hc, s_mt = sem("hiddenT_ready"), sem("hiddenT_copied"), sem("block_gates_kept")
        s_xhf = sem("half_x2_ready")
        s_y, s_yc = sem("block_y_ready"), sem("block_y_gated")
        s_ys = [sem(f"block_y_sent{d}") for d in range(DEEP)]
        s_z = [sem(f"sums_loaded{q}") for q in range(NQ)]
        s_z2 = [sem(f"second_sums_loaded{q}") for q in range(NQ)]
        s_za, s_zb = sem("sums_added"), sem("shift3_ready")
        s_zst, s_zag, s_zv, s_zp, s_zn = sem("stats3"), sem("mean_var3"), sem("var3_ready"), sem("rstd3_ready"), sem("out_normed")
        s_out = sem("out_saved")

        def over(n, k):
            return n > k if isinstance(n, int) else True

        def last(n):
            return isinstance(n, int) and n == NB - 1

        def over_blocks(eng, steps):
            for n in range(3):
                steps(n, n, 0)
            with eng.Fori(0, (NB - DEEP) // DEEP) as m:
                for k in range(3, 3 + DEEP):
                    steps(DEEP * m + k, k % DEEP, m + k // DEEP)
            steps(NB - 1, DEEP - 1, NB // DEEP - 1)

        def row0(eng, n):
            return eng.value_load(first[0:1, n:n + 1] if isinstance(n, int) else first[0:1, bass.ds(n, 1)],
                                  min_val=0, max_val=ROWS - P)

        with nc.Block() as block:
            @block.gpsimd
            def _(pool):
                pool.dma_start(xa[:, :, :], x[0].rearrange("(t p) d -> p t d", p=P)).then_inc(s_x, 16)
                pool.wait_ge(s_pr, 4)
                pool.dma_start(xa[:, :, :], x[1].rearrange("(t p) d -> p t d", p=P)).then_inc(s_x, 16)

                def batch(b, then):
                    pool.wait_ge(s_sc, b * 2 * NT * 16 + 16)
                    pool.tensor_tensor(mark[:, 0:1], nhalf[:, 0:1], nhalf[:, 0:1], ALU.mult).then_inc(s_left, 1)
                    pool.wait_ge(s_ve1, b + 1)
                    pool.tensor_tensor(rstd[:, 0, :], ve[:, 0, :], nhalf[:, :], ALU.pow).then_inc(s_pow1, 1)
                    if then:
                        pool.wait_ge(s_pr, (b + 1) * N_PROJ + 4)
                        pool.dma_start(xa[:, :, :], x[bass.ds((b + 2) % B, 1)].rearrange("o (t p) d -> p (o t) d", p=P)
                                       ).then_inc(s_x, 16)
                    pool.wait_ge(s_ve2, b + 1)
                    pool.tensor_tensor(rstd[:, 1, :], ve[:, 1, :], nhalf[:, :], ALU.pow).then_inc(s_pow2, 1)
                    pool.wait_ge(s_meta, b * 2 + 2)
                    pool.wait_ge(s_x2b, b + 1)
                    pool.wait_ge(s_slot, b * 2 + 2)
                    pool.tensor_tensor(mark[:, 1:2], nhalf[:, 0:1], nhalf[:, 0:1], ALU.mult).then_inc(s_held, 1)
                    for t in range(NT):
                        for k, rows in enumerate((x2, x2b)):
                            pool.indirect_dma_start(
                                out=xs[:, :], out_offset=bass.IndirectOffsetOnAxis(slots[:, k, t:t + 1], 0),
                                in_=rows[:, t, :], in_offset=None).then_inc(s_sc, 16)

                with pool.Fori(0, B - 1) as b:
                    batch(b, True)
                batch(B - 1, False)

                def send(n, d, uses):
                    pool.wait_ge(s_held, B + n)
                    pool.wait_ge(s_yc, n + 1)
                    pool.tensor_tensor(mark[:, 1:2], nhalf[:, 0:1], nhalf[:, 0:1], ALU.mult).then_inc(s_held, 1)
                    pool.indirect_dma_start(out=sums[:, :], out_offset=bass.IndirectOffsetOnAxis(ib[:, d, :], 0),
                                            in_=yb[:, d, :], in_offset=None).then_inc(s_ys[d], 16)

                over_blocks(pool, send)
                for q in range(NQ):
                    pool.wait_ge(s_zv, q + 1)
                    pool.tensor_tensor(zrs[:, q, :], zve[:, q, :], nhalf[:, 0:QT], ALU.pow).then_inc(s_zp, 1)

            @block.sync
            def _(sp):
                def load_heads(b, g, h):
                    p, cols = g % 2, slice(h * HALF, (h + 1) * HALF)
                    for scr, dst, parts in ((scr_q, qs, (0, 1)), (scr_k, kas, (0, 0))):
                        for r, part in enumerate(parts):
                            src = scr[bass.ds(b, 1), part, g * HG * HD:(g + 1) * HG * HD, cols]
                            sp.dma_start(dst[r * HD:(r + 1) * HD, p, :, cols].bitcast(F32),
                                         src.rearrange("o (h r) n -> r (o h) n", r=HD)).then_inc(s_qk[p][h], 16)

                def load_klow(b, g, h):
                    cols = slice(h * HALF, (h + 1) * HALF)
                    for r in range(2):
                        src = scr_k[bass.ds(b, 1), 1, g * HG * HD:(g + 1) * HG * HD, cols]
                        sp.dma_start(kbs[r * HD:(r + 1) * HD, :, cols].bitcast(F32),
                                     src.rearrange("o (h r) n -> r (o h) n", r=HD)).then_inc(s_kb[h], 16)

                def place_rope(dst, part, sem_):
                    for h in range(2):
                        cols = slice(h * HALF, (h + 1) * HALF)
                        for k in range(2):
                            src = rs[:, part + (k if part == 0 else 0), cols].bitcast(F32)
                            sp.dma_start(dst[DR + k * DR:2 * DR + k * DR, :, cols].bitcast(F32),
                                         src.rearrange("p (o n) -> p o n", o=1).to_broadcast([DR, HG, HALF])
                                         ).then_inc(sem_[h], 16)

                def save_parts(b):
                    for m in range(8):
                        name, c, h = PROJ[6 + m]
                        sp.wait_ge(s_pl, b * N_SPLIT + 7 + m)
                        dst = (scr_q if name == "q" else scr_k)[bass.ds(b, 1), :, c * P:(c + 1) * P, h * HALF:(h + 1) * HALF]
                        sp.dma_start(dst.rearrange("o s p n -> p (o s) n"), stg[:, m % 4, :, :].bitcast(F32)
                                     ).then_inc(s_stg[m % 4], 16)

                def first_set(b):
                    place_rope(qs[:, 0], 0, s_qk[0])
                    place_rope(kas[:, 0], 2, s_qk[0])
                    place_rope(kbs, 3, s_kb)
                    for s in s_stg:
                        sp.wait_ge(s, b * 32 + 32)
                    for h in range(2):
                        load_heads(b, 0, h)
                    for h in range(2):
                        load_klow(b, 0, h)

                def batch(b, then):
                    sp.wait_ge(s_left, b + 1)
                    for h in range(2):
                        load_heads(b, 1, h)
                    place_rope(qs[:, 1], 0, s_qk[1])
                    place_rope(kas[:, 1], 2, s_qk[1])
                    sp.dma_start(kas[KROWS:KROWS + 1, 1, :, :].bitcast(F32), one[0:HG * T // P, :]).then_inc(s_ones, 16)
                    for g in range(NG):
                        sp.wait_ge(s_s1r, b * NG * N_S1 + s1_at(g + 1, 0))
                        sp.dma_start(qs[KROWS:KROWS + 1, g % 2, :, :].bitcast(F32),
                                     nmaxT[:, :].bitcast(F32)).then_inc(s_mx, 16)
                        if g >= 1:
                            for h in range(2):
                                sp.wait_ge(s_s2, (b * NG + g - 1) * N_S2 + (8 * HG if h == 0 else N_S2))
                                load_klow(b, g, h)
                                if g + 1 < NG:
                                    load_heads(b, g + 1, h)
                            if g == NG - 1:
                                sp.dma_start(xr[:, :, :], x[bass.ds(b, 1)].rearrange("o (t p) d -> p (o t) d", p=P)).then_inc(s_xr, 16)
                                sp.dma_start(mk[:, :, :], mask[bass.ds(b, 1)].rearrange("o (t p) n -> p (o t) n", p=P)).then_inc(s_mk, 16)
                    if then:
                        save_parts(b + 1)
                        sp.wait_ge(s_t9, (b + 1) * 2)
                        first_set(b + 1)

                save_parts(0)
                sp.wait_ge(s_rs, 4)
                first_set(0)
                with sp.Fori(0, B - 1) as b:
                    batch(b, True)
                batch(B - 1, False)

                for e in range(E):
                    if e == 0:
                        sp.wait_ge(s_pv, B * NG * N_PV)
                    for k, w in enumerate((w1, w3)):
                        sp.dma_start(w13l[:, e, k, :, :].bitcast(F32), w[e].rearrange("(c p) f -> p c f", p=P)
                                     ).then_inc(s_wst[2 * e + k], 16)
                sp.wait_ge(s_took, 1)
                for e in range(E):
                    n_e = sp.value_load(cnti[0:1, 2, e:e + 1].bitcast(U32), min_val=0, max_val=B * T)
                    sp.dma_start(xs[bass.ds(n_e + e * CAP, P)], filling[e * P:(e + 1) * P]).then_inc(s_pad, 16)
                sp.wait_ge(s_own, 1)
                sp.wait_ge(s_pad, 16 * E)
                sp.wait_ge(s_sc, B * 2 * NT * 16 + 16)

                def fetch(n, d):
                    if over(n, 3):
                        sp.wait_ge(s_xt, n - 3)
                        sp.wait_ge(s_mt, n - 3)
                        sp.wait_ge(s_xhf, n - 3)
                    sp.wait_ge(s_own, 1)
                    sp.dma_start(xb[:, d, :], xs[bass.ds(row0(sp, n), P)]).then_inc(s_xb[d], 16)

                for n in range(DEEP):
                    fetch(n, n)
                for e in range(E):
                    sp.dma_start(w2s[:, e, :, :], w2[e].rearrange("(c p) d -> p c d", p=P)).then_inc(s_w2, 16)
                with sp.Fori(1, NB // DEEP) as m:
                    for d in range(DEEP):
                        fetch(DEEP * m + d, d)
                for d in range(DEEP):
                    sp.wait_ge(s_ys[d], NB // DEEP * 16)
                sp.wait_ge(s_y, NB)
                for q in range(NQ):
                    sp.dma_start(z[:, q, :, :], sums[q * QT * P:(q + 1) * QT * P].rearrange("(t p) d -> p t d", p=P)
                                 ).then_inc(s_z[q], 16)
                for q in range(NQ):
                    sp.wait_ge(s_zn, (q + 1) * QT)
                    t0 = q * QT
                    sp.dma_start(out[t0 // NT, t0 % NT * P:(t0 % NT + QT) * P].rearrange("(t p) d -> p t d", p=P),
                                 z[:, q, :, :]).then_inc(s_out, 16)
                sp.wait_ge(s_out, NQ * 16)

            @block.tensor
            def _(pe):
                def products(outp, terms, last=True, first=True):
                    for n, (a, w) in enumerate(terms):
                        ins = pe.matmul(outp, a, w, start=first and n == 0, stop=last and n == len(terms) - 1)
                    return ins

                def parts(ah, al, bh, bl):
                    return [(ah, bh), (al, bh), (ah, bl)]

                def wsl(o, n):
                    return wh[:, o:o + n], wl[:, o:o + n]

                def s1_unit(b, g, n):
                    slot, before_ = s1_slot(g, n)
                    if before_ is not None:
                        pe.wait_ge(s_s1r, b * NG * N_S1 + before_ + 1)
                    if n < N_S1 - 1:
                        i, h = S1_UNITS[n]
                        for bank in range((i * P) // HALF + 1):
                            k0, k1 = bank * HALF, min((bank + 1) * HALF, (i + 1) * P)
                            diag = k1 == (i + 1) * P
                            n_k = max(k1 - k0, WIDE)
                            ins = pe.matmul(ps[:, slot + bank, 0:n_k], qs[0:KROWS, g % 2, h, i * P:(i + 1) * P],
                                            kas[0:KROWS, g % 2, h, k0:k0 + n_k], start=True, stop=not diag)
                            if diag:
                                ins = pe.matmul(ps[:, slot + bank, i * P - k0:k1 - k0], idb, mask_q,
                                                start=False, stop=True)
                        ins.then_inc(s_s1, 1)
                    else:
                        pe.wait_ge(s_s1r, b * NG * N_S1 + s1_at(g, n))
                        pe.transpose(ps[0:HG * NT, slot, 0:P], nmax[:, :], idf[:, :]).then_inc(s_s1, 1)

                def s2_unit(b, g, u, h):
                    n = g * N_S2 + u * HG + h
                    j, c = S2_STEPS[u]
                    q0, q1 = max(j * P, c * HALF), (c + 1) * HALF
                    w0 = min(q0, q1 - WIDE)
                    o = ps[:, s2_bank(g, n), 0:q1 - w0]
                    k = u * HG + h
                    if g < NG - 1 or k < 2:
                        if n >= 2:
                            pe.wait_ge(s_exp, b * NG * N_S2 + n - 1)
                    elif k >= 4:
                        pe.wait_ge(s_exp, b * NG * N_S2 + n - 3)
                    diag = q0 == j * P
                    pe.matmul(o, kas[:, g % 2, h, j * P:(j + 1) * P], qs[:, g % 2, h, w0:q1], start=True, stop=False)
                    ins = pe.matmul(o, kbs[:, h, j * P:(j + 1) * P], qs[0:KROWS, g % 2, h, w0:q1],
                                    start=False, stop=not diag)
                    if diag:
                        ins = pe.matmul(o[:, q0 - w0:q0 - w0 + P], idb, mask_k, start=False, stop=True)
                    ins.then_inc(s_s2, 1)

                def pv_step(b, g, u):
                    j, c = S2_STEPS[u]
                    q0, q1 = max(j * P, c * HALF), (c + 1) * HALF
                    if u == 0 and g > 0:
                        pe.wait_ge(s_oT, b * NG + g)
                    pe.wait_ge(s_exp, (b * NG + g) * N_S2 + (u + 1) * HG)
                    last = S2_STEPS.index((3, 0)) if c == 0 else N_PV - 1
                    for h in range(HG):
                        ins = pe.matmul(ps[h * 32:h * 32 + HD + 1, 6 + c, q0 - c * HALF:HALF],
                                        vaug[:, j, g * HG + h, :], pT[:, u % 3, h, 0:q1 - q0],
                                        start=j == 0, stop=u == last, tile_position=(0, h * 32))
                    ins.then_inc(s_pv, 1)

                freed = {"v": (s_vc, 4), "qr": (s_rr, 4), "kr": (s_rr, 4)}

                def proj(b, u, first=False):
                    name, c, h = PROJ[u]
                    cols = slice(h * HALF, (h + 1) * HALF)
                    ring = 6 if first else 2
                    if u == 0:
                        pe.wait_ge(s_x, b * 16 + 16)
                    if u >= ring:
                        prev = PROJ[u - ring][0]
                        s, per = freed.get(prev, (s_pl, N_SPLIT))
                        k = sum(freed.get(p[0], (s_pl, 0))[0] is s for p in PROJ[:u - ring + 1])
                        pe.wait_ge(s, b * per + k)
                    o = proj_bank(u, first)
                    if name == "x":
                        for t in range(4):
                            ins = pe.transpose(o[:, t * P:(t + 1) * P], xa[:, h * 4 + t, c * P:(c + 1) * P], idf[:, :])
                    elif name == "ckv":
                        pe.wait_ge(s_pl, b * N_SPLIT + 2 * (h + 1))
                        terms = []
                        for m in range(2):
                            terms += parts(*wsl(W_KV + m * DC, DC), xTh[:, m, cols], xTl[:, m, cols])
                        ins = products(o, terms)
                    elif name == "q":
                        terms = []
                        for m in range(2):
                            terms += parts(*wsl(W_Q + m * D + c * P, P), xTh[:, m, cols], xTl[:, m, cols])
                        ins = products(o, terms)
                    elif name == "k":
                        pe.wait_ge(s_pl, b * N_SPLIT + 6)
                        ins = products(o, parts(*wsl(W_KU + c * P, P), ckh[:, cols], ckl[:, cols]))
                    elif name == "qr":
                        terms = []
                        for m in range(2):
                            terms += parts(*wsl(W_QR + m * 2 * DR, 2 * DR), xTh[:, m, cols], xTl[:, m, cols])
                        ins = products(o[0:2 * DR, :], terms)
                    elif name == "kr":
                        ins = products(o[0:2 * DR, :], parts(*wsl(W_KR, 2 * DR), ckh[:, cols], ckl[:, cols]))
                    else:
                        for t in range(2):
                            tok = slice((2 * h + t) * P, (2 * h + t + 1) * P)
                            vh, vl = wsl(W_VU, D)
                            ins = products(o[:, t * D:(t + 1) * D], [(ckh[:, tok], vh), (ckl[:, tok], vh), (ckh[:, tok], vl)])
                    ins.then_inc(s_pr, 1)

                def attention(b):
                    pe.wait_ge(s_vc, b * 4 + 4)
                    pe.wait_ge(s_rr, b * 4 + 4)

                    def heads_here(g, h):
                        p, k = g % 2, g // 2
                        pe.wait_ge(s_qk[p][h], b * 192 + (128 if k == 0 else 192))

                    def klow_here(g, h):
                        pe.wait_ge(s_kb[h], b * 160 + 64 + 32 * g)

                    def due(unit, k):
                        all_k = N_S2 - SPARE
                        return k >= FIRST and S1_TIME[unit] / S1_TIME[-1] <= S2_TIME[k] / S2_TIME[all_k]

                    heads_here(0, 0)
                    for n in range(N_S1):
                        if n == 16:
                            heads_here(0, 1)
                        s1_unit(b, 0, n)
                    for g in range(NG):
                        done = 0
                        if g == 0:
                            heads_here(1, 0)
                            for done in range(AHEAD):
                                s1_unit(b, 1, done)
                            done = AHEAD
                        pe.wait_ge(s_mx, (b * NG + g + 1) * 16)
                        if g == 1:
                            pe.wait_ge(s_ones, b * 16 + 16)
                        klow_here(g, 0)
                        for u in range(N_PV):
                            if u == 8:
                                klow_here(g, 1)
                            for h in range(HG):
                                s2_unit(b, g, u, h)
                                k = u * HG + h
                                while g + 1 < NG and done < N_S1 and due(done, k):
                                    if done == 0:
                                        heads_here(g + 1, 0)
                                    if done == 16:
                                        heads_here(g + 1, 1)
                                    s1_unit(b, g + 1, done)
                                    done += 1
                            if u >= 1:
                                pv_step(b, g, u - 1)
                        pv_step(b, g, N_PV - 1)
                        assert g + 1 == NG or done == N_S1

                def batch(b, then):
                    attention(b)

                    def nxt(*units):
                        if then:
                            for u in units:
                                proj(b + 1, u)

                    pe.wait_ge(s_oT, b * NG + NG)
                    for t in range(NT + 1):
                        if t < NT:
                            if t >= 2:
                                pe.wait_ge(s_t1r, b * NT + t - 1)
                            for g in range(NG):
                                ins = pe.transpose(ps[:, t % 2, g * P:(g + 1) * P], oT[:, g, t * P:(t + 1) * P], idf[:, :])
                            ins.then_inc(s_t1, 1)
                        if t >= 1:
                            u = t - 1
                            pe.wait_ge(s_t1r, b * NT + u + 1)
                            if u >= 2:
                                pe.wait_ge(s_t2l, b * NT + u - 1)
                            for c in range(2):
                                ins = pe.transpose(ps[:, 2 + u % 2, c * P:(c + 1) * P], att[:, u, c * P:(c + 1) * P], idf[:, :])
                            ins.then_inc(s_t2, 1)
                        nxt(t)
                        if t >= 1:
                            pe.wait_ge(s_t2l, b * NT + u + 1)
                            if u >= 2:
                                pe.wait_ge(s_t3r, b * NT + u - 1)
                            terms = []
                            for c in range(2):
                                vh, vl = wsl(W_O + c * D, D)
                                terms += [(atth[:, u % 2, c, :], vh), (attl[:, u % 2, c, :], vh), (atth[:, u % 2, c, :], vl)]
                            products(ps[:, 4 + u % 2, 0:D], terms).then_inc(s_t3, 1)

                    def turn(src, ready, done_sem, copied, units):
                        for t in range(NT):
                            pe.wait_ge(ready, b * NT + t + 1)
                            if t >= 2:
                                pe.wait_ge(copied, b * NT + t - 1)
                            for c in range(2):
                                ins = pe.transpose(ps[:, t % 2, c * P:(c + 1) * P], src[:, t, c * P:(c + 1) * P], idf[:, :])
                            ins.then_inc(done_sem, 1)
                            if t % 4 == 3:
                                nxt(*units[t // 4])

                    nxt(9, 10)
                    turn(x1, s_ln1, s_t4, s_t4r, ((11,), (12,)))
                    for hf in range(2):
                        pe.wait_ge(s_t4r, b * NT + 4 * hf + 4)
                        for t in range(4 * hf, 4 * hf + 4):
                            for c in range(2):
                                ins = pe.matmul(ps[:, 2 + hf, (t % 4) * NSP:(t % 4 + 1) * NSP], x1T[:, c, t, :],
                                                m_all[:, c, bass.ds(b, 1), :].rearrange("p o n -> p (o n)"),
                                                start=c == 0, stop=c == 1)
                        ins.then_inc(s_t5, 1)
                    nxt(13, 14)
                    pe.wait_ge(s_xe, b + 1)
                    for hf in range(2):
                        for t in range(4 * hf, 4 * hf + 4):
                            ins = pe.transpose(ps[0:NSP, 4 + hf, (t % 4) * P:(t % 4 + 1) * P], px[:, t, :], idf[:, :])
                        ins.then_inc(s_t6, 1)
                    nxt(15)
                    for t in range(NT):
                        pe.wait_ge(s_t6r, b * 2 + t // 4 + 1)
                        if t >= 2:
                            pe.wait_ge(s_t7r, b * NT + t - 1)
                        pe.matmul(ps[:, 2 + t % 2, 0:D], pxT[:, t, :],
                                  vall[:, bass.ds(b, 1), :].rearrange("p o n -> p (o n)"),
                                  start=True, stop=True).then_inc(s_t7, 1)
                        if t % 4 == 3:
                            nxt(16 + t // 4)
                    nxt(18, 19)
                    turn(x2, s_ln2, s_t8, s_t8r, ((20,), ()))
                    for hf in range(2):
                        pe.wait_ge(s_t8r, b * NT + 4 * hf + 4)
                        for t in range(4 * hf, 4 * hf + 4):
                            for c in range(2):
                                ins = pe.matmul(ps[:, 2 + hf, (t % 4) * NSP:(t % 4 + 1) * NSP], x2T[:, c, t, :], wr[:, c, :],
                                                start=c == 0, stop=c == 1)
                        ins.then_inc(s_t9, 1)
                    nxt(21)
                    pe.wait_ge(s_oh, b + 1)
                    picked = oh[:, 2, :, :].rearrange("p t e -> p (t e)")
                    pe.matmul(ps[:, 4, 0:NT * E], bef[:, :], picked, start=True, stop=True)
                    pe.matmul(ps[:, 5, 0:NT * E], one[:, :], picked, start=True, stop=True).then_inc(s_cnt, 1)
                    pe.wait_ge(s_cr, b * 2 + 2)

                for u in range(N_PROJ):
                    proj(0, u, True)
                with pe.Fori(0, B - 1) as b:
                    batch(b, True)
                batch(B - 1, False)

                pe.wait_ge(s_own, 1)

                def turn_rows(n, d, uses):
                    p = d % 2
                    pe.wait_ge(s_xb[d], (uses + 1) * 16)
                    for c in range(2):
                        ins = pe.transpose(ps[:, p, c * P:(c + 1) * P], xb[:, d, c * P:(c + 1) * P], idf[:, :])
                    ins.then_inc(s_xt, 1)

                def expert(n):
                    return pe.value_load(owner[0:1, n:n + 1] if isinstance(n, int) else owner[0:1, bass.ds(n, 1)],
                                         min_val=0, max_val=E - 1)

                def wide(w, e, *at_):
                    return w[(slice(None), bass.ds(e, 1)) + at_ + (slice(None),)].rearrange("p o f -> p (o f)")

                def y_block(n, p, e):
                    pe.wait_ge(s_hc, n + 1)
                    if over(n, 0):
                        pe.wait_ge(s_yc, n)
                    else:
                        pe.wait_ge(s_w2, E * 16)
                    for c in range(F // P):
                        ins = pe.matmul(ps[:, 7, 0:D], hidT[:, p, c, :], wide(w2s, e, c), start=c == 0, stop=c == F // P - 1)
                    ins.then_inc(s_y, 1)

                def block_steps(n, d, uses):
                    p = d % 2
                    e = expert(n)
                    if not last(n):
                        turn_rows(n + 1, (d + 1) % DEEP, uses + (d + 1) // DEEP)
                    pe.wait_ge(s_wsl, 2 * e + 2)
                    pe.wait_ge(s_xl, n + 1)
                    for bank, part, done in ((2, 0, s_h1), (4, 1, s_h3)):
                        terms = [(a, w, c) for c in range(2) for a, w in ((xbh, w13h), (xbl, w13h), (xbh, w13l))]
                        for k, (a, w, c) in enumerate(terms):
                            ins = pe.matmul(ps[:, bank + p, :], a[:, p, c, :], wide(w, e, part, c), start=k == 0, stop=k == len(terms) - 1)
                        ins.then_inc(done, 1)
                    if over(n, 0):
                        y_block(n - 1, 1 - p, expert(n - 1))
                    pe.wait_ge(s_hd, n + 1)
                    if over(n, 0):
                        pe.wait_ge(s_hc, n)
                    for c in range(F // P):
                        ins = pe.transpose(ps[:, 6, c * P:(c + 1) * P], hid[:, p, c * P:(c + 1) * P], idf[:, :])
                    ins.then_inc(s_ht, 1)

                turn_rows(0, 0, 0)
                over_blocks(pe, block_steps)
                y_block(NB - 1, 1, expert(NB - 1))

            @block.scalar
            def _(act):
                def proj(b, u, first=False):
                    name, c, h = PROJ[u]
                    cols = slice(h * HALF, (h + 1) * HALF)

                    def high(dst):
                        act.wait_ge(s_pr, b * N_PROJ + u + 1)
                        act.activation(dst, proj_bank(u, first), ACT.Copy).then_inc(s_ph, 1)

                    if name == "x":
                        high(xTh[:, c, cols])
                    elif name == "ckv":
                        high(ckh[:, cols])
                    elif name in "qk":
                        m = u - 6
                        if m >= 4:
                            act.wait_ge(s_stg[m % 4], b * 32 + 16)
                        high(stg[:, m % 4, 0, :])
                    elif name == "v":
                        act.wait_ge(s_pr, b * N_PROJ + u + 1)
                        act.activation(vaug[:, 2 * h:2 * h + 2, :, 0:HD],
                                       proj_bank(u, first).rearrange("p (t h d) -> p t h d", t=2, h=NH), ACT.Copy).then_inc(s_vc, 1)

                def batch(b, then):
                    def nxt(*units):
                        if then:
                            for u in units:
                                proj(b + 1, u)

                    for g in range(NG):
                        for u, (j, c) in enumerate(S2_STEPS):
                            q0, q1 = max(j * P, c * HALF), (c + 1) * HALF
                            w0 = min(q0, q1 - WIDE)
                            if g * N_PV + u >= 3:
                                act.wait_ge(s_pv, b * NG * N_PV + g * N_PV + u - 2)
                            for h in range(HG):
                                n = g * N_S2 + u * HG + h
                                act.wait_ge(s_s2, b * NG * N_S2 + n + 1)
                                act.activation(pT[:, u % 3, h, 0:q1 - q0], ps[:, s2_bank(g, n), q0 - w0:q1 - w0], ACT.Exp,
                                               scale=ATT_SCALE).then_inc(s_exp, 1)
                        act.wait_ge(s_pv, (b * NG + g + 1) * N_PV)
                        act.activation(oT[:, g, :], ps[:, 6:8, :].rearrange("p c n -> p (c n)"), ACT.Copy).then_inc(s_oT, 1)
                    nxt(0)
                    for t in range(NT):
                        act.wait_ge(s_t2, b * NT + t + 1)
                        if t >= 2:
                            act.wait_ge(s_t3, b * NT + t - 1)
                        act.activation(atth[:, t % 2, :, :], ps[:, 2 + t % 2, 0:D].rearrange("p (c n) -> p c n", c=2),
                                       ACT.Copy).then_inc(s_t2h, 1)
                        nxt(t + 1)
                    nxt(9, 10)

                    def copies(ready, dst, done_sem, units):
                        for t in range(NT):
                            act.wait_ge(ready, b * NT + t + 1)
                            act.activation(dst[:, :, t, :], ps[:, t % 2, 0:D].rearrange("p (c n) -> p c n", c=2),
                                           ACT.Copy).then_inc(done_sem, 1)
                            if t % 4 == 3:
                                nxt(*units[t // 4])

                    copies(s_t4, x1T, s_t4r, ((11,), (12,)))
                    nxt(13)
                    act.wait_ge(s_sh, b + 1)
                    act.activation(px[:, :, 0:NS], sc[:, :, :], ACT.Exp, scale=X_SCALE).then_inc(s_xe, 1)
                    for hf in range(2):
                        act.wait_ge(s_t6, b * 2 + hf + 1)
                        act.activation(pxT[:, 4 * hf:4 * hf + 4, :],
                                       ps[0:NSP, 4 + hf, :].rearrange("p (t n) -> p t n", t=4), ACT.Copy).then_inc(s_t6r, 1)
                    nxt(15, 16, 17, 18, 19)
                    copies(s_t8, x2T, s_t8r, ((20,), ()))
                    nxt(21)
                    act.wait_ge(s_le, b + 1)
                    act.activation(lg[:, 1, :, :], lg[:, 0, :, :], ACT.Exp).then_inc(s_lex, 1)
                    act.wait_ge(s_t8, (b + 1) * NT)
                    act.activation(x2b[:, :, 0:D], x2[:, :, 0:D], ACT.Copy).then_inc(s_x2b, 1)

                for u in range(N_PROJ):
                    proj(0, u, True)
                with act.Fori(0, B - 1) as b:
                    batch(b, True)
                batch(B - 1, False)

                act.wait_ge(s_x, (B + 1) * 16)
                for n in range(2 * E):
                    act.wait_ge(s_wst[n], 16)
                    act.activation(w13h[:, n // 2, n % 2, :, :], w13l[:, n // 2, n % 2, :, :].bitcast(F32),
                                   ACT.Copy).then_inc(s_wsh, 1)

                def high(n, p):
                    act.wait_ge(s_xt, n + 1)
                    if over(n, 1):
                        act.wait_ge(s_h3, n - 1)
                    act.activation(xbh[:, p, :, :], ps[:, p, 0:D].rearrange("p (c n) -> p c n", c=2), ACT.Copy).then_inc(s_xh, 1)

                def block_steps(n, d, uses):
                    p = d % 2
                    if not last(n):
                        high(n + 1, 1 - p)
                    act.wait_ge(s_h1, n + 1)
                    if over(n, 1):
                        act.wait_ge(s_hd, n - 1)
                    act.activation(sil[:, p, :], ps[:, 2 + p, :], ACT.Silu).then_inc(s_si, 1)
                    if over(n, 1):
                        act.wait_ge(s_yc, n - 1)
                    act.activation(xhf[:, p, :], xb[:, d, 0:D], ACT.Copy, scale=0.5).then_inc(s_xhf, 1)
                    act.wait_ge(s_ht, n + 1)
                    if over(n, 1):
                        act.wait_ge(s_y, n - 1)
                    act.activation(hidT[:, p, :, :], ps[:, 6, :].rearrange("p (c n) -> p c n", c=F // P), ACT.Copy).then_inc(s_hc, 1)

                high(0, 0)
                over_blocks(act, block_steps)
                for d in range(DEEP):
                    act.wait_ge(s_ys[d], NB // DEEP * 16)
                act.wait_ge(s_y, NB)
                for q in range(NQ):
                    act.dma_start(z2[:, q, :, :], sums[B * T + q * QT * P:B * T + (q + 1) * QT * P].rearrange(
                        "(t p) d -> p t d", p=P)).then_inc(s_z2[q], 16)
                for q in range(NQ):
                    act.wait_ge(s_zb, q + 1)
                    for t in range(QT):
                        act.activation(z[:, q, t, :], z[:, q, t, :], ACT.Identity, bias=zbi[:, q, t:t + 1],
                                       scale=zrs[:, q, t:t + 1]).then_inc(s_zn, 1)

            @block.vector
            def _(dve):
                def proj(b, u, first=False):
                    name, c, h = PROJ[u]
                    cols = slice(h * HALF, (h + 1) * HALF)
                    o = proj_bank(u, first)

                    def low(dst, high_):
                        dve.wait_ge(s_ph, b * N_SPLIT + u + 1)
                        dve.tensor_tensor(dst, o, high_.bitcast(F32), ALU.subtract).then_inc(s_pl, 1)

                    if name == "x":
                        low(xTl[:, c, cols], xTh[:, c, cols])
                    elif name == "ckv":
                        low(ckl[:, cols], ckh[:, cols])
                    elif name in "qk":
                        m = u - 6
                        low(stg[:, m % 4, 1, :], stg[:, m % 4, 0, :])
                    elif name in ("qr", "kr"):
                        part = 0 if name == "qr" else 2
                        step = Steps(dve, s_rope, b, N_ROPE)
                        step.n = (part + h) * 2
                        dve.wait_ge(s_pr, b * N_PROJ + u + 1)
                        dve.tensor_tensor(rt[:, 0, :], o[0:DR, :], cs[0:DR, cols], ALU.mult)
                        ins = dve.tensor_tensor(rt[:, 1, :], o[DR:2 * DR, :], cs[DR:2 * DR, cols], ALU.mult)
                        ins.then_inc(s_rr, 1)
                        dve.wait_ge(s_rr, b * 4 + (part + h + 1))
                        step(dve.tensor_tensor(rt[:, 2, :], rt[:, 0, :], rt[:, 1, :], ALU.add))
                        step(dve.tensor_copy(rs[:, part, cols], rt[:, 2, :]))
                        dve.tensor_tensor(rs[:, part + 1, cols], rt[:, 2, :], rs[:, part, cols].bitcast(F32),
                                          ALU.subtract).then_inc(s_rs, 1)
                        dve.wait_ge(s_rs, b * 4 + (part + h + 1))

                def batch(b, then):
                    step = Steps(dve, s_dve, b, DVE_STEPS)

                    def nxt(*units):
                        if then:
                            for u in units:
                                proj(b + 1, u)

                    for g in range(NG):
                        for n in range(N_S1):
                            slot, _ = s1_slot(g, n)
                            dve.wait_ge(s_s1, b * NG * N_S1 + s1_at(g, n) + 1)
                            if n < N_S1 - 1:
                                i, h = S1_UNITS[n]
                                k = h * NT + i
                                dve.tensor_reduce(nmax[:, k:k + 1],
                                                  ps[:, slot:slot + 2, :].rearrange("p s n -> p (s n)")[:, 0:(i + 1) * P],
                                                  AX.X, ALU.max, negate=True).then_inc(s_s1r, 1)
                            else:
                                if g > 0:
                                    dve.wait_ge(s_mx, (b * NG + g) * 16)
                                dve.tensor_copy(nmaxT[:, :], ps[0:HG * NT, slot, 0:P]).then_inc(s_s1r, 1)
                    dve.wait_ge(s_xr, b * 16 + 16)
                    dve.wait_ge(s_mk, b * 16 + 16)
                    dve.wait_ge(s_s2, (b + 1) * NG * N_S2)
                    dve.tensor_scalar(keep[:, :, :], mk[:, :, :], -1.0, 1.0, ALU.mult, ALU.add)
                    step(dve.tensor_scalar(neg[:, :, :], mk[:, :, :], MASKED, None, ALU.mult))

                    def stats(k, t, src):
                        if t > 0:
                            dve.wait_ge(s_stat, b * 2 * NT + k * NT + t)
                        dve.bn_stats(st[:, k, t, :], src).then_inc(s_stat, 1)
                        if t > 0:
                            dve.bn_aggr(mv[:, k, t - 1, :], st[:, k, t - 1, :]).then_inc(s_agg, 1)

                    for t in range(NT + 1):
                        if t < NT:
                            dve.wait_ge(s_t1, b * NT + t + 1)
                            po = ps[:, t % 2, :].rearrange("p (h d) -> p h d", h=NH)
                            step(dve.reciprocal(rden[:, t % 2, :], po[:, :, HD]))
                            dve.tensor_tensor(att[:, t, :].rearrange("p (h d) -> p h d", h=NH), po[:, :, 0:HD],
                                              rden[:, t % 2, :].rearrange("p (h o) -> p h o", o=1).to_broadcast([P, NH, HD]),
                                              ALU.mult).then_inc(s_t1r, 1)
                        if t >= 1:
                            u = t - 1
                            dve.wait_ge(s_t2h, b * NT + u + 1)
                            dve.tensor_tensor(attl[:, u % 2, :, :], ps[:, 2 + u % 2, 0:D].rearrange("p (c n) -> p c n", c=2),
                                              atth[:, u % 2, :, :].bitcast(F32), ALU.subtract).then_inc(s_t2l, 1)
                        nxt(t)
                        if t >= 1:
                            dve.wait_ge(s_t3, b * NT + u + 1)
                            dve.tensor_tensor(x1[:, u, :], ps[:, 4 + u % 2, 0:D], xr[:, u, :], ALU.add).then_inc(s_t3r, 1)
                            dve.wait_ge(s_t3r, b * NT + u + 1)
                            stats(0, u, x1[:, u, :])

                    def norm(k, buf, s_ve, s_pow, s_ln, *units):
                        def add_eps(t0, t1, n):
                            dve.wait_ge(s_agg, b * 2 * NT + k * NT + n)
                            return dve.tensor_scalar(ve[:, k, t0:t1], mv[:, k, t0:t1, 1], EPS, None, ALU.add)

                        dve.wait_ge(s_stat, b * 2 * NT + (k + 1) * NT)
                        add_eps(0, NT - 1, NT - 1)
                        dve.bn_aggr(mv[:, k, NT - 1, :], st[:, k, NT - 1, :]).then_inc(s_agg, 1)
                        add_eps(NT - 1, NT, NT).then_inc(s_ve, 1)
                        nxt(*units)
                        dve.wait_ge(s_pow, b + 1)
                        for t in range(NT):
                            dve.tensor_scalar(buf[:, t, 0:D], buf[:, t, 0:D], mv[:, k, t, 0:1], rstd[:, k, t:t + 1],
                                              ALU.subtract, ALU.mult).then_inc(s_ln, 1)

                    norm(0, x1, s_ve1, s_pow1, s_ln1, 9)
                    nxt(10, 11, 12)
                    for hf in range(2):
                        dve.wait_ge(s_t5, b * 2 + hf + 1)
                        ins = dve.tensor_tensor(
                            sc[:, 4 * hf:4 * hf + 4, :],
                            ps[:, 2 + hf, 0:4 * NSP].rearrange("p (t n) -> p t n", t=4)[:, :, 0:NS],
                            brow[:, bass.ds(b, 1), 0:NS].to_broadcast([P, 4, NS]), ALU.add)
                    ins.then_inc(s_t5r, 1)
                    dve.wait_ge(s_t5r, b + 1)
                    step(dve.tensor_tensor(sc[:, :, :], sc[:, :, :], keep[:, :, :], ALU.mult))
                    step(dve.tensor_tensor(sc[:, :, :], sc[:, :, :], neg[:, :, :], ALU.add))
                    step(dve.tensor_reduce(sx[:, 0, :], sc[:, :, :], AX.X, ALU.max))
                    dve.tensor_tensor(sc[:, :, :], sc[:, :, :],
                                      sx[:, 0, :].rearrange("p (t o) -> p t o", o=1).to_broadcast([P, NT, NS]),
                                      ALU.subtract).then_inc(s_sh, 1)
                    nxt(13)
                    dve.wait_ge(s_xe, b + 1)
                    step(dve.tensor_reduce(sx[:, 1, :], px[:, :, 0:NS], AX.X, ALU.add))
                    step(dve.reciprocal(sx[:, 2, :], sx[:, 1, :]))
                    nxt(14, 15)
                    for t in range(NT):
                        dve.wait_ge(s_t7, b * NT + t + 1)
                        dve.scalar_tensor_tensor(x2[:, t, 0:D], ps[:, 2 + t % 2, 0:D], sx[:, 2, t:t + 1], x1[:, t, :],
                                                 ALU.mult, ALU.add).then_inc(s_t7r, 1)
                        dve.wait_ge(s_t7r, b * NT + t + 1)
                        stats(1, t, x2[:, t, 0:D])
                        if t == 3:
                            nxt(16)
                    norm(1, x2, s_ve2, s_pow2, s_ln2, 17)
                    nxt(18, 19, 20)
                    for hf in range(2):
                        dve.wait_ge(s_t9, b * 2 + hf + 1)
                        ins = dve.tensor_copy(lg[:, 0, 4 * hf:4 * hf + 4, :],
                                              ps[:, 2 + hf, 0:4 * NSP].rearrange("p (t n) -> p t n", t=4)[:, :, 0:E])
                        ins.then_inc(s_t9r, 1)
                    dve.wait_ge(s_t9r, b * 2 + 2)
                    step(dve.tensor_reduce(sl[:, 0, :], lg[:, 0, :, :], AX.X, ALU.max))
                    dve.tensor_tensor(lg[:, 0, :, :], lg[:, 0, :, :],
                                      sl[:, 0, :].rearrange("p (t o) -> p t o", o=1).to_broadcast([P, NT, E]),
                                      ALU.subtract).then_inc(s_le, 1)
                    dve.wait_ge(s_lex, b + 1)
                    step(dve.tensor_reduce(sl[:, 1, :], lg[:, 1, :, :], AX.X, ALU.add))
                    step(dve.reciprocal(sl[:, 2, :], sl[:, 1, :]))
                    nxt(21)
                    halves = [slice(0, NT // 2), slice(NT // 2, NT)]

                    def spread(buf, j):
                        return sl[:, j, :].rearrange("p (t o) -> p t o", o=1)[:, buf, :]

                    def probs(hf):
                        return dve.tensor_tensor(lg[:, 2, hf, :], lg[:, 1, hf, :], spread(hf, 2).to_broadcast([P, NT // 2, E]), ALU.mult)

                    def find(call, hf):
                        for t in range(hf.start, hf.stop):
                            ins = call(t)
                        return ins

                    def best(t):
                        return dve.max(top8[:, t, :], lg[:, 2, t, :])

                    def where(t):
                        return dve.max_index(idx8[:, t, :], top8[:, t, :], lg[:, 2, t, :])

                    def both(hf):
                        return dve.tensor_tensor(sl[:, 3, hf], top8[:, hf, 0], top8[:, hf, 1], ALU.add)

                    step(probs(halves[0]))
                    probs(halves[1]).then_inc(s_dve, 1)
                    find(best, halves[0]).then_inc(s_dve, 1)
                    step.n += 2
                    dve.wait_ge(s_dve, b * DVE_STEPS + step.n)
                    both(halves[0])
                    step(find(best, halves[1]))
                    both(halves[1])
                    find(where, halves[0])
                    step(find(where, halves[1]))
                    step(dve.reciprocal(sl[:, 0, :], sl[:, 3, :]))
                    g_of = sl[:, 0, :].rearrange("p (t o) -> p t o", o=1)
                    dve.wait_ge(s_t8, (b + 1) * NT)
                    for k, rows in enumerate((x2, x2b)):
                        dve.tensor_tensor(rows[:, :, D:D + 1], top8[:, :, k:k + 1], g_of, ALU.mult)
                        dve.tensor_scalar(rows[:, :, D + 1], ids[:, :], float(k * B * T), None, ALU.add).then_inc(s_meta, 1)
                    step(dve.tensor_copy(picks[:, :, :], idx8[:, :, 0:2]))
                    for k in range(2):
                        step(dve.tensor_tensor(oh[:, k, :, :], picks[:, :, k:k + 1].to_broadcast([P, NT, E]),
                                               num[:, 0:E].rearrange("p (o e) -> p o e", o=1).to_broadcast([P, NT, E]), ALU.is_equal))
                    dve.tensor_tensor(oh[:, 2, :, :], oh[:, 0, :, :], oh[:, 1, :, :], ALU.add).then_inc(s_oh, 1)
                    step(dve.tensor_scalar(ids[:, :], ids[:, :], float(T), None, ALU.add))
                    dve.wait_ge(s_cnt, b + 1)
                    tot = ps[:, 5, 0:NT * E].rearrange("p (t e) -> p t e", e=E)
                    for e in range(E):
                        ins = dve.tensor_tensor_scan(run_[:, :, e], one[:, 0:NT], tot[:, :, e], taken[:, e:e + 1], ALU.mult, ALU.add)
                    step(ins)
                    dve.tensor_tensor(pos[:, :, :], run_[:, :, :], tot, ALU.subtract).then_inc(s_cr, 1)
                    dve.wait_ge(s_cr, b * 2 + 1)
                    dve.tensor_tensor(pos[:, :, :], pos[:, :, :], ps[:, 4, 0:NT * E].rearrange("p (t e) -> p t e", e=E),
                                      ALU.add).then_inc(s_cr, 1)
                    dve.wait_ge(s_cr, b * 2 + 2)
                    step(dve.tensor_tensor(pos[:, :, :], pos[:, :, :],
                                           exp_at[:, :].rearrange("p (o e) -> p o e", o=1).to_broadcast([P, NT, E]), ALU.add))
                    for k in range(2):
                        step(dve.tensor_tensor(sel[:, k, :, :], pos[:, :, :], oh[:, k, :, :], ALU.mult))
                        step(dve.tensor_reduce(slf[:, k, :], sel[:, k, :, :], AX.X, ALU.add))
                        dve.tensor_copy(slots[:, k, :], slf[:, k, :]).then_inc(s_slot, 1)
                    step(dve.tensor_copy(taken[:, :], run_[:, NT - 1, :]))
                    assert step.n == DVE_STEPS, (step.n, DVE_STEPS)

                for u in range(N_PROJ):
                    proj(0, u, True)
                with dve.Fori(0, B - 1) as b:
                    batch(b, True)
                batch(B - 1, False)

                n_step = [0]

                def step(ins):
                    n_step[0] += 1
                    ins.then_inc(s_rstep, 1)
                    dve.wait_ge(s_rstep, n_step[0])

                dve.tensor_copy(cnti[:, 2, :], taken[:, :]).then_inc(s_took, 1)
                step(dve.tensor_scalar(cnti[:, 0, :], taken[:, :], float(P - 1), None, ALU.add))
                step(dve.tensor_scalar(cnti[:, 1, :], cnti[:, 0, :], 7, None, ALU.logical_shift_right))
                step(dve.tensor_copy(cnt[:, 0, :], cnti[:, 1, :]))
                step(dve.tensor_tensor_scan(cnt[:, 1, :], one[:, 0:E], cnt[:, 0, :], 0.0, ALU.mult, ALU.add))
                step(dve.tensor_tensor(cmp_[:, 0, :, :], num[:, :].rearrange("p (n o) -> p n o", o=1).to_broadcast([P, NB, E]),
                                       cnt[:, 1, :].rearrange("p (o e) -> p o e", o=1).to_broadcast([P, NB, E]), ALU.is_ge))
                step(dve.tensor_tensor(cmp_[:, 1, :, :], cmp_[:, 0, :, :],
                                       cnt[:, 0, :].rearrange("p (o e) -> p o e", o=1).to_broadcast([P, NB, E]), ALU.mult))
                step(dve.tensor_reduce(own[:, 0:2, :], cmp_[:, :, :, :], AX.X, ALU.add))
                step(dve.tensor_tensor(own[:, 2, :], num[:, :], own[:, 1, :], ALU.subtract))
                step(dve.tensor_scalar(own[:, 3, :], own[:, 2, :], float(P), None, ALU.mult))
                step(dve.tensor_scalar(own[:, 4, :], own[:, 0, :], float(CAP), None, ALU.mult))
                step(dve.tensor_tensor(first[:, :], own[:, 3, :], own[:, 4, :], ALU.add))
                dve.tensor_scalar(owner[:, :], own[:, 0, :], float(E - 1), None, ALU.min).then_inc(s_own, 1)
                for n in range(2 * E):
                    e, k = n // 2, n % 2
                    dve.wait_ge(s_wsh, n + 1)
                    dve.tensor_tensor(w13l[:, e, k, :, :], w13l[:, e, k, :, :].bitcast(F32), w13h[:, e, k, :, :].bitcast(F32),
                                      ALU.subtract).then_inc(s_wsl, 1)

                def low(n, p):
                    dve.wait_ge(s_xh, n + 1)
                    dve.tensor_tensor(xbl[:, p, :, :], ps[:, p, 0:D].rearrange("p (c n) -> p c n", c=2),
                                      xbh[:, p, :, :].bitcast(F32), ALU.subtract).then_inc(s_xl, 1)

                def gate(n, d, uses):
                    p = d % 2
                    dve.wait_ge(s_si, n + 1)
                    dve.wait_ge(s_h3, n + 1)
                    if over(n, 1):
                        dve.wait_ge(s_ht, n - 1)
                    dve.tensor_tensor(hid[:, p, :], ps[:, 4 + p, :], sil[:, p, :], ALU.mult).then_inc(s_hd, 1)
                    if over(n, 3):
                        dve.wait_ge(s_ys[d], uses * 16)
                    dve.tensor_copy(gb[:, d, :], xb[:, d, D:D + 1])
                    dve.tensor_copy(ib[:, d, :], xb[:, d, D + 1:D + 2]).then_inc(s_mt, 1)

                def y_out(n, d):
                    dve.wait_ge(s_y, n + 1)
                    dve.wait_ge(s_mt, n + 1)
                    dve.wait_ge(s_xhf, n + 1)
                    dve.scalar_tensor_tensor(yb[:, d, :], ps[:, 7, 0:D], gb[:, d, :], xhf[:, d % 2, :],
                                             ALU.mult, ALU.add).then_inc(s_yc, 1)

                def block_steps(n, d, uses):
                    if not last(n):
                        low(n + 1, (d + 1) % 2)
                    gate(n, d, uses)
                    if over(n, 0):
                        y_out(n - 1, (d - 1) % DEEP)

                low(0, 0)
                over_blocks(dve, block_steps)
                y_out(NB - 1, DEEP - 1)
                def shift(q):
                    dve.wait_ge(s_zp, q + 1)
                    dve.scalar_tensor_tensor(zbi[:, q, :], zmv[:, q, :, 0], -1.0, zrs[:, q, :],
                                             ALU.mult, ALU.mult).then_inc(s_zb, 1)

                for q in range(NQ):
                    dve.wait_ge(s_z[q], 16)
                    dve.wait_ge(s_z2[q], 16)
                    dve.tensor_tensor(z[:, q, :, :], z[:, q, :, :], z2[:, q, :, :], ALU.add).then_inc(s_za, 1)
                    dve.wait_ge(s_za, q + 1)
                    for t in range(QT):
                        dve.bn_stats(zst[:, q, t, :], z[:, q, t, :]).then_inc(s_zst, 1)
                    for t in range(QT):
                        dve.wait_ge(s_zst, q * QT + t + 1)
                        dve.bn_aggr(zmv[:, q, t, :], zst[:, q, t, :]).then_inc(s_zag, 1)
                    dve.wait_ge(s_zag, (q + 1) * QT)
                    dve.tensor_scalar(zve[:, q, :], zmv[:, q, :, 1], EPS, None, ALU.add).then_inc(s_zv, 1)
                    if q > 0:
                        shift(q - 1)
                shift(NQ - 1)


def rope_tables():
    inv = (np.float32(1.0) / np.power(np.float32(10000.0), np.arange(0, DR, 2, dtype=np.float32) / np.float32(DR))).astype(np.float32)
    ang = np.outer(np.arange(T, dtype=np.float32), inv).astype(np.float32)
    c, s = np.cos(ang).astype(np.float32).T, np.sin(ang).astype(np.float32).T
    return np.ascontiguousarray(np.concatenate([c, c, -s, s], 0))


def chunks(w):
    return np.concatenate([w[i:i + P] for i in range(0, w.shape[0], P)], 1)


def kernel(**inputs):
    import concourse.bacc as bacc
    from concourse.bass_utils import run_bass_kernel_spmd

    a = {k: np.asarray(v) for k, v in inputs.items()}
    pre = "L0_attn_W_"
    swap = np.r_[DR // 2:DR, 0:DR // 2]
    numbers = np.tile(np.concatenate([np.arange(NB), np.arange(E) * CAP, np.zeros(NT)]).astype(np.float32), (P, 1))
    numbers[:, NB + E:] = np.arange(T, dtype=np.float32).reshape(NT, P).T
    filling = np.zeros((2 * E * P, W_ROW), np.float32)
    filling[:, D + 1] = 2 * B * T + np.arange(2 * E * P)
    wq_r, wk_r = a[pre + "q_rope"], a[pre + "k_rope"]
    w_all = np.concatenate([
        chunks(a[pre + "kv_down"]), chunks(a[pre + "q"]), chunks(np.concatenate([wq_r, wq_r[:, swap]], 1)),
        a[pre + "k_up"], a[pre + "v_up"], wk_r, wk_r[:, swap], chunks(a[pre + "o"])], 1)
    tri = np.triu(np.ones((P, P), np.float32), 1) * np.float32(CAUSAL)
    arrays = {
        "x": a["x"], "ctxT": a["ctx_1024"].transpose(2, 0, 1).reshape(D, B * NS), "mask": a["mask_BxSxS2_bk1"],
        "w_all": w_all, "kwT": a["L0_xattn_k_w"].T, "qw": a["L0_xattn_q_w"], "vwT": a["L0_xattn_v_w"].T,
        "qb": a["L0_xattn_q_b"].reshape(2, P).T, "kb": a["L0_xattn_k_b"].reshape(2, P).T, "vb": a["L0_xattn_v_b"], "wrT": a["L0_ffn_Wr"].T,
        "ident": np.eye(P, dtype=np.float32), "causal_q": tri, "causal_k": tri.T,
        "before": np.triu(np.ones((P, P), np.float32), 1), "numbers": numbers, "filling": filling,
        "w1": a["L0_ffn_w1"], "w3": a["L0_ffn_w3"], "w2": a["L0_ffn_w2"], "rope": rope_tables(),
    }
    arrays = {k: np.ascontiguousarray(v) for k, v in arrays.items()}
    nc = bacc.Bacc("TRN2", target_bir_lowering=False, num_devices=1)
    args = {k: nc.dram_tensor(k, v.shape, mybir.dt.from_np(v.dtype), kind="ExternalInput").ap() for k, v in arrays.items()}
    args["out"] = nc.dram_tensor("out", (B, T, D), F32, kind="ExternalOutput").ap()
    layer(nc, **args)
    r = run_bass_kernel_spmd(nc, [arrays], core_ids=[0])
    return r.results[0]["out"]
```

```python
from contextlib import ExitStack

import numpy as np

import concourse.bass as bass
from concourse import mybir

F32 = mybir.dt.float32
F32R = mybir.dt.float32r
BF16 = mybir.dt.bfloat16
U32 = mybir.dt.uint32
U8 = mybir.dt.uint8
ALU = mybir.AluOpType
ACT = mybir.ActivationFunctionType
AX = mybir.AxisListType

P = 128
B, T, D = 4, 1024, 256
NT = T // P
NH, HD, DR, DC = 16, 16, 32, 128
NS, NSP = 77, 96
E = 8
HG = 4
NG = NH // HG
F = 512
NB = 2 * B * T // P + E
CAP = B * T + P
ROWS = E * CAP + E * P
W_ROW = D + 2
KROWS = 2 * (HD + DR)
ATT_SCALE = 1.0 / float(np.sqrt(HD + DR))
X_SCALE = 1.0 / 16.0
EPS = 1e-5
MASKED = -1e9 / X_SCALE
CAUSAL = -1e30
WIDE = 256
HALF = T // 2

W_KV, W_Q, W_QR, W_KU, W_VU, W_KR, W_O = 0, 256, 768, 896, 1152, 1408, 1472
W_COLS = 1984

PROJ = ([("x", c, h) for h in range(2) for c in range(2)] + [("ckv", 0, h) for h in range(2)]
        + [("qr", 0, h) for h in range(2)] + [("kr", 0, h) for h in range(2)]
        + [("q", c, h) for c in range(2) for h in range(2)] + [("k", c, h) for c in range(2) for h in range(2)] + [("v", 0, j) for j in range(4)])
N_PROJ = len(PROJ)
N_SPLIT = 14
SPLIT = [sum(name in ("x", "ckv", "q", "k") for name, _, _ in PROJ[:u]) for u in range(N_PROJ)]
ROPE = [u for u in range(N_PROJ) if PROJ[u][0] in ("qr", "kr")]

S1_UNITS = ([(i, (h, h + 1)) for i in range(NT // 2) for h in range(0, HG, 2)]
            + [(i, (h,)) for i in range(NT // 2, NT) for h in range(HG)])
SECOND = NT // 2 * HG // 2
N_S1 = len(S1_UNITS) + 1
S2_STEPS = [(j, c) for j in range(NT) for c in range(2) if c == 1 or j < NT // 2]
N_S2 = len(S2_STEPS) * HG
N_PV = len(S2_STEPS)
LAG = 1
S1_TIME = [int(t) for t in np.cumsum([0] + [len(hs) * (i + 1) * P + 64 for i, hs in S1_UNITS] + [P])]
S2_TIME = [int(t) for t in np.cumsum([0] + [(c + 1) * HALF - max(j * P, c * HALF) + 64 for j, c in S2_STEPS for _ in range(HG)])]
BEFORE_COUNTS = 8
AHEAD = 4
LATE = 39
FIRST, SPARE = 1, 11


class Steps:

    def __init__(self, eng, sem, base, per):
        self.eng, self.sem, self.base, self.per, self.n = eng, sem, base, per, 0

    def __call__(self, ins):
        ins.then_inc(self.sem, 1)
        self.n += 1
        self.eng.wait_ge(self.sem, self.base * self.per + self.n)


def layer(nc, x, ctxT, mask, w_all, kwT, qw, vwT, qb, kb, vb, wrT, w1, w3, w2, ident, causal, before,
          numbers, filling, rope, out):
    ctx = ExitStack()
    with ctx:
        top = [16512]

        def at(name, shape, dt, offset=None):
            size = int(np.prod(shape[1:])) * mybir.dt.size(dt)
            if offset is None:
                offset = top[0]
                top[0] += (size + 63) // 64 * 64
            return nc.alloc_sbuf_tensor_at(name, shape, dt, offset=offset)

        def region(size):
            top[0] += size
            return top[0] - size

        def sem(name):
            return ctx.enter_context(nc.semaphore(name))

        idf = at("idf", [P, P], F32)
        cst_b = at("cst_b", [P, 3, P], BF16)

        idb, mask_q, mask_k = cst_b[:, 0, :], cst_b[:, 1, :], cst_b[:, 2, :]
        mark = at("mark", [P, 2], F32)
        nhalf = at("nhalf", [P, NT], F32)
        taken = at("taken", [P, E], F32)
        one = at("one", [P, P], F32)
        num = at("num", [P, NB], F32)
        kept = top[0]
        cs = at("cs", [2 * DR, T], F32)
        wh = at("wh", [P, W_COLS], F32R)
        wl = at("wl", [P, W_COLS], F32R)
        m_all = at("m_all", [P, 2, B, NSP], F32)
        brow = at("brow", [P, B, NSP], F32)
        vall = at("vall", [NSP, B, D], F32)
        wr = at("wr", [P, 2, NSP], F32)
        vaug = at("vaug", [P, NT, NH, HD + 1], F32)
        nmax = at("nmax", [P, HG * NT], F32)
        nmaxT = at("nmaxT", [HG * NT, P], F32R)
        xa = at("xa", [P, NT, D], F32)
        ckh = at("ckh", [P, T], F32R)
        ckl = at("ckl", [P, T], F32R)
        r2 = region(16384)
        oT = at("oT", [P, NG, T], F32, r2)
        r1 = region(32768)
        stg = at("stg", [P, 4, 2, HALF], F32R, r1)
        rs = at("rs", [DR, 4, T], F32R, r1 + 16384)
        pT = at("pT", [P, 3, HG, HALF], F32, r1)
        kas_at = region(32768)
        kas = at("kas", [KROWS + 1, 2, HG, T], F32R, kas_at)
        xTh = at("xTh", [P, 2, T], F32R, kas_at + 16384)
        xTl = at("xTl", [P, 2, T], F32R, kas_at + 24576)
        rt = at("rt", [DR, 2, 3, HALF], F32, kas_at)
        qs_at = region(32768)
        qs = at("qs", [KROWS + 1, 2, HG, T], F32R, qs_at)
        kbs_at = region(16384)
        kbs = at("kbs", [KROWS, HG, T], F32R, kbs_at)
        att = at("att", [P, NT, D], F32, qs_at)
        xr = at("xr", [P, NT, D], F32, qs_at + 8192)
        x1T = at("x1T", [P, 2, NT, P], F32, qs_at + 16384)
        x1 = at("x1", [P, NT, D], F32, qs_at + 24576)
        x2T = at("x2T", [P, 2, NT, P], F32, qs_at + 16384)
        sc = at("sc", [P, NT, NS], F32, kbs_at)
        keep = at("keep", [P, NT, NS], F32, kbs_at + 2496)
        neg = at("neg", [P, NT, NS], F32, kbs_at + 2 * 2496)
        pxT = at("pxT", [NSP, NT, P], F32, kbs_at + 3 * 2496 + 640)
        after_kbs = top[0]
        px = at("px", [P, NT, NSP], F32)
        x2 = at("x2", [P, NT, W_ROW], F32)
        x2b = at("x2b", [P, NT, W_ROW], F32, r1 - NT * W_ROW * 4 // 64 * 64 - 64)
        ids = at("ids", [P, NT], F32)
        mk = at("mk", [P, NT, NS], U8)
        picks = at("picks", [P, NT, 2], F32)
        bef = at("bef", [P, P], F32)
        oh = at("oh", [P, 3, NT, E], F32)
        run_ = at("run_", [P, NT, E], F32)
        pos = at("pos", [P, NT, E], F32)
        sel = at("sel", [P, 2, NT, E], F32)
        slf = at("slf", [P, 2, NT], F32)
        slots = at("slots", [P, 2, NT], U32)
        exp_at = at("exp_at", [P, E], F32)
        atth = at("atth", [P, 2, 2, P], F32R)
        attl = at("attl", [P, 2, 2, P], F32R)
        rden = at("rden", [P, 2, NH], F32)
        st = at("st", [P, 2, NT, 6], F32)
        mv = at("mv", [P, 2, NT, 2], F32)
        ve = at("ve", [P, 2, NT], F32)
        rstd = at("rstd", [P, 2, NT], F32)
        sx = at("sx", [P, 3, NT], F32)
        lg = at("lg", [P, 3, NT, E], F32)
        top8 = at("top8", [P, NT, E], F32)
        idx8 = at("idx8", [P, NT, E], U32)
        sl = at("sl", [P, 4, NT], F32)
        set_at = qs_at + 16384
        w_in = at("w_in", [P, W_COLS], F32, r1)
        cst_f = at("cst_f", [P, 2, P], F32, set_at + 13376)
        cxT = at("cxT", [P, 2, B * NS], F32, set_at)
        kw_s = at("kw_s", [P, 2, D], F32, set_at + 2560)
        qw_s = at("qw_s", [P, 2, D], F32, set_at + 4608)
        vw_s = at("vw_s", [P, 2, D], F32, set_at + 6656)
        kxT = at("kxT", [P, 2, B * NS], F32, set_at + 8704)
        bias_s = at("bias_s", [P, 4], F32, set_at + 11264)
        qb_b = at("qb_b", [P, 2, P], F32, set_at + 11328)
        vb_b = at("vb_b", [P, D], F32, set_at + 12352)

        ps = ctx.enter_context(nc.psum_tensor("ps", [P, 8, 512], F32))

        scr_q = nc.dram_tensor("scr_q", [B, 2, D, T], F32)
        scr_k = nc.dram_tensor("scr_k", [B, 2, D, T], F32)
        sums = nc.dram_tensor("sums", [2 * B * T + 2 * E * P, D], F32)
        xs = nc.dram_tensor("xs", [ROWS, W_ROW], F32)

        s_x, s_sc = sem("x_loaded"), sem("rows_sorted")
        s_w, s_cx, s_c = sem("w_loaded"), sem("ctx_loaded"), sem("consts_loaded")
        s_wh, s_wl, s_init = sem("w_high_done"), sem("w_low_done"), sem("init_done")
        s_qbb, s_xk, s_xk_read = sem("qb_spread"), sem("xk_ready"), sem("xk_read")
        s_xm, s_xm_read = sem("xm_ready"), sem("xm_read")
        with nc.Block() as block:
            @block.sync
            def _(sp):
                sp.dma_start(w_in[:, :], w_all).then_inc(s_w, 16)
                sp.dma_start(idf[:, :], ident).then_inc(s_c, 16)
                sp.dma_start(cst_f[:, :, :], causal).then_inc(s_c, 16)
                sp.dma_start(cs[:, :], rope).then_inc(s_c, 16)
                sp.dma_start(bef[:, :], before).then_inc(s_c, 16)
                sp.dma_start(num[:, :], numbers[:, 0:NB]).then_inc(s_c, 16)
                sp.dma_start(exp_at[:, :], numbers[:, NB:NB + E]).then_inc(s_c, 16)
                sp.dma_start(ids[:, :], numbers[:, NB + E:]).then_inc(s_c, 16)
                sp.wait_ge(s_init, 1)
                sp.dma_start(wr[:, :, 0:E], wrT.rearrange("(c p) e -> p c e", p=P)).then_inc(s_c, 16)

            @block.scalar
            def _(act):
                act.dma_start(cxT[:, :, :], ctxT.rearrange("(c p) n -> p c n", p=P)).then_inc(s_cx, 16)
                act.dma_start(kw_s[:, :, :], kwT.rearrange("(c p) n -> p c n", p=P)).then_inc(s_cx, 16)
                act.dma_start(qw_s[:, :, :], qw.rearrange("(c p) n -> p c n", p=P)).then_inc(s_cx, 16)
                act.dma_start(vw_s[:, :, :], vwT.rearrange("(c p) n -> p c n", p=P)).then_inc(s_cx, 16)
                act.dma_start(bias_s[:, 0:2], qb).then_inc(s_cx, 16)
                act.dma_start(bias_s[:, 2:4], kb).then_inc(s_cx, 16)
                act.dma_start(vb_b[:, :], vb.rearrange("(o n) -> o n", o=1).to_broadcast([P, D])).then_inc(s_cx, 16)
                act.wait_ge(s_w, 16)
                act.activation(wh[:, :], w_in[:, :], ACT.Copy).then_inc(s_wh, 1)

            @block.gpsimd
            def _(pool):
                pool.dma_start(xa[:, :, :], x[0].rearrange("(t p) d -> p t d", p=P)).then_inc(s_x, 16)
                pool.dma_start(xs[E * CAP:ROWS], filling[E * P:]).then_inc(s_sc, 16)
                pool.memset(wr[:, :, :], 0.0).then_inc(s_init, 1)
                pool.memset(m_all[:, :, :, :], 0.0).then_inc(s_init, 1)
                pool.memset(vall[:, :, :], 0.0).then_inc(s_init, 1)
                pool.memset(vaug[:, :, :, HD:HD + 1], 1.0).then_inc(s_init, 1)
                pool.memset(px[:, :, :], 0.0).then_inc(s_init, 1)
                pool.memset(one[:, :], 1.0).then_inc(s_init, 1)
                pool.memset(taken[:, :], 0.0).then_inc(s_init, 1)
                pool.memset(nhalf[:, :], -0.5).then_inc(s_init, 1)
                pool.wait_ge(s_init, 8)
                pool.memset(kas[KROWS:KROWS + 1, :, :, :].bitcast(F32), 1.0).then_inc(s_init, 1)

            @block.vector
            def _(dve):
                dve.memset(ps[:, 6:8, :], 0.0).then_inc(s_wl, 1)
                dve.wait_ge(s_c, 128)
                dve.tensor_copy(cst_b[:, 0, :], idf[:, :]).then_inc(s_wl, 1)
                dve.tensor_copy(cst_b[:, 1:3, :], cst_f[:, :, :]).then_inc(s_wl, 1)
                dve.wait_ge(s_wh, 1)
                dve.tensor_tensor(wl[:, :], w_in[:, :], wh[:, :].bitcast(F32), ALU.subtract).then_inc(s_wl, 1)

        s_pr, s_ph, s_pl = sem("proj_ready"), sem("proj_high"), sem("proj_low")
        s_rr, s_rs, s_vc = sem("rope_psum_read"), sem("rope_done"), sem("v_copied")
        s_stg = [sem(f"stage{i}_saved") for i in range(4)]
        s_qk = [[sem(f"heads_set{p}_half{h}") for h in range(2)] for p in range(2)]
        s_kb = [sem(f"klow_half{h}") for h in range(2)]
        s_s1, s_s1r = sem("scores_for_max"), sem("max_taken")
        s_mx = sem("max_rows_placed")
        s_s2, s_exp, s_pv = sem("scores_ready"), sem("probs_ready"), sem("probs_used")
        s_oT = sem("heads_out_copied")
        s_xr, s_mk = sem("residual_loaded"), sem("mask_loaded")
        s_t1, s_t1r = sem("attn_turned"), sem("attn_normed")
        s_t2, s_t2h, s_t2l = sem("attnT_ready"), sem("attnT_high"), sem("attnT_low")
        s_t3, s_t3r = sem("y_ready"), sem("y_added")
        s_ve1, s_pow1, s_ln1 = sem("var1_ready"), sem("rstd1_ready"), sem("x1_ready")
        s_t4, s_t4r = sem("x1T_ready"), sem("x1T_copied")
        s_t5, s_t5r, s_sh = sem("xscores_ready"), sem("xscores_read"), sem("xscores_shifted")
        s_xe = sem("xprobs_ready")
        s_t6, s_t6r = sem("xprobsT_ready"), sem("xprobsT_copied")
        s_t7, s_t7r = sem("xy_ready"), sem("xy_added")
        s_ve2, s_pow2, s_ln2 = sem("var2_ready"), sem("rstd2_ready"), sem("x2_ready")
        s_t8, s_t8r = sem("x2T_ready"), sem("x2T_copied")
        s_t9, s_t9r, s_le, s_lex = sem("logits_ready"), sem("logits_read"), sem("logits_shifted"), sem("logits_exp")
        s_stat, s_agg = sem("stats_ready"), sem("mean_var_ready")
        s_x2b, s_meta, s_oh, s_cnt = sem("second_rows_copied"), sem("gates_placed"), sem("onehots_ready"), sem("counts_ready")
        s_left, s_held = sem("rows_left"), sem("pool_waits_met")
        s_cr, s_slot = sem("counts_read"), sem("slots_ready")
        s_dve, s_ones = sem("dve_step"), sem("ones_row_placed")
        s_ra, s_rh = sem("rope_added"), sem("rope_high")

        DVE_STEPS = 1 + NT + 5 + 9 + 4 + 1 + 1 + 4 + 1

        def s1_at(g, n):
            return g * N_S1 + n

        def s1_slot(g, n):
            pairs = [((k % 3 if k < N_S1 else k % 2) * 2) for k in range(s1_at(g, n) + 1)]
            used = [k for k, p in enumerate(pairs[:-1]) if p == pairs[-1]]
            return pairs[-1], used[-1] if used else None

        def s2_bank(n):
            return (4, 5, 2, 3)[n % 4] if n >= (NG - 1) * N_S2 or n % N_S2 >= LATE else 4 + n % 2

        def proj_bank(u, first):
            return ps[:, u % 6 if first else 6 + u % 2, :]

        DEEP = 4
        assert r1 - kept >= 4 * 2 * E * 2 * F and kas_at == r1 + 32768 and qs_at == r1 + 65536
        w13h = at("w13h", [P, E, 2, 2, F], F32R, kept)
        w13l = at("w13l", [P, E, 2, 2, F], F32R, r1)
        w2s = at("w2s", [P, E, F // P, D], F32, qs_at)
        top[0] = kbs_at
        xb = at("xb", [P, DEEP, W_ROW], F32)
        cmp_ = at("cmp_", [P, 2, NB, E], F32, top[0])
        own = at("own", [P, 5, NB], F32, top[0] + 2 * NB * E * 4)
        sil = at("sil", [P, 2, F], F32)
        hid = at("hid", [P, 2, F], F32)
        cnt = at("cnt", [P, 3, E], F32)
        cnti = at("cnti", [P, 3, E], mybir.dt.int32)
        owner = at("owner", [P, NB], U32)
        first = at("first", [P, NB], U32)
        xbh = at("xbh", [P, 2, 2, P], F32R)
        assert top[0] <= after_kbs
        top[0] = after_kbs
        xbl = at("xbl", [P, 2, 2, P], F32R)
        hidT = at("hidT", [P, 2, F // P, P], F32)
        yb = at("yb", [P, DEEP, D], F32)
        xhf = at("xhf", [P, 2, D], F32)
        gb = at("gb", [P, DEEP, 1], F32)
        ib = at("ib", [P, DEEP, 1], U32)
        NQ, QT = 8, B * NT // 8
        z = at("z", [P, NQ, QT, D], F32, kept)
        z2 = at("z2", [P, NQ, QT, D], F32, kept + 35840)
        zbi = at("zbi", [P, NQ, QT], F32, kept + 34816)
        zst = at("zst", [P, NQ, QT, 6], F32, kept + 32768)
        zmv = at("zmv", [P, NQ, QT, 2], F32, kept + 33792)
        zve = at("zve", [P, NQ, QT], F32, kept + 34304)
        zrs = at("zrs", [P, NQ, QT], F32, kept + 34560)

        s_rstep = sem("block_list_step")
        s_took, s_own = sem("counts_whole"), sem("owners_ready")
        s_pad = sem("fillings_placed")
        s_wst, s_wsh, s_wsl = [sem(f"w13_loaded{n}") for n in range(2 * E)], sem("w13_high"), sem("w_expert_low")
        s_w2 = sem("w2_loaded")
        s_xb = [sem(f"block_rows{d}") for d in range(DEEP)]
        s_xt, s_xh, s_xl = sem("blockT_ready"), sem("blockT_high"), sem("blockT_low")
        s_h1, s_h3, s_si, s_hd = sem("h1_ready"), sem("h3_ready"), sem("silu_ready"), sem("hidden_ready")
        s_ht, s_hc, s_mt = sem("hiddenT_ready"), sem("hiddenT_copied"), sem("block_gates_kept")
        s_xhf = sem("half_x2_ready")
        s_y, s_yc = sem("block_y_ready"), sem("block_y_gated")
        s_ys = [sem(f"block_y_sent{d}") for d in range(DEEP)]
        s_z = [sem(f"sums_loaded{q}") for q in range(NQ)]
        s_z2 = [sem(f"second_sums_loaded{q}") for q in range(NQ)]
        s_za, s_zo, s_zb = sem("even_sums_added"), sem("odd_sums_added"), sem("shift3_ready")
        s_zst, s_zag, s_zv, s_zp, s_zn = sem("stats3"), sem("mean_var3"), sem("var3_ready"), sem("rstd3_ready"), sem("out_normed")
        s_out = sem("out_saved")

        def over(n, k):
            return n > k if isinstance(n, int) else True

        def last(n):
            return isinstance(n, int) and n == NB - 1

        def over_blocks(eng, steps):
            for n in range(3):
                steps(n, n, 0)
            with eng.Fori(0, (NB - DEEP) // DEEP) as m:
                for k in range(3, 3 + DEEP):
                    steps(DEEP * m + k, k % DEEP, m + k // DEEP)
            steps(NB - 1, DEEP - 1, NB // DEEP - 1)

        def row0(eng, n):
            return eng.value_load(first[0:1, n:n + 1] if isinstance(n, int) else first[0:1, bass.ds(n, 1)],
                                  min_val=0, max_val=ROWS - P)

        with nc.Block() as block:
            @block.gpsimd
            def _(pool):
                def hold(before_):
                    pool.wait_ge(s_held, before_ + 1)
                    pool.tensor_tensor(mark[:, 1:2], nhalf[:, 0:1], nhalf[:, 0:1], ALU.mult).then_inc(s_held, 1)

                pool.tensor_tensor(mark[:, 1:2], nhalf[:, 0:1], nhalf[:, 0:1], ALU.mult).then_inc(s_held, 1)
                def rope(b, *units):
                    for m in units:
                        cols = slice(m % 2 * HALF, (m % 2 + 1) * HALF)
                        pool.wait_ge(s_rr, b * 4 + m + 1)
                        pool.tensor_tensor(rt[:, m % 2, 2, :], rt[:, m % 2, 0, :], rt[:, m % 2, 1, :], ALU.add).then_inc(s_ra, 1)
                        pool.wait_ge(s_rh, b * 4 + m + 1)
                        pool.tensor_tensor(rs[:, m // 2 * 2 + 1, cols], rt[:, m % 2, 2, :], rs[:, m // 2 * 2, cols].bitcast(F32),
                                           ALU.subtract).then_inc(s_rs, 1)

                pool.wait_ge(s_pr, 4)
                pool.dma_start(xa[:, :, :], x[1].rearrange("(t p) d -> p t d", p=P)).then_inc(s_x, 16)

                rope(0, 0, 1, 2, 3)

                def batch(b, then):
                    pool.wait_ge(s_sc, b * 2 * NT * 16 + 16)
                    pool.tensor_tensor(mark[:, 0:1], nhalf[:, 0:1], nhalf[:, 0:1], ALU.mult).then_inc(s_left, 1)
                    def power(k, hf, ready, done_sem):
                        half = slice(hf * NT // 2, (hf + 1) * NT // 2)
                        pool.wait_ge(ready, b * 2 + hf + 1)
                        pool.tensor_tensor(rstd[:, k, half], ve[:, k, half], nhalf[:, half], ALU.pow).then_inc(done_sem, 1)

                    power(0, 0, s_ve1, s_pow1)
                    if then:
                        rope(b + 1, 0, 1)
                    power(0, 1, s_ve1, s_pow1)
                    if then:
                        rope(b + 1, 2, 3)
                        pool.wait_ge(s_pr, (b + 1) * N_PROJ + 4)
                        pool.dma_start(xa[:, :, :], x[bass.ds((b + 2) % B, 1)].rearrange("o (t p) d -> p (o t) d", p=P)
                                       ).then_inc(s_x, 16)
                    power(1, 0, s_ve2, s_pow2)
                    power(1, 1, s_ve2, s_pow2)
                    pool.wait_ge(s_meta, b * 2 + 2)
                    pool.wait_ge(s_x2b, b + 1)
                    pool.wait_ge(s_slot, b * 2 + 2)
                    hold(b)
                    for t in range(NT):
                        for k, rows in enumerate((x2, x2b)):
                            pool.indirect_dma_start(
                                out=xs[:, :], out_offset=bass.IndirectOffsetOnAxis(slots[:, k, t:t + 1], 0),
                                in_=rows[:, t, :], in_offset=None).then_inc(s_sc, 16)

                with pool.Fori(0, B - 1) as b:
                    batch(b, True)
                batch(B - 1, False)

                def send(n, d, uses):
                    pool.wait_ge(s_yc, n + 1)
                    hold(B + n)
                    pool.indirect_dma_start(out=sums[:, :], out_offset=bass.IndirectOffsetOnAxis(ib[:, d, :], 0),
                                            in_=yb[:, d, :], in_offset=None).then_inc(s_ys[d], 16)

                over_blocks(pool, send)
                for q in range(NQ):
                    if q % 2 == 0:
                        pool.wait_ge(s_z[q + 1], 16)
                        pool.wait_ge(s_z2[q + 1], 16)
                        pool.tensor_tensor(z[:, q + 1, :, :], z[:, q + 1, :, :], z2[:, q + 1, :, :], ALU.add).then_inc(s_zo, 1)
                    pool.wait_ge(s_zv, q + 1)
                    pool.tensor_tensor(zrs[:, q, :], zve[:, q, :], nhalf[:, 0:QT], ALU.pow).then_inc(s_zp, 1)

            @block.sync
            def _(sp):
                def load_heads(b, g, h):
                    p, cols = g % 2, slice(h * HALF, (h + 1) * HALF)
                    for scr, dst, parts in ((scr_q, qs, (0, 1)), (scr_k, kas, (0, 0))):
                        for r, part in enumerate(parts):
                            src = scr[bass.ds(b, 1), part, g * HG * HD:(g + 1) * HG * HD, cols]
                            sp.dma_start(dst[r * HD:(r + 1) * HD, p, :, cols].bitcast(F32),
                                         src.rearrange("o (h r) n -> r (o h) n", r=HD)).then_inc(s_qk[p][h], 16)

                def load_klow(b, g, h):
                    cols = slice(h * HALF, (h + 1) * HALF)
                    for r in range(2):
                        src = scr_k[bass.ds(b, 1), 1, g * HG * HD:(g + 1) * HG * HD, cols]
                        sp.dma_start(kbs[r * HD:(r + 1) * HD, :, cols].bitcast(F32),
                                     src.rearrange("o (h r) n -> r (o h) n", r=HD)).then_inc(s_kb[h], 16)

                def place_rope(dst, part, sem_):
                    for h in range(2):
                        cols = slice(h * HALF, (h + 1) * HALF)
                        for k in range(2):
                            src = rs[:, part + (k if part == 0 else 0), cols].bitcast(F32)
                            sp.dma_start(dst[DR + k * DR:2 * DR + k * DR, :, cols].bitcast(F32),
                                         src.rearrange("p (o n) -> p o n", o=1).to_broadcast([DR, HG, HALF])
                                         ).then_inc(sem_[h], 16)

                def save_parts(b):
                    for m in range(8):
                        name, c, h = PROJ[PROJ.index(("q", 0, 0)) + m]
                        sp.wait_ge(s_pl, b * N_SPLIT + 7 + m)
                        dst = (scr_q if name == "q" else scr_k)[bass.ds(b, 1), :, c * P:(c + 1) * P, h * HALF:(h + 1) * HALF]
                        sp.dma_start(dst.rearrange("o s p n -> p (o s) n"), stg[:, m % 4, :, :].bitcast(F32)
                                     ).then_inc(s_stg[m % 4], 16)

                def first_set(b):
                    sp.wait_ge(s_rs, b * 4 + 4)
                    place_rope(qs[:, 0], 0, s_qk[0])
                    place_rope(kas[:, 0], 2, s_qk[0])
                    for s in s_stg:
                        sp.wait_ge(s, b * 32 + 32)
                    for h in range(2):
                        load_heads(b, 0, h)

                def batch(b, then):
                    for h in range(2):
                        load_klow(b, 0, h)
                    for h in range(2):
                        load_heads(b, 1, h)
                    place_rope(qs[:, 1], 0, s_qk[1])
                    place_rope(kas[:, 1], 2, s_qk[1])
                    sp.dma_start(kas[KROWS:KROWS + 1, 1, :, :].bitcast(F32), one[0:HG * T // P, :]).then_inc(s_ones, 16)
                    for g in range(NG):
                        sp.wait_ge(s_s1r, b * NG * N_S1 + s1_at(g + 1, 0))
                        sp.dma_start(qs[KROWS:KROWS + 1, g % 2, :, :].bitcast(F32),
                                     nmaxT[:, :].bitcast(F32)).then_inc(s_mx, 16)
                        if g >= 1:
                            for h in range(2):
                                sp.wait_ge(s_s2, (b * NG + g - 1) * N_S2 + (8 * HG if h == 0 else N_S2))
                                load_klow(b, g, h)
                                if g + 1 < NG:
                                    load_heads(b, g + 1, h)
                            if g == NG - 1:
                                sp.dma_start(xr[:, :, :], x[bass.ds(b, 1)].rearrange("o (t p) d -> p (o t) d", p=P)).then_inc(s_xr, 16)
                                sp.dma_start(mk[:, :, :], mask[bass.ds(b, 1)].rearrange("o (t p) n -> p (o t) n", p=P)).then_inc(s_mk, 16)
                    if then:
                        save_parts(b + 1)
                        first_set(b + 1)
                        sp.wait_ge(s_t9, (b + 1) * 2)
                        place_rope(kbs, 3, s_kb)

                save_parts(0)
                first_set(0)
                place_rope(kbs, 3, s_kb)
                sp.wait_ge(s_xm, 3)
                sp.wait_ge(s_xm_read, B + 3)
                with sp.Fori(0, B - 1) as b:
                    batch(b, True)
                batch(B - 1, False)

                for e in range(E):
                    if e == 0:
                        sp.wait_ge(s_pv, B * NG * N_PV)
                    for k, w in enumerate((w1, w3)):
                        sp.dma_start(w13l[:, e, k, :, :].bitcast(F32), w[e].rearrange("(c p) f -> p c f", p=P)
                                     ).then_inc(s_wst[2 * e + k], 16)
                sp.wait_ge(s_t9, B * 2)
                for e in range(E):
                    sp.dma_start(w2s[:, e, :, :], w2[e].rearrange("(c p) d -> p c d", p=P)).then_inc(s_w2, 16)
                sp.wait_ge(s_took, 1)
                for e in range(E):
                    n_e = sp.value_load(cnti[0:1, 2, e:e + 1].bitcast(U32), min_val=0, max_val=B * T)
                    sp.dma_start(xs[bass.ds(n_e + e * CAP, P)], filling[e * P:(e + 1) * P]).then_inc(s_pad, 16)
                sp.wait_ge(s_own, 1)
                sp.wait_ge(s_pad, 16 * E)
                sp.wait_ge(s_sc, B * 2 * NT * 16 + 16)

                def fetch(n, d):
                    if over(n, 3):
                        sp.wait_ge(s_xt, n - 3)
                        sp.wait_ge(s_mt, n - 3)
                        sp.wait_ge(s_xhf, n - 3)
                    sp.wait_ge(s_own, 1)
                    sp.dma_start(xb[:, d, :], xs[bass.ds(row0(sp, n), P)]).then_inc(s_xb[d], 16)

                for n in range(DEEP):
                    fetch(n, n)
                with sp.Fori(1, NB // DEEP) as m:
                    for d in range(DEEP):
                        fetch(DEEP * m + d, d)
                for d in range(DEEP):
                    sp.wait_ge(s_ys[d], NB // DEEP * 16)
                sp.wait_ge(s_y, NB)
                for q in range(NQ):
                    sp.dma_start(z[:, q, :, :], sums[q * QT * P:(q + 1) * QT * P].rearrange("(t p) d -> p t d", p=P)
                                 ).then_inc(s_z[q], 16)
                for q in range(NQ):
                    sp.wait_ge(s_zn, (q + 1) * QT)
                    t0 = q * QT
                    sp.dma_start(out[t0 // NT, t0 % NT * P:(t0 % NT + QT) * P].rearrange("(t p) d -> p t d", p=P),
                                 z[:, q, :, :]).then_inc(s_out, 16)
                sp.wait_ge(s_out, NQ * 16)

            @block.tensor
            def _(pe):
                def products(outp, terms, last=True, first=True):
                    for n, (a, w) in enumerate(terms):
                        ins = pe.matmul(outp, a, w, start=first and n == 0, stop=last and n == len(terms) - 1)
                    return ins

                def parts(ah, al, bh, bl):
                    return [(ah, bh), (al, bh), (ah, bl)]

                def wsl(o, n):
                    return wh[:, o:o + n], wl[:, o:o + n]

                def s1_unit(b, g, n):
                    slot, before_ = s1_slot(g, n)
                    if before_ is not None:
                        pe.wait_ge(s_s1r, b * NG * N_S1 + before_ + 1)
                    if g >= 2 and n < 2 and slot == 2:
                        pe.wait_ge(s_exp, (b * NG + g - 1) * N_S2)
                    if n < N_S1 - 1:
                        i, hs = S1_UNITS[n]
                        for bank, h in enumerate(hs if len(hs) == 2 else hs * 2):
                            k0 = bank * HALF if len(hs) == 1 else 0
                            k1 = min(k0 + HALF, (i + 1) * P)
                            diag = k1 == (i + 1) * P
                            n_k = max(k1 - k0, WIDE)
                            ins = pe.matmul(ps[:, slot + bank, 0:n_k], qs[0:KROWS, g % 2, h, i * P:(i + 1) * P],
                                            kas[0:KROWS, g % 2, h, k0:k0 + n_k], start=True, stop=not diag)
                            if diag:
                                ins = pe.matmul(ps[:, slot + bank, i * P - k0:k1 - k0], idb, mask_q,
                                                start=False, stop=True)
                        ins.then_inc(s_s1, 1)
                    else:
                        pe.wait_ge(s_s1r, b * NG * N_S1 + s1_at(g, n))
                        pe.transpose(ps[0:HG * NT, slot, 0:P], nmax[:, :], idf[:, :]).then_inc(s_s1, 1)

                def s2_unit(b, g, u, h):
                    n = g * N_S2 + u * HG + h
                    j, c = S2_STEPS[u]
                    q0, q1 = max(j * P, c * HALF), (c + 1) * HALF
                    w0 = min(q0, q1 - WIDE)
                    o = ps[:, s2_bank(n), 0:q1 - w0]
                    if g < NG - 1 and u * HG + h == LATE:
                        pe.wait_ge(s_s1r, b * NG * N_S1 + s1_at(g + 2, 0))
                    had = [m for m in range(n) if s2_bank(m) == s2_bank(n)]
                    if had:
                        pe.wait_ge(s_exp, b * NG * N_S2 + had[-1] + 1)
                    diag = q0 == j * P
                    pe.matmul(o, kas[:, g % 2, h, j * P:(j + 1) * P], qs[:, g % 2, h, w0:q1], start=True, stop=False)
                    ins = pe.matmul(o, kbs[:, h, j * P:(j + 1) * P], qs[0:KROWS, g % 2, h, w0:q1],
                                    start=False, stop=not diag)
                    if diag:
                        ins = pe.matmul(o[:, q0 - w0:q0 - w0 + P], idb, mask_k, start=False, stop=True)
                    ins.then_inc(s_s2, 1)

                def pv_step(b, g, u):
                    j, c = S2_STEPS[u]
                    q0, q1 = max(j * P, c * HALF), (c + 1) * HALF
                    if u == 0 and g > 0:
                        pe.wait_ge(s_oT, b * NG + g)
                    pe.wait_ge(s_exp, (b * NG + g) * N_S2 + (u + 1) * HG)
                    last = S2_STEPS.index((3, 0)) if c == 0 else N_PV - 1
                    for h in range(HG):
                        ins = pe.matmul(ps[h * 32:h * 32 + HD + 1, 6 + c, q0 - c * HALF:HALF],
                                        vaug[:, j, g * HG + h, :], pT[:, u % 3, h, 0:q1 - q0],
                                        start=j == 0, stop=u == last, tile_position=(0, h * 32))
                    ins.then_inc(s_pv, 1)

                freed = {"v": (s_vc, 4), "qr": (s_rr, 4), "kr": (s_rr, 4)}

                def proj(b, u, first=False):
                    name, c, h = PROJ[u]
                    cols = slice(h * HALF, (h + 1) * HALF)
                    ring = 6 if first else 2
                    if u == 0:
                        pe.wait_ge(s_x, b * 16 + 16)
                    if u >= ring:
                        prev = PROJ[u - ring][0]
                        s, per = freed.get(prev, (s_pl, N_SPLIT))
                        k = sum(freed.get(p[0], (s_pl, 0))[0] is s for p in PROJ[:u - ring + 1])
                        pe.wait_ge(s, b * per + k)
                    o = proj_bank(u, first)
                    if name == "x":
                        for t in range(4):
                            ins = pe.transpose(o[:, t * P:(t + 1) * P], xa[:, h * 4 + t, c * P:(c + 1) * P], idf[:, :])
                    elif name == "ckv":
                        pe.wait_ge(s_pl, b * N_SPLIT + 2 * (h + 1))
                        terms = []
                        for m in range(2):
                            terms += parts(*wsl(W_KV + m * DC, DC), xTh[:, m, cols], xTl[:, m, cols])
                        ins = products(o, terms)
                    elif name == "q":
                        terms = []
                        for m in range(2):
                            terms += parts(*wsl(W_Q + m * D + c * P, P), xTh[:, m, cols], xTl[:, m, cols])
                        ins = products(o, terms)
                    elif name == "k":
                        pe.wait_ge(s_pl, b * N_SPLIT + 6)
                        ins = products(o, parts(*wsl(W_KU + c * P, P), ckh[:, cols], ckl[:, cols]))
                    elif name == "qr":
                        terms = []
                        for m in range(2):
                            terms += parts(*wsl(W_QR + m * 2 * DR, 2 * DR), xTh[:, m, cols], xTl[:, m, cols])
                        ins = products(o[0:2 * DR, :], terms)
                    elif name == "kr":
                        pe.wait_ge(s_pl, b * N_SPLIT + 6)
                        ins = products(o[0:2 * DR, :], parts(*wsl(W_KR, 2 * DR), ckh[:, cols], ckl[:, cols]))
                    else:
                        for t in range(2):
                            tok = slice((2 * h + t) * P, (2 * h + t + 1) * P)
                            vh, vl = wsl(W_VU, D)
                            ins = products(o[:, t * D:(t + 1) * D], [(ckh[:, tok], vh), (ckl[:, tok], vh), (ckh[:, tok], vl)])
                    ins.then_inc(s_pr, 1)

                def heads_here(b, g, h):
                    pe.wait_ge(s_qk[g % 2][h], b * 192 + (128 if g < 2 else 192))

                def first_maxima(b, n):
                    if n == 0:
                        pe.wait_ge(s_vc, b * 4 + 4)
                        pe.wait_ge(s_rr, b * 4 + 4)
                        heads_here(b, 0, 0)
                    if n == SECOND:
                        heads_here(b, 0, 1)
                    s1_unit(b, 0, n)

                def attention(b):
                    def klow_here(g, h):
                        pe.wait_ge(s_kb[h], b * 160 + 64 + 32 * g)

                    def due(unit, k):
                        all_k = N_S2 - SPARE
                        return k >= FIRST and S1_TIME[unit] / S1_TIME[-1] <= S2_TIME[k] / S2_TIME[all_k]

                    for g in range(NG):
                        done = 0
                        if g == 0:
                            heads_here(b, 1, 0)
                            for done in range(AHEAD):
                                s1_unit(b, 1, done)
                            done = AHEAD
                        pe.wait_ge(s_mx, (b * NG + g + 1) * 16)
                        if g == 1:
                            pe.wait_ge(s_ones, b * 16 + 16)
                        klow_here(g, 0)
                        for u in range(N_PV):
                            if u == 8:
                                klow_here(g, 1)
                            for h in range(HG):
                                s2_unit(b, g, u, h)
                                k = u * HG + h
                                while g + 1 < NG and done < N_S1 and due(done, k):
                                    if done == 0:
                                        heads_here(b, g + 1, 0)
                                    if done == SECOND:
                                        heads_here(b, g + 1, 1)
                                    s1_unit(b, g + 1, done)
                                    done += 1
                                assert k < LATE or g + 1 == NG or done == N_S1
                            if u >= LAG:
                                pv_step(b, g, u - LAG)
                        for u in range(N_PV - LAG, N_PV):
                            pv_step(b, g, u)
                        assert g + 1 == NG or done == N_S1

                def batch(b, then):
                    attention(b)

                    def nxt(*units):
                        if then:
                            for u in units:
                                proj(b + 1, u)

                    pe.wait_ge(s_oT, b * NG + NG)
                    for t in range(NT + 1):
                        if t < NT:
                            if t >= 2:
                                pe.wait_ge(s_t1r, b * NT + t - 1)
                            for g in range(NG):
                                ins = pe.transpose(ps[:, t % 2, g * P:(g + 1) * P], oT[:, g, t * P:(t + 1) * P], idf[:, :])
                            ins.then_inc(s_t1, 1)
                        if t >= 1:
                            u = t - 1
                            pe.wait_ge(s_t1r, b * NT + u + 1)
                            if u >= 2:
                                pe.wait_ge(s_t2l, b * NT + u - 1)
                            for c in range(2):
                                ins = pe.transpose(ps[:, 2 + u % 2, c * P:(c + 1) * P], att[:, u, c * P:(c + 1) * P], idf[:, :])
                            ins.then_inc(s_t2, 1)
                        nxt(t)
                        if t >= 1:
                            pe.wait_ge(s_t2l, b * NT + u + 1)
                            if u >= 2:
                                pe.wait_ge(s_t3r, b * NT + u - 1)
                            terms = []
                            for c in range(2):
                                vh, vl = wsl(W_O + c * D, D)
                                terms += [(atth[:, u % 2, c, :], vh), (attl[:, u % 2, c, :], vh), (atth[:, u % 2, c, :], vl)]
                            products(ps[:, 4 + u % 2, 0:D], terms).then_inc(s_t3, 1)

                    def turn(src, ready, done_sem, copied, units):
                        for t in range(NT):
                            pe.wait_ge(ready, b * NT + t + 1)
                            if t >= 2:
                                pe.wait_ge(copied, b * NT + t - 1)
                            for c in range(2):
                                ins = pe.transpose(ps[:, t % 2, c * P:(c + 1) * P], src[:, t, c * P:(c + 1) * P], idf[:, :])
                            ins.then_inc(done_sem, 1)
                            if t % 4 == 3:
                                nxt(*units[t // 4])

                    turn(x1, s_ln1, s_t4, s_t4r, ((9, 10, 11), (12,)))
                    for hf in range(2):
                        pe.wait_ge(s_t4r, b * NT + 4 * hf + 4)
                        for t in range(4 * hf, 4 * hf + 4):
                            for c in range(2):
                                ins = pe.matmul(ps[:, 2 + hf, (t % 4) * NSP:(t % 4 + 1) * NSP], x1T[:, c, t, :],
                                                m_all[:, c, bass.ds(b, 1), :].rearrange("p o n -> p (o n)"),
                                                start=c == 0, stop=c == 1)
                        ins.then_inc(s_t5, 1)
                    nxt(13, 14)
                    pe.wait_ge(s_xe, b + 1)
                    for hf in range(2):
                        for t in range(4 * hf, 4 * hf + 4):
                            ins = pe.transpose(ps[0:NSP, 4 + hf, (t % 4) * P:(t % 4 + 1) * P], px[:, t, :], idf[:, :])
                        ins.then_inc(s_t6, 1)
                    nxt(15)
                    for t in range(NT):
                        pe.wait_ge(s_t6r, b * 2 + t // 4 + 1)
                        if t >= 2:
                            pe.wait_ge(s_t7r, b * NT + t - 1)
                        pe.matmul(ps[:, 2 + t % 2, 0:D], pxT[:, t, :],
                                  vall[:, bass.ds(b, 1), :].rearrange("p o n -> p (o n)"),
                                  start=True, stop=True).then_inc(s_t7, 1)
                        if t % 4 == 3:
                            nxt(16 + t // 4)
                    turn(x2, s_ln2, s_t8, s_t8r, ((18, 19), (20,)))
                    for hf in range(2):
                        pe.wait_ge(s_t8r, b * NT + 4 * hf + 4)
                        for t in range(4 * hf, 4 * hf + 4):
                            for c in range(2):
                                ins = pe.matmul(ps[:, 2 + hf, (t % 4) * NSP:(t % 4 + 1) * NSP], x2T[:, c, t, :], wr[:, c, :],
                                                start=c == 0, stop=c == 1)
                        ins.then_inc(s_t9, 1)
                    nxt(21)
                    if then:
                        pe.wait_ge(s_t9r, b * 2 + 2)
                        for n in range(BEFORE_COUNTS):
                            first_maxima(b + 1, n)
                    pe.wait_ge(s_oh, b + 1)
                    picked = oh[:, 2, :, :].rearrange("p t e -> p (t e)")
                    pe.matmul(ps[:, 6, 0:NT * E], bef[:, :], picked, start=True, stop=True)
                    pe.matmul(ps[:, 7, 0:NT * E], one[:, :], picked, start=True, stop=True).then_inc(s_cnt, 1)
                    if then:
                        for n in range(BEFORE_COUNTS, N_S1):
                            first_maxima(b + 1, n)
                    pe.wait_ge(s_cr, b * 2 + 2)

                for u in range(N_PROJ):
                    proj(0, u, True)
                pe.wait_ge(s_vc, 4)
                pe.wait_ge(s_rr, 4)
                pe.wait_ge(s_pl, N_SPLIT)
                pe.wait_ge(s_cx, 112)
                for c in range(2):
                    for m in range(2):
                        ins = pe.matmul(ps[:, c, 0:B * NS], kw_s[:, m, c * P:(c + 1) * P], cxT[:, m, :],
                                        start=m == 0, stop=m == 1)
                    ins.then_inc(s_xk, 1)
                for b in range(B):
                    for m in range(2):
                        ins = pe.matmul(ps[0:NS, 2 + b, 0:D], cxT[:, m, b * NS:(b + 1) * NS], vw_s[:, m, :],
                                        start=m == 0, stop=m == 1)
                    ins.then_inc(s_xk, 1)
                pe.wait_ge(s_xk_read, 2)
                for c in range(2):
                    for q in range(2):
                        ins = pe.matmul(ps[:, c, 0:B * NS], qw_s[:, q, c * P:(c + 1) * P], kxT[:, q, :],
                                        start=q == 0, stop=q == 1)
                    ins.then_inc(s_xm, 1)
                pe.wait_ge(s_qbb, 2)
                pe.wait_ge(s_xm_read, 1)
                for q in range(2):
                    ins = pe.matmul(ps[:, 2, 0:B * NS], qb_b[:, q, :], kxT[:, q, :], start=q == 0, stop=q == 1)
                ins.then_inc(s_xm, 1)
                pe.wait_ge(s_xm_read, B + 3)
                for n in range(N_S1):
                    first_maxima(0, n)
                with pe.Fori(0, B - 1) as b:
                    batch(b, True)
                batch(B - 1, False)

                pe.wait_ge(s_own, 1)

                def turn_rows(n, d, uses):
                    p = d % 2
                    pe.wait_ge(s_xb[d], (uses + 1) * 16)
                    for c in range(2):
                        ins = pe.transpose(ps[:, p, c * P:(c + 1) * P], xb[:, d, c * P:(c + 1) * P], idf[:, :])
                    ins.then_inc(s_xt, 1)

                def expert(n):
                    return pe.value_load(owner[0:1, n:n + 1] if isinstance(n, int) else owner[0:1, bass.ds(n, 1)],
                                         min_val=0, max_val=E - 1)

                def wide(w, e, *at_):
                    return w[(slice(None), bass.ds(e, 1)) + at_ + (slice(None),)].rearrange("p o f -> p (o f)")

                def y_block(n, p, e):
                    pe.wait_ge(s_hc, n + 1)
                    if over(n, 0):
                        pe.wait_ge(s_yc, n)
                    else:
                        pe.wait_ge(s_w2, E * 16)
                    for c in range(F // P):
                        ins = pe.matmul(ps[:, 7, 0:D], hidT[:, p, c, :], wide(w2s, e, c), start=c == 0, stop=c == F // P - 1)
                    ins.then_inc(s_y, 1)

                def block_steps(n, d, uses):
                    p = d % 2
                    e = expert(n)
                    if not last(n):
                        turn_rows(n + 1, (d + 1) % DEEP, uses + (d + 1) // DEEP)
                    pe.wait_ge(s_wsl, 2 * e + 2)
                    pe.wait_ge(s_xl, n + 1)
                    for bank, part, done in ((2, 0, s_h1), (4, 1, s_h3)):
                        terms = [(a, w, c) for c in range(2) for a, w in ((xbh, w13h), (xbl, w13h), (xbh, w13l))]
                        for k, (a, w, c) in enumerate(terms):
                            ins = pe.matmul(ps[:, bank + p, :], a[:, p, c, :], wide(w, e, part, c), start=k == 0, stop=k == len(terms) - 1)
                        ins.then_inc(done, 1)
                    if over(n, 0):
                        y_block(n - 1, 1 - p, expert(n - 1))
                    pe.wait_ge(s_hd, n + 1)
                    if over(n, 0):
                        pe.wait_ge(s_hc, n)
                    for c in range(F // P):
                        ins = pe.transpose(ps[:, 6, c * P:(c + 1) * P], hid[:, p, c * P:(c + 1) * P], idf[:, :])
                    ins.then_inc(s_ht, 1)

                turn_rows(0, 0, 0)
                over_blocks(pe, block_steps)
                y_block(NB - 1, 1, expert(NB - 1))

            @block.scalar
            def _(act):
                def proj(b, u, first=False):
                    name, c, h = PROJ[u]
                    cols = slice(h * HALF, (h + 1) * HALF)

                    def high(dst):
                        act.wait_ge(s_pr, b * N_PROJ + u + 1)
                        act.activation(dst, proj_bank(u, first), ACT.Copy).then_inc(s_ph, 1)

                    if name == "x":
                        high(xTh[:, c, cols])
                    elif name == "ckv":
                        high(ckh[:, cols])
                    elif name in "qk":
                        m = SPLIT[u] - 6
                        if m >= 4:
                            act.wait_ge(s_stg[m % 4], b * 32 + 16)
                        high(stg[:, m % 4, 0, :])
                    elif name in ("qr", "kr"):
                        m = ROPE.index(u)
                        act.wait_ge(s_ra, b * 4 + m + 1)
                        act.activation(rs[:, m // 2 * 2, cols], rt[:, m % 2, 2, :], ACT.Copy).then_inc(s_rh, 1)
                    elif name == "v":
                        act.wait_ge(s_pr, b * N_PROJ + u + 1)
                        act.activation(vaug[:, 2 * h:2 * h + 2, :, 0:HD],
                                       proj_bank(u, first).rearrange("p (t h d) -> p t h d", t=2, h=NH), ACT.Copy).then_inc(s_vc, 1)

                def batch(b, then):
                    def nxt(*units):
                        if then:
                            for u in units:
                                proj(b + 1, u)

                    for g in range(NG):
                        for u, (j, c) in enumerate(S2_STEPS):
                            q0, q1 = max(j * P, c * HALF), (c + 1) * HALF
                            w0 = min(q0, q1 - WIDE)
                            if g * N_PV + u >= 3:
                                act.wait_ge(s_pv, b * NG * N_PV + g * N_PV + u - 2)
                            for h in range(HG):
                                n = g * N_S2 + u * HG + h
                                act.wait_ge(s_s2, b * NG * N_S2 + n + 1)
                                act.activation(pT[:, u % 3, h, 0:q1 - q0], ps[:, s2_bank(n), q0 - w0:q1 - w0], ACT.Exp,
                                               scale=ATT_SCALE).then_inc(s_exp, 1)
                        act.wait_ge(s_pv, (b * NG + g + 1) * N_PV)
                        if g == 0:
                            act.wait_ge(s_left, b + 1)
                        act.activation(oT[:, g, :], ps[:, 6:8, :].rearrange("p c n -> p (c n)"), ACT.Copy).then_inc(s_oT, 1)
                    nxt(0)
                    for t in range(NT):
                        act.wait_ge(s_t2, b * NT + t + 1)
                        if t >= 2:
                            act.wait_ge(s_t3, b * NT + t - 1)
                        act.activation(atth[:, t % 2, :, :], ps[:, 2 + t % 2, 0:D].rearrange("p (c n) -> p c n", c=2),
                                       ACT.Copy).then_inc(s_t2h, 1)
                        if t < NT - 1:
                            nxt(t + 1)

                    def copies(ready, dst, done_sem, units):
                        for t in range(NT):
                            act.wait_ge(ready, b * NT + t + 1)
                            act.activation(dst[:, :, t, :], ps[:, t % 2, 0:D].rearrange("p (c n) -> p c n", c=2),
                                           ACT.Copy).then_inc(done_sem, 1)
                            if t % 4 == 3:
                                nxt(*units[t // 4])

                    copies(s_t4, x1T, s_t4r, ((10, 11), (12,)))
                    nxt(8, 9, 13, 14)
                    act.wait_ge(s_sh, b + 1)
                    act.activation(px[:, :, 0:NS], sc[:, :, :], ACT.Exp, scale=X_SCALE).then_inc(s_xe, 1)
                    for hf in range(2):
                        act.wait_ge(s_t6, b * 2 + hf + 1)
                        act.activation(pxT[:, 4 * hf:4 * hf + 4, :],
                                       ps[0:NSP, 4 + hf, :].rearrange("p (t n) -> p t n", t=4), ACT.Copy).then_inc(s_t6r, 1)
                    nxt(15, 16, 17)
                    copies(s_t8, x2T, s_t8r, ((18, 19), (20,)))
                    nxt(21)
                    act.wait_ge(s_le, b + 1)
                    act.activation(lg[:, 1, :, :], lg[:, 0, :, :], ACT.Exp).then_inc(s_lex, 1)
                    act.wait_ge(s_t8, (b + 1) * NT)
                    act.activation(x2b[:, :, 0:D], x2[:, :, 0:D], ACT.Copy).then_inc(s_x2b, 1)

                for u in range(N_PROJ):
                    proj(0, u, True)
                with act.Fori(0, B - 1) as b:
                    batch(b, True)
                batch(B - 1, False)

                act.wait_ge(s_x, (B + 1) * 16)
                for n in range(2 * E):
                    if n == 2 * E - 2:
                        act.wait_ge(s_sc, B * 2 * NT * 16 + 16)
                    act.wait_ge(s_wst[n], 16)
                    act.activation(w13h[:, n // 2, n % 2, :, :], w13l[:, n // 2, n % 2, :, :].bitcast(F32),
                                   ACT.Copy).then_inc(s_wsh, 1)

                def high(n, p):
                    act.wait_ge(s_xt, n + 1)
                    if over(n, 1):
                        act.wait_ge(s_h3, n - 1)
                    act.activation(xbh[:, p, :, :], ps[:, p, 0:D].rearrange("p (c n) -> p c n", c=2), ACT.Copy).then_inc(s_xh, 1)

                def block_steps(n, d, uses):
                    p = d % 2
                    if not last(n):
                        high(n + 1, 1 - p)
                    act.wait_ge(s_h1, n + 1)
                    if over(n, 1):
                        act.wait_ge(s_hd, n - 1)
                    act.activation(sil[:, p, :], ps[:, 2 + p, :], ACT.Silu).then_inc(s_si, 1)
                    if over(n, 1):
                        act.wait_ge(s_yc, n - 1)
                    act.activation(xhf[:, p, :], xb[:, d, 0:D], ACT.Copy, scale=0.5).then_inc(s_xhf, 1)
                    act.wait_ge(s_ht, n + 1)
                    if over(n, 1):
                        act.wait_ge(s_y, n - 1)
                    act.activation(hidT[:, p, :, :], ps[:, 6, :].rearrange("p (c n) -> p c n", c=F // P), ACT.Copy).then_inc(s_hc, 1)

                high(0, 0)
                over_blocks(act, block_steps)
                for d in range(DEEP):
                    act.wait_ge(s_ys[d], NB // DEEP * 16)
                act.wait_ge(s_y, NB)
                for q in range(NQ):
                    act.dma_start(z2[:, q, :, :], sums[B * T + q * QT * P:B * T + (q + 1) * QT * P].rearrange(
                        "(t p) d -> p t d", p=P)).then_inc(s_z2[q], 16)
                for q in range(NQ):
                    act.wait_ge(s_zb, q + 1)
                    for t in range(QT):
                        act.activation(z[:, q, t, :], z[:, q, t, :], ACT.Identity, bias=zbi[:, q, t:t + 1],
                                       scale=zrs[:, q, t:t + 1]).then_inc(s_zn, 1)

            @block.vector
            def _(dve):
                def proj(b, u, first=False):
                    name, c, h = PROJ[u]
                    cols = slice(h * HALF, (h + 1) * HALF)
                    o = proj_bank(u, first)

                    def low(dst, high_):
                        dve.wait_ge(s_ph, b * N_SPLIT + SPLIT[u] + 1)
                        dve.tensor_tensor(dst, o, high_.bitcast(F32), ALU.subtract).then_inc(s_pl, 1)

                    if name == "x":
                        low(xTl[:, c, cols], xTh[:, c, cols])
                    elif name == "ckv":
                        low(ckl[:, cols], ckh[:, cols])
                    elif name in "qk":
                        m = SPLIT[u] - 6
                        low(stg[:, m % 4, 1, :], stg[:, m % 4, 0, :])
                    elif name in ("qr", "kr"):
                        m = ROPE.index(u)
                        dve.wait_ge(s_pr, b * N_PROJ + u + 1)
                        if m >= 2:
                            dve.wait_ge(s_rs, b * 4 + m - 1)
                        dve.tensor_tensor(rt[:, m % 2, 0, :], o[0:DR, :], cs[0:DR, cols], ALU.mult)
                        ins = dve.tensor_tensor(rt[:, m % 2, 1, :], o[DR:2 * DR, :], cs[DR:2 * DR, cols], ALU.mult)
                        ins.then_inc(s_rr, 1)

                def maxima(b, g, n):
                    slot, _ = s1_slot(g, n)
                    dve.wait_ge(s_s1, b * NG * N_S1 + s1_at(g, n) + 1)
                    if n < N_S1 - 1:
                        i, hs = S1_UNITS[n]
                        k = hs[0] * NT + i
                        if len(hs) == 2:
                            dve.tensor_reduce(nmax[:, k:k + NT + 1:NT], ps[:, slot:slot + 2, 0:(i + 1) * P],
                                              AX.X, ALU.max, negate=True).then_inc(s_s1r, 1)
                        else:
                            dve.tensor_reduce(nmax[:, k:k + 1],
                                              ps[:, slot:slot + 2, :].rearrange("p s n -> p (s n)")[:, 0:(i + 1) * P],
                                              AX.X, ALU.max, negate=True).then_inc(s_s1r, 1)
                    else:
                        if g > 0:
                            dve.wait_ge(s_mx, (b * NG + g) * 16)
                        dve.tensor_copy(nmaxT[:, :], ps[0:HG * NT, slot, 0:P]).then_inc(s_s1r, 1)

                def batch(b, then):
                    step = Steps(dve, s_dve, b, DVE_STEPS)

                    def nxt(*units):
                        if then:
                            for u in units:
                                proj(b + 1, u)

                    for g in range(1, NG):
                        for n in range(N_S1):
                            maxima(b, g, n)
                    dve.wait_ge(s_xr, b * 16 + 16)
                    dve.wait_ge(s_mk, b * 16 + 16)
                    dve.wait_ge(s_s2, (b + 1) * NG * N_S2)
                    dve.tensor_scalar(keep[:, :, :], mk[:, :, :], -1.0, 1.0, ALU.mult, ALU.add)
                    step(dve.tensor_scalar(neg[:, :, :], mk[:, :, :], MASKED, None, ALU.mult))

                    def stats(k, t, src):
                        if t > 0:
                            dve.wait_ge(s_stat, b * 2 * NT + k * NT + t)
                        dve.bn_stats(st[:, k, t, :], src).then_inc(s_stat, 1)
                        if t > 0:
                            dve.bn_aggr(mv[:, k, t - 1, :], st[:, k, t - 1, :]).then_inc(s_agg, 1)

                    def variance(k, hf, s_ve):
                        def add_eps(t0, t1):
                            dve.wait_ge(s_agg, b * 2 * NT + k * NT + t1)
                            return dve.tensor_scalar(ve[:, k, t0:t1], mv[:, k, t0:t1, 1], EPS, None, ALU.add)

                        if hf == 0:
                            add_eps(0, NT // 2).then_inc(s_ve, 1)
                        else:
                            dve.wait_ge(s_stat, b * 2 * NT + (k + 1) * NT)
                            add_eps(NT // 2, NT - 1)
                            dve.bn_aggr(mv[:, k, NT - 1, :], st[:, k, NT - 1, :]).then_inc(s_agg, 1)
                            add_eps(NT - 1, NT).then_inc(s_ve, 1)

                    def norm(k, hf, buf, s_pow, s_ln):
                        dve.wait_ge(s_pow, b * 2 + hf + 1)
                        for t in range(hf * NT // 2, (hf + 1) * NT // 2):
                            dve.tensor_scalar(buf[:, t, 0:D], buf[:, t, 0:D], mv[:, k, t, 0:1], rstd[:, k, t:t + 1],
                                              ALU.subtract, ALU.mult).then_inc(s_ln, 1)

                    for t in range(NT + 1):
                        if t < NT:
                            dve.wait_ge(s_t1, b * NT + t + 1)
                            po = ps[:, t % 2, :].rearrange("p (h d) -> p h d", h=NH)
                            step(dve.reciprocal(rden[:, t % 2, :], po[:, :, HD]))
                            dve.tensor_tensor(att[:, t, :].rearrange("p (h d) -> p h d", h=NH), po[:, :, 0:HD],
                                              rden[:, t % 2, :].rearrange("p (h o) -> p h o", o=1).to_broadcast([P, NH, HD]),
                                              ALU.mult).then_inc(s_t1r, 1)
                        if t >= 1:
                            u = t - 1
                            dve.wait_ge(s_t2h, b * NT + u + 1)
                            dve.tensor_tensor(attl[:, u % 2, :, :], ps[:, 2 + u % 2, 0:D].rearrange("p (c n) -> p c n", c=2),
                                              atth[:, u % 2, :, :].bitcast(F32), ALU.subtract).then_inc(s_t2l, 1)
                        nxt(t)
                        if t >= 1:
                            dve.wait_ge(s_t3, b * NT + u + 1)
                            dve.tensor_tensor(x1[:, u, :], ps[:, 4 + u % 2, 0:D], xr[:, u, :], ALU.add).then_inc(s_t3r, 1)
                            dve.wait_ge(s_t3r, b * NT + u + 1)
                            stats(0, u, x1[:, u, :])
                            if u == NT // 2:
                                variance(0, 0, s_ve1)
                            if u == NT // 2 + 2:
                                norm(0, 0, x1, s_pow1, s_ln1)

                    variance(0, 1, s_ve1)
                    nxt(9)
                    norm(0, 1, x1, s_pow1, s_ln1)
                    nxt(10, 11, 12)
                    for hf in range(2):
                        dve.wait_ge(s_t5, b * 2 + hf + 1)
                        ins = dve.tensor_tensor(
                            sc[:, 4 * hf:4 * hf + 4, :],
                            ps[:, 2 + hf, 0:4 * NSP].rearrange("p (t n) -> p t n", t=4)[:, :, 0:NS],
                            brow[:, bass.ds(b, 1), 0:NS].to_broadcast([P, 4, NS]), ALU.add)
                    ins.then_inc(s_t5r, 1)
                    dve.wait_ge(s_t5r, b + 1)
                    step(dve.tensor_tensor(sc[:, :, :], sc[:, :, :], keep[:, :, :], ALU.mult))
                    step(dve.tensor_tensor(sc[:, :, :], sc[:, :, :], neg[:, :, :], ALU.add))
                    step(dve.tensor_reduce(sx[:, 0, :], sc[:, :, :], AX.X, ALU.max))
                    dve.tensor_tensor(sc[:, :, :], sc[:, :, :],
                                      sx[:, 0, :].rearrange("p (t o) -> p t o", o=1).to_broadcast([P, NT, NS]),
                                      ALU.subtract).then_inc(s_sh, 1)
                    nxt(13)
                    dve.wait_ge(s_xe, b + 1)
                    step(dve.tensor_reduce(sx[:, 1, :], px[:, :, 0:NS], AX.X, ALU.add))
                    step(dve.reciprocal(sx[:, 2, :], sx[:, 1, :]))
                    nxt(14, 15)
                    for t in range(NT):
                        dve.wait_ge(s_t7, b * NT + t + 1)
                        dve.scalar_tensor_tensor(x2[:, t, 0:D], ps[:, 2 + t % 2, 0:D], sx[:, 2, t:t + 1], x1[:, t, :],
                                                 ALU.mult, ALU.add).then_inc(s_t7r, 1)
                        dve.wait_ge(s_t7r, b * NT + t + 1)
                        stats(1, t, x2[:, t, 0:D])
                        if t == 3:
                            nxt(16)
                        if t == NT // 2:
                            variance(1, 0, s_ve2)
                        if t == NT // 2 + 2:
                            norm(1, 0, x2, s_pow2, s_ln2)
                    variance(1, 1, s_ve2)
                    nxt(17)
                    norm(1, 1, x2, s_pow2, s_ln2)
                    nxt(18, 19, 20)
                    for hf in range(2):
                        dve.wait_ge(s_t9, b * 2 + hf + 1)
                        ins = dve.tensor_copy(lg[:, 0, 4 * hf:4 * hf + 4, :],
                                              ps[:, 2 + hf, 0:4 * NSP].rearrange("p (t n) -> p t n", t=4)[:, :, 0:E])
                        ins.then_inc(s_t9r, 1)
                    dve.wait_ge(s_t9r, b * 2 + 2)
                    step(dve.tensor_reduce(sl[:, 0, :], lg[:, 0, :, :], AX.X, ALU.max))
                    dve.tensor_tensor(lg[:, 0, :, :], lg[:, 0, :, :],
                                      sl[:, 0, :].rearrange("p (t o) -> p t o", o=1).to_broadcast([P, NT, E]),
                                      ALU.subtract).then_inc(s_le, 1)
                    dve.wait_ge(s_lex, b + 1)
                    step(dve.tensor_reduce(sl[:, 1, :], lg[:, 1, :, :], AX.X, ALU.add))
                    step(dve.reciprocal(sl[:, 2, :], sl[:, 1, :]))
                    nxt(21)
                    m = 0

                    def maxima_to(end):
                        nonlocal m
                        while then and m < end:
                            maxima(b + 1, 0, m)
                            m += 1

                    halves = [slice(0, NT // 2), slice(NT // 2, NT)]

                    def spread(buf, j):
                        return sl[:, j, :].rearrange("p (t o) -> p t o", o=1)[:, buf, :]

                    def probs(hf):
                        return dve.tensor_tensor(lg[:, 2, hf, :], lg[:, 1, hf, :], spread(hf, 2).to_broadcast([P, NT // 2, E]), ALU.mult)

                    def find(call, hf):
                        for t in range(hf.start, hf.stop):
                            ins = call(t)
                        return ins

                    def best(t):
                        return dve.max(top8[:, t, :], lg[:, 2, t, :])

                    def where(t):
                        return dve.max_index(idx8[:, t, :], top8[:, t, :], lg[:, 2, t, :])

                    def both(hf):
                        return dve.tensor_tensor(sl[:, 3, hf], top8[:, hf, 0], top8[:, hf, 1], ALU.add)

                    step(probs(halves[0]))
                    probs(halves[1]).then_inc(s_dve, 1)
                    find(best, halves[0]).then_inc(s_dve, 1)
                    step.n += 2
                    dve.wait_ge(s_dve, b * DVE_STEPS + step.n)
                    maxima_to(1)
                    both(halves[0])
                    step(find(best, halves[1]))
                    maxima_to(2)
                    both(halves[1])
                    find(where, halves[0])
                    step(find(where, halves[1]))
                    maxima_to(3)
                    step(dve.reciprocal(sl[:, 0, :], sl[:, 3, :]))
                    maxima_to(4)
                    g_of = sl[:, 0, :].rearrange("p (t o) -> p t o", o=1)
                    dve.wait_ge(s_t8, (b + 1) * NT)
                    for k, rows in enumerate((x2, x2b)):
                        dve.tensor_tensor(rows[:, :, D:D + 1], top8[:, :, k:k + 1], g_of, ALU.mult)
                        dve.tensor_scalar(rows[:, :, D + 1], ids[:, :], float(k * B * T), None, ALU.add).then_inc(s_meta, 1)
                    step(dve.tensor_copy(picks[:, :, :], idx8[:, :, 0:2]))
                    for k in range(2):
                        maxima_to(5 + k)
                        step(dve.tensor_tensor(oh[:, k, :, :], picks[:, :, k:k + 1].to_broadcast([P, NT, E]),
                                               num[:, 0:E].rearrange("p (o e) -> p o e", o=1).to_broadcast([P, NT, E]), ALU.is_equal))
                    dve.tensor_tensor(oh[:, 2, :, :], oh[:, 0, :, :], oh[:, 1, :, :], ALU.add).then_inc(s_oh, 1)
                    maxima_to(BEFORE_COUNTS)
                    step(dve.tensor_scalar(ids[:, :], ids[:, :], float(T), None, ALU.add))
                    maxima_to(BEFORE_COUNTS + 1)
                    dve.wait_ge(s_cnt, b + 1)
                    tot = ps[:, 7, 0:NT * E].rearrange("p (t e) -> p t e", e=E)
                    for e in range(E):
                        ins = dve.tensor_tensor_scan(run_[:, :, e], one[:, 0:NT], tot[:, :, e], taken[:, e:e + 1], ALU.mult, ALU.add)
                    step(ins)
                    maxima_to(BEFORE_COUNTS + 2)
                    dve.tensor_tensor(pos[:, :, :], run_[:, :, :], tot, ALU.subtract).then_inc(s_cr, 1)
                    maxima_to(BEFORE_COUNTS + 3)
                    dve.wait_ge(s_cr, b * 2 + 1)
                    dve.tensor_tensor(pos[:, :, :], pos[:, :, :], ps[:, 6, 0:NT * E].rearrange("p (t e) -> p t e", e=E),
                                      ALU.add).then_inc(s_cr, 1)
                    maxima_to(BEFORE_COUNTS + 4)
                    dve.wait_ge(s_cr, b * 2 + 2)
                    step(dve.tensor_tensor(pos[:, :, :], pos[:, :, :],
                                           exp_at[:, :].rearrange("p (o e) -> p o e", o=1).to_broadcast([P, NT, E]), ALU.add))
                    for k in range(2):
                        step(dve.tensor_tensor(sel[:, k, :, :], pos[:, :, :], oh[:, k, :, :], ALU.mult))
                        step(dve.tensor_reduce(slf[:, k, :], sel[:, k, :, :], AX.X, ALU.add))
                        dve.tensor_copy(slots[:, k, :], slf[:, k, :]).then_inc(s_slot, 1)
                    step(dve.tensor_copy(taken[:, :], run_[:, NT - 1, :]))
                    maxima_to(N_S1)
                    assert step.n == DVE_STEPS, (step.n, DVE_STEPS)

                for u in range(N_PROJ):
                    proj(0, u, True)
                dve.wait_ge(s_cx, 112)
                for c in range(2):
                    dve.tensor_copy(qb_b[:, c, :], bias_s[:, c:c + 1].to_broadcast([P, P])).then_inc(s_qbb, 1)
                dve.wait_ge(s_init, 9)
                for c in range(2):
                    dve.wait_ge(s_xk, c + 1)
                    dve.tensor_scalar(kxT[:, c, :], ps[:, c, 0:B * NS], bias_s[:, 2 + c:3 + c], None,
                                      ALU.add).then_inc(s_xk_read, 1)
                for b in range(B):
                    dve.wait_ge(s_xk, 3 + b)
                    dve.tensor_tensor(vall[0:NS, b, :], ps[0:NS, 2 + b, 0:D], vb_b[0:NS, :],
                                      ALU.add).then_inc(s_xm_read, 1)
                for c in range(2):
                    dve.wait_ge(s_xm, c + 1)
                    dve.tensor_copy(m_all[:, c, :, 0:NS],
                                    ps[:, c, 0:B * NS].rearrange("p (b n) -> p b n", b=B)).then_inc(s_xm_read, 1)
                dve.wait_ge(s_xm, 3)
                dve.tensor_copy(brow[:, :, 0:NS],
                                ps[:, 2, 0:B * NS].rearrange("p (b n) -> p b n", b=B)).then_inc(s_xm_read, 1)
                for n in range(N_S1):
                    maxima(0, 0, n)
                with dve.Fori(0, B - 1) as b:
                    batch(b, True)
                batch(B - 1, False)

                n_step = [0]

                def step(ins):
                    n_step[0] += 1
                    ins.then_inc(s_rstep, 1)
                    dve.wait_ge(s_rstep, n_step[0])

                dve.tensor_copy(cnti[:, 2, :], taken[:, :]).then_inc(s_took, 1)
                step(dve.tensor_scalar(cnti[:, 0, :], taken[:, :], float(P - 1), None, ALU.add))
                step(dve.tensor_scalar(cnti[:, 1, :], cnti[:, 0, :], 7, None, ALU.logical_shift_right))
                step(dve.tensor_copy(cnt[:, 0, :], cnti[:, 1, :]))
                step(dve.tensor_tensor_scan(cnt[:, 1, :], one[:, 0:E], cnt[:, 0, :], 0.0, ALU.mult, ALU.add))
                step(dve.tensor_tensor(cmp_[:, 0, :, :], num[:, :].rearrange("p (n o) -> p n o", o=1).to_broadcast([P, NB, E]),
                                       cnt[:, 1, :].rearrange("p (o e) -> p o e", o=1).to_broadcast([P, NB, E]), ALU.is_ge))
                step(dve.tensor_tensor(cmp_[:, 1, :, :], cmp_[:, 0, :, :],
                                       cnt[:, 0, :].rearrange("p (o e) -> p o e", o=1).to_broadcast([P, NB, E]), ALU.mult))
                step(dve.tensor_reduce(own[:, 0:2, :], cmp_[:, :, :, :], AX.X, ALU.add))
                step(dve.tensor_tensor(own[:, 2, :], num[:, :], own[:, 1, :], ALU.subtract))
                step(dve.tensor_scalar(own[:, 3, :], own[:, 2, :], float(P), None, ALU.mult))
                step(dve.tensor_scalar(own[:, 4, :], own[:, 0, :], float(CAP), None, ALU.mult))
                step(dve.tensor_tensor(first[:, :], own[:, 3, :], own[:, 4, :], ALU.add))
                dve.tensor_scalar(owner[:, :], own[:, 0, :], float(E - 1), None, ALU.min).then_inc(s_own, 1)
                for n in range(2 * E):
                    e, k = n // 2, n % 2
                    dve.wait_ge(s_wsh, n + 1)
                    dve.tensor_tensor(w13l[:, e, k, :, :], w13l[:, e, k, :, :].bitcast(F32), w13h[:, e, k, :, :].bitcast(F32),
                                      ALU.subtract).then_inc(s_wsl, 1)

                def low(n, p):
                    dve.wait_ge(s_xh, n + 1)
                    dve.tensor_tensor(xbl[:, p, :, :], ps[:, p, 0:D].rearrange("p (c n) -> p c n", c=2),
                                      xbh[:, p, :, :].bitcast(F32), ALU.subtract).then_inc(s_xl, 1)

                def gate(n, d, uses):
                    p = d % 2
                    dve.wait_ge(s_si, n + 1)
                    dve.wait_ge(s_h3, n + 1)
                    if over(n, 1):
                        dve.wait_ge(s_ht, n - 1)
                    dve.tensor_tensor(hid[:, p, :], ps[:, 4 + p, :], sil[:, p, :], ALU.mult).then_inc(s_hd, 1)
                    if over(n, 3):
                        dve.wait_ge(s_ys[d], uses * 16)
                    dve.tensor_copy(gb[:, d, :], xb[:, d, D:D + 1])
                    dve.tensor_copy(ib[:, d, :], xb[:, d, D + 1:D + 2]).then_inc(s_mt, 1)

                def y_out(n, d):
                    dve.wait_ge(s_y, n + 1)
                    dve.wait_ge(s_mt, n + 1)
                    dve.wait_ge(s_xhf, n + 1)
                    dve.scalar_tensor_tensor(yb[:, d, :], ps[:, 7, 0:D], gb[:, d, :], xhf[:, d % 2, :],
                                             ALU.mult, ALU.add).then_inc(s_yc, 1)

                def block_steps(n, d, uses):
                    if not last(n):
                        low(n + 1, (d + 1) % 2)
                    gate(n, d, uses)
                    if over(n, 0):
                        y_out(n - 1, (d - 1) % DEEP)

                low(0, 0)
                over_blocks(dve, block_steps)
                y_out(NB - 1, DEEP - 1)
                def shift(q):
                    dve.wait_ge(s_zp, q + 1)
                    dve.scalar_tensor_tensor(zbi[:, q, :], zmv[:, q, :, 0], -1.0, zrs[:, q, :],
                                             ALU.mult, ALU.mult).then_inc(s_zb, 1)

                for q in range(NQ):
                    if q % 2 == 0:
                        dve.wait_ge(s_z[q], 16)
                        dve.wait_ge(s_z2[q], 16)
                        dve.tensor_tensor(z[:, q, :, :], z[:, q, :, :], z2[:, q, :, :], ALU.add).then_inc(s_za, 1)
                        dve.wait_ge(s_za, q // 2 + 1)
                    else:
                        dve.wait_ge(s_zo, q // 2 + 1)
                    for t in range(QT):
                        dve.bn_stats(zst[:, q, t, :], z[:, q, t, :]).then_inc(s_zst, 1)
                    for t in range(QT):
                        dve.wait_ge(s_zst, q * QT + t + 1)
                        dve.bn_aggr(zmv[:, q, t, :], zst[:, q, t, :]).then_inc(s_zag, 1)
                    dve.wait_ge(s_zag, (q + 1) * QT)
                    dve.tensor_scalar(zve[:, q, :], zmv[:, q, :, 1], EPS, None, ALU.add).then_inc(s_zv, 1)
                    if q > 0:
                        shift(q - 1)
                shift(NQ - 1)


def rope_tables():
    inv = (np.float32(1.0) / np.power(np.float32(10000.0), np.arange(0, DR, 2, dtype=np.float32) / np.float32(DR))).astype(np.float32)
    ang = np.outer(np.arange(T, dtype=np.float32), inv).astype(np.float32)
    c, s = np.cos(ang).astype(np.float32).T, np.sin(ang).astype(np.float32).T
    return np.ascontiguousarray(np.concatenate([c, c, -s, s], 0))


def chunks(w):
    return np.concatenate([w[i:i + P] for i in range(0, w.shape[0], P)], 1)


def kernel(**inputs):
    import concourse.bacc as bacc
    from concourse.bass_utils import run_bass_kernel_spmd

    a = {k: np.asarray(v) for k, v in inputs.items()}
    pre = "L0_attn_W_"
    swap = np.r_[DR // 2:DR, 0:DR // 2]
    numbers = np.tile(np.concatenate([np.arange(NB), np.arange(E) * CAP, np.zeros(NT)]).astype(np.float32), (P, 1))
    numbers[:, NB + E:] = np.arange(T, dtype=np.float32).reshape(NT, P).T
    filling = np.zeros((2 * E * P, W_ROW), np.float32)
    filling[:, D + 1] = 2 * B * T + np.arange(2 * E * P)
    wq_r, wk_r = a[pre + "q_rope"], a[pre + "k_rope"]
    w_all = np.concatenate([
        chunks(a[pre + "kv_down"]), chunks(a[pre + "q"]), chunks(np.concatenate([wq_r, wq_r[:, swap]], 1)),
        a[pre + "k_up"], a[pre + "v_up"], wk_r, wk_r[:, swap], chunks(a[pre + "o"])], 1)
    tri = np.triu(np.ones((P, P), np.float32), 1) * np.float32(CAUSAL)
    arrays = {
        "x": a["x"], "ctxT": a["ctx_1024"].transpose(2, 0, 1).reshape(D, B * NS), "mask": a["mask_BxSxS2_bk1"],
        "w_all": w_all, "kwT": a["L0_xattn_k_w"].T, "qw": a["L0_xattn_q_w"], "vwT": a["L0_xattn_v_w"].T,
        "qb": a["L0_xattn_q_b"].reshape(2, P).T, "kb": a["L0_xattn_k_b"].reshape(2, P).T, "vb": a["L0_xattn_v_b"], "wrT": a["L0_ffn_Wr"].T,
        "ident": np.eye(P, dtype=np.float32), "causal": np.stack([tri, tri.T], 1),
        "before": np.triu(np.ones((P, P), np.float32), 1), "numbers": numbers, "filling": filling,
        "w1": a["L0_ffn_w1"], "w3": a["L0_ffn_w3"], "w2": a["L0_ffn_w2"], "rope": rope_tables(),
    }
    arrays = {k: np.ascontiguousarray(v) for k, v in arrays.items()}
    nc = bacc.Bacc("TRN2", target_bir_lowering=False, num_devices=1)
    args = {k: nc.dram_tensor(k, v.shape, mybir.dt.from_np(v.dtype), kind="ExternalInput").ap() for k, v in arrays.items()}
    args["out"] = nc.dram_tensor("out", (B, T, D), F32, kind="ExternalOutput").ap()
    layer(nc, **args)
    r = run_bass_kernel_spmd(nc, [arrays], core_ids=[0])
    return r.results[0]["out"]
```
